# Optimizing a Trainium2 kernel written in Bass

```python
import numpy as np
import jax
import jax.numpy as jnp

def _softmax(x, axis=-1):
    return jax.nn.softmax(x, axis=axis)

def _gelu(x):
    return jax.nn.gelu(x, approximate=True)

def _silu(x):
    return jax.nn.silu(x)

def _sigmoid(x):
    return jax.nn.sigmoid(x)

def _layernorm(x, axis=-1, eps=1e-05):
    m = jnp.mean(x, axis=axis, keepdims=True)
    v = jnp.var(x, axis=axis, keepdims=True)
    return (x - m) / jnp.sqrt(v + eps)

def _scatter_add(tgt, idx, src, axis=0):
    return tgt.at[idx].add(src)

def _segment_sum(src, seg, n):
    return jax.ops.segment_sum(src, seg, n)
kernel_name = 'mk_xattn_ffn_d1_seqx_r2_7a18c0'

def setup_inputs(seed: int=0):
    np.random.seed(seed)
    _w = jnp.asarray

    def _rec_inputs():
        import jax
        import jax.numpy as jnp
        _rk = jax.random.key(seed)
        x = -0.0002928 + 1 * jax.random.normal(jax.random.fold_in(_rk, 1), (16, 512, 512), jnp.float32)
        _lenS = 512 - jax.random.randint(jax.random.fold_in(_rk, 7), (16,), 0, max(1, 512 // 4) + 1, jnp.int32)
        _lenS2 = 77 - jax.random.randint(jax.random.fold_in(_rk, 8), (16,), 0, max(1, 77 // 4) + 1, jnp.int32)
        _ctx_1024P = jax.random.normal(jax.random.fold_in(_rk, 11), (16, 16, 512), jnp.float32)
        _ctx_1024c = jax.random.dirichlet(jax.random.fold_in(_rk, 511), 0.3 * jnp.ones((16,), jnp.float32), (16, 77))
        _ctx_1024t = jnp.einsum('bsk,bkd->bsd', _ctx_1024c, _ctx_1024P)
        _ctx_1024t = _ctx_1024t * jax.lax.rsqrt(jnp.mean(jnp.square(_ctx_1024t)) + 1e-12) * 0.953939
        ctx_1024 = -1.39393e-06 + 0.999914 * (_ctx_1024t + 0.3 * jax.random.normal(jax.random.fold_in(_rk, 611), (16, 77, 512), jnp.float32))
        _validS = jnp.arange(512)[None, :] < _lenS[:, None]
        _validS2 = jnp.arange(77)[None, :] < _lenS2[:, None]
        _causal = jnp.tril(jnp.ones((512, 512), dtype=bool))
        mask_Bx1xSxS2_ik0 = jnp.where(jnp.broadcast_to(_validS2[:, None, None, :], (16, 1, 512, 77)), 0, 1).astype(jnp.int32)
        return (x, ctx_1024, mask_Bx1xSxS2_ik0)
    x, ctx_1024, mask_Bx1xSxS2_ik0 = _rec_inputs()

    def _L0_xattn_setup():
        import jax, jax.numpy as jnp
        import numpy as np
        D_MODEL = 512
        H = 16
        D_K = D_MODEL // H
        B = 2
        S = 1024

        def _split_heads(x):
            b, s, _ = x.shape
            return x.reshape(b, s, H, D_K).transpose(0, 2, 1, 3)
        key = jax.random.key(seed)
        ks = jax.random.split(key, 11)
        scale = 1.0 / np.sqrt(D_MODEL)
        inp = {'query': jax.random.normal(ks[0], (B, S, D_MODEL), jnp.float32), 'key_in': jax.random.normal(ks[1], (B, S, D_MODEL), jnp.float32), 'value': jax.random.normal(ks[2], (B, S, D_MODEL), jnp.float32), 'mask': jnp.tril(jnp.ones((S, S), jnp.int32))[None, None, :, :].repeat(B, axis=0), 'w_q': jax.random.normal(ks[3], (D_MODEL, D_MODEL), jnp.float32) * scale, 'b_q': jax.random.normal(ks[4], (D_MODEL,), jnp.float32) * 0.01, 'w_k': jax.random.normal(ks[5], (D_MODEL, D_MODEL), jnp.float32) * scale, 'b_k': jax.random.normal(ks[6], (D_MODEL,), jnp.float32) * 0.01, 'w_v': jax.random.normal(ks[7], (D_MODEL, D_MODEL), jnp.float32) * scale, 'b_v': jax.random.normal(ks[8], (D_MODEL,), jnp.float32) * 0.01, 'w_out': jax.random.normal(ks[9], (D_MODEL, D_MODEL), jnp.float32) * scale, 'b_out': jax.random.normal(ks[10], (D_MODEL,), jnp.float32) * 0.01}
        return inp
    _L0_xattn_all = _L0_xattn_setup()
    _L0_xattn_in = {k: v for k, v in _L0_xattn_all.items() if k in ('w_q', 'b_q', 'w_k', 'b_k', 'w_v', 'b_v', 'w_out', 'b_out')}
    del _L0_xattn_all

    def _L0_ffn_setup():
        import jax, jax.numpy as jnp
        import numpy as np
        B, S, H, F, G = (8, 1024, 512, 2048, 128)
        EPS = 1e-05

        def _dequant(q, scales, g):
            K, N = q.shape
            w = (q.astype(jnp.float32) - 128.0).reshape(K // g, g, N) * scales[:, None, :]
            return w.reshape(K, N)
        key = jax.random.key(seed)
        ks = jax.random.split(key, 8)
        x = jax.random.normal(ks[0], (B, S, H), dtype=jnp.float32)
        ln_gamma = jnp.ones((H,), jnp.float32)
        ln_beta = jnp.zeros((H,), jnp.float32)
        fc1_q = jax.random.randint(ks[1], (H, F), 0, 128, dtype=jnp.int32)
        fc2_q = jax.random.randint(ks[2], (F, H), 0, 128, dtype=jnp.int32)
        fc1_scales = jax.random.uniform(ks[3], (H // G, F), jnp.float32) * 0.02 + 0.001
        fc2_scales = jax.random.uniform(ks[4], (F // G, H), jnp.float32) * 0.02 + 0.001
        fc1_bias = jax.random.normal(ks[5], (F,), jnp.float32) * 0.02
        fc2_bias = jax.random.normal(ks[6], (H,), jnp.float32) * 0.02
        return {'x': x, 'ln_gamma': ln_gamma, 'ln_beta': ln_beta, 'fc1_q': fc1_q, 'fc1_scales': fc1_scales, 'fc1_bias': fc1_bias, 'fc2_q': fc2_q, 'fc2_scales': fc2_scales, 'fc2_bias': fc2_bias}
    _L0_ffn_all = _L0_ffn_setup()
    _L0_ffn_in = {k: v for k, v in _L0_ffn_all.items() if k in ('ln_gamma', 'ln_beta', 'fc1_q', 'fc1_scales', 'fc1_bias', 'fc2_q', 'fc2_scales', 'fc2_bias')}
    del _L0_ffn_all
    return {'x': x, 'ctx_1024': ctx_1024, 'mask_Bx1xSxS2_ik0': mask_Bx1xSxS2_ik0, 'L0_xattn_w_q': _L0_xattn_in['w_q'], 'L0_xattn_b_q': _L0_xattn_in['b_q'], 'L0_xattn_w_k': _L0_xattn_in['w_k'], 'L0_xattn_b_k': _L0_xattn_in['b_k'], 'L0_xattn_w_v': _L0_xattn_in['w_v'], 'L0_xattn_b_v': _L0_xattn_in['b_v'], 'L0_xattn_w_out': _L0_xattn_in['w_out'], 'L0_xattn_b_out': _L0_xattn_in['b_out'], 'L0_ffn_ln_gamma': _L0_ffn_in['ln_gamma'], 'L0_ffn_ln_beta': _L0_ffn_in['ln_beta'], 'L0_ffn_fc1_q': _L0_ffn_in['fc1_q'], 'L0_ffn_fc1_scales': _L0_ffn_in['fc1_scales'], 'L0_ffn_fc1_bias': _L0_ffn_in['fc1_bias'], 'L0_ffn_fc2_q': _L0_ffn_in['fc2_q'], 'L0_ffn_fc2_scales': _L0_ffn_in['fc2_scales'], 'L0_ffn_fc2_bias': _L0_ffn_in['fc2_bias']}

def reference(x, ctx_1024, mask_Bx1xSxS2_ik0, L0_xattn_w_q, L0_xattn_b_q, L0_xattn_w_k, L0_xattn_b_k, L0_xattn_w_v, L0_xattn_b_v, L0_xattn_w_out, L0_xattn_b_out, L0_ffn_ln_gamma, L0_ffn_ln_beta, L0_ffn_fc1_q, L0_ffn_fc1_scales, L0_ffn_fc1_bias, L0_ffn_fc2_q, L0_ffn_fc2_scales, L0_ffn_fc2_bias):
    import jax
    import jax.numpy as jnp

    def _L0_xattn_ref(query, key_in, value, mask, w_q, b_q, w_k, b_k, w_v, b_v, w_out, b_out):
        import jax, jax.numpy as jnp
        import numpy as np
        D_MODEL = 512
        H = 16
        D_K = D_MODEL // H
        B = 2
        S = 1024

        def _split_heads(x):
            b, s, _ = x.shape
            return x.reshape(b, s, H, D_K).transpose(0, 2, 1, 3)
        q = _split_heads(query @ w_q.T + b_q)
        k = _split_heads(key_in @ w_k.T + b_k)
        v = _split_heads(value @ w_v.T + b_v)
        scores = jnp.einsum('bhqd,bhkd->bhqk', q, k) / jnp.sqrt(jnp.float32(D_K))
        scores = jnp.where(mask == 0, jnp.float32(-1000000000.0), scores)
        attn = jax.nn.softmax(scores, axis=-1)
        out = jnp.einsum('bhqk,bhkd->bhqd', attn, v)
        out = out.transpose(0, 2, 1, 3).reshape(query.shape[0], -1, D_MODEL)
        return out @ w_out.T + b_out

    def _L0_ffn_ref(x, ln_gamma, ln_beta, fc1_q, fc1_scales, fc1_bias, fc2_q, fc2_scales, fc2_bias):
        import jax, jax.numpy as jnp
        import numpy as np
        B, S, H, F, G = (8, 1024, 512, 2048, 128)
        EPS = 1e-05

        def _dequant(q, scales, g):
            K, N = q.shape
            w = (q.astype(jnp.float32) - 128.0).reshape(K // g, g, N) * scales[:, None, :]
            return w.reshape(K, N)
        residual = x
        mu = jnp.mean(x, axis=-1, keepdims=True)
        var = jnp.mean(jnp.square(x - mu), axis=-1, keepdims=True)
        h = (x - mu) * jax.lax.rsqrt(var + EPS) * ln_gamma + ln_beta
        hf = h.reshape(-1, H)
        w1 = _dequant(fc1_q, fc1_scales, G)
        y = hf @ w1 + fc1_bias
        y = jax.nn.silu(y)
        w2 = _dequant(fc2_q, fc2_scales, G)
        z = y @ w2 + fc2_bias
        return residual + 0.5 * z.reshape(residual.shape)
    x = x + _L0_xattn_ref(_layernorm(x, axis=-1), ctx_1024, ctx_1024, mask_Bx1xSxS2_ik0, L0_xattn_w_q, L0_xattn_b_q, L0_xattn_w_k, L0_xattn_b_k, L0_xattn_w_v, L0_xattn_b_v, L0_xattn_w_out, L0_xattn_b_out)
    x = x + _L0_ffn_ref(_layernorm(x, axis=-1), L0_ffn_ln_gamma, L0_ffn_ln_beta, L0_ffn_fc1_q, L0_ffn_fc1_scales, L0_ffn_fc1_bias, L0_ffn_fc2_q, L0_ffn_fc2_scales, L0_ffn_fc2_bias)
    return x

_drawn_inputs = setup_inputs


def setup_inputs(seed=0):
    import zlib

    import numpy as np

    out = dict(_drawn_inputs(seed))
    spreads = {'L0_ffn_ln_gamma': (1.0, 0.2), 'L0_ffn_ln_beta': (0.0, 0.1)}
    factors = {'L0_xattn_b_q': 64.0,
     'L0_xattn_b_k': 64.0,
     'L0_xattn_b_v': 45.971,
     'L0_xattn_b_out': 21.543,
     'L0_ffn_fc1_bias': 64.0,
     'L0_ffn_fc2_bias': 64.0}
    for name, (base, spread) in spreads.items():
        noise = np.random.default_rng([zlib.crc32(name.encode()), seed]).standard_normal(out[name].shape)
        drawn = base * np.exp(spread * noise) if base else spread * noise
        out[name] = jnp.asarray(drawn.astype(out[name].dtype))
    for name, factor in factors.items():
        out[name] = (out[name] * factor).astype(out[name].dtype)
    return out
```

```python
from contextlib import ExitStack

import concourse.bass as bass
from concourse import mybir

F32 = mybir.dt.float32
F32R = mybir.dt.float32r
I32 = mybir.dt.int32
ALU = mybir.AluOpType
ACT = mybir.ActivationFunctionType
AX = mybir.AxisListType

P = 128
HI, LO = 0, 1
PASSES = ((HI, HI), (HI, LO), (LO, HI))

BATCH, SEQ, DM = 16, 512, 512
KEYS = 77
HEADS, DK = 16, 32
FF = 2048
EPS = 1e-5
ZERO_POINT = 128.0
SCALE = float(DK) ** -0.5
MASKED = -1.0e30

TT = SEQ // P
KT = DM // P
HG = P // DK
GK = HG * KEYS
NF = FF // P
CUTS = (0, 103, 206, GK)
CTX = BATCH * KEYS
CHUNK_B = 4
CHUNK = CHUNK_B * KEYS
LAST = BATCH - 1


def value_pieces():
    out = []
    for t in range(3):
        for j in range(HG):
            a, b = max(CUTS[t], j * KEYS), min(CUTS[t + 1], (j + 1) * KEYS)
            if a < b:
                out.append((t, a - CUTS[t], a - j * KEYS, b - a, j))
    return out


def wait(eng, sem, value):
    if isinstance(value, int) and value <= 0:
        return
    eng.wait_ge(sem, value)


def by_parity(b, par):
    return b - par if par else b


def one(ap, b):
    return ap[b:b + 1] if isinstance(b, int) else ap[bass.ds(b, 1)]


def keys_and_values(nc, outer, ctxT, wT, b_k, b_v, k_dram, v_dram, w_q, w_o, k_diag, v_diag):
    ROWS = [(r, min(P, CTX - r)) for r in range(0, CTX, P)]
    NR = len(ROWS)
    NC = BATCH // CHUNK_B
    with ExitStack() as ctx:
        def sb(name, shape, dt=F32):
            return ctx.enter_context(nc.sbuf_tensor(name, shape, dt))

        def sem(name):
            return ctx.enter_context(nc.semaphore(name))

        raw = [sb(f"w_raw{i}", [P, KT, DM]) for i in range(2)]
        ctx_raw = [sb(f"ctx_raw{i}", [P, KT, CHUNK]) for i in range(2)]
        w_k = sb("w_k", [P, 2, KT, DM], F32R)
        w_v = sb("w_v", [P, 2, KT, DM], F32R)
        ctx_s = sb("ctx_split", [P, 2, KT, CTX], F32R)
        bk = sb("bk_col", [P, KT])
        bv = sb("bv_row", [P, DM])
        k_out = [sb(f"k_out{i}", [P, 2, CHUNK], F32R) for i in range(2)]
        v32 = [sb(f"v32_{i}", [P, DM]) for i in range(2)]
        v_out = [sb(f"v_out{i}", [P, 2, DM], F32R) for i in range(2)]
        bank = [ctx.enter_context(nc.psum_tensor(f"kv_bank{i}", [P, 512], F32)) for i in range(4)]

        split_to = [w_k, w_v, w_q, w_o]
        w_in = [sem(f"w_in{i}") for i in range(4)]
        c_in = [sem(f"ctx_in{i}") for i in range(NC)]
        bias_in = sem("kv_bias_in")
        w_hi, w_lo = sem("kv_w_hi"), sem("kv_w_lo")
        c_hi, c_lo = sem("ctx_hi"), sem("ctx_lo")
        full = sem("kv_full")
        k_hi, k_lo = sem("k_hi"), sem("k_lo")
        v_sum, v_hi, v_lo = sem("v_sum"), sem("v_hi"), sem("v_lo")
        k_kept = [sem(f"k_kept{i}") for i in range(2)]
        v_kept = [sem(f"v_kept{i}") for i in range(2)]
        block = ctx.enter_context(nc.Block())
        NK = NC * KT

        @block.sync
        def _(sp):
            def load_w(i):
                sp.dma_start(raw[i % 2][:, :, :], wT[i].rearrange("(k p) n -> p k n", p=P)).then_inc(w_in[i], 16)

            def load_ctx(c):
                sp.dma_start(ctx_raw[c % 2][:, :, :],
                             ctxT.rearrange("(k p) n -> p k n", p=P)[:, :, c * CHUNK:(c + 1) * CHUNK]
                             ).then_inc(c_in[c], 16)

            load_w(0)
            load_ctx(0)
            sp.dma_start(bk[:, :], b_k).then_inc(bias_in, 16)
            sp.dma_start(bv[:, :], b_v.partition_broadcast(P)).then_inc(bias_in, 16)
            load_ctx(1)
            load_w(1)
            for c in range(2, NC):
                sp.wait_ge(c_lo, c - 1)
                load_ctx(c)
            for i in range(2, 4):
                sp.wait_ge(w_lo, i - 1)
                load_w(i)
            for n in range(NK):
                c, g = n // KT, n % KT
                sp.wait_ge(k_lo, n + 1)
                for part in (HI, LO):
                    sp.dma_start(
                        k_dram[c * CHUNK_B:(c + 1) * CHUNK_B, :, part, g, :].rearrange("b p k -> p b k").bitcast(F32),
                        k_out[n % 2][:, part, :].rearrange("p (b k) -> p b k", k=KEYS).bitcast(F32),
                    ).then_inc(k_kept[n % 2], 16)
            for r, (row, rows) in enumerate(ROWS):
                sp.wait_ge(v_lo, r + 1)
                sp.dma_start(v_dram[row:row + rows, :].bitcast(F32),
                             v_out[r % 2][0:rows, :, :].rearrange("p t n -> p (t n)").bitcast(F32)
                             ).then_inc(v_kept[r % 2], 16)
            for i in range(2):
                sp.wait_ge(k_kept[i], 32 * (NK // 2))
                sp.wait_ge(v_kept[i], 16 * (NR // 2))

        @block.gpsimd
        def _(pool):
            nc.gpsimd.memset(k_diag[:, :, :, :].bitcast(F32), 0.0)
            nc.gpsimd.memset(v_diag[:, :, :, :, :].bitcast(F32), 0.0)

        @block.scalar
        def _(act):
            def hi_w(i):
                act.wait_ge(w_in[i], 16)
                nc.scalar.activation(split_to[i][:, HI, :, :], raw[i % 2][:, :, :], ACT.Copy).then_inc(w_hi, 1)

            def hi_ctx(c):
                act.wait_ge(c_in[c], 16)
                nc.scalar.activation(ctx_s[:, HI, :, c * CHUNK:(c + 1) * CHUNK], ctx_raw[c % 2][:, :, :],
                                     ACT.Copy).then_inc(c_hi, 1)

            hi_w(0)
            hi_ctx(0)
            hi_ctx(1)
            hi_w(1)
            for c in range(2, NC):
                hi_ctx(c)
            act.wait_ge(bias_in, 32)
            for n in range(NK):
                c, g = n // KT, n % KT
                act.wait_ge(full, n + 1)
                if n >= 2:
                    act.wait_ge(k_kept[n % 2], 32 * (n // 2))
                nc.scalar.activation(k_out[n % 2][:, HI, :], bank[n % 4][:, 0:CHUNK], ACT.Identity,
                                     bias=bk[:, g:g + 1]).then_inc(k_hi, 1)
                if n in (4, 8):
                    hi_w(1 + n // 4)
            for r, (row, rows) in enumerate(ROWS):
                act.wait_ge(v_sum, r + 1)
                if r >= 2:
                    act.wait_ge(v_kept[r % 2], 16 * (r // 2))
                nc.scalar.activation(v_out[r % 2][0:rows, HI, :], v32[r % 2][0:rows, :], ACT.Copy).then_inc(v_hi, 1)

        @block.vector
        def _(dve):
            def lo_w(i):
                dve.wait_ge(w_hi, i + 1)
                nc.vector.tensor_tensor(split_to[i][:, LO, :, :], raw[i % 2][:, :, :],
                                        split_to[i][:, HI, :, :].bitcast(F32), ALU.subtract).then_inc(w_lo, 1)

            def lo_ctx(c):
                dve.wait_ge(c_hi, c + 1)
                cols = slice(c * CHUNK, (c + 1) * CHUNK)
                nc.vector.tensor_tensor(ctx_s[:, LO, :, cols], ctx_raw[c % 2][:, :, :],
                                        ctx_s[:, HI, :, cols].bitcast(F32), ALU.subtract).then_inc(c_lo, 1)

            lo_w(0)
            lo_ctx(0)
            lo_ctx(1)
            lo_w(1)
            for c in range(2, NC):
                lo_ctx(c)
            for n in range(NK):
                g = n % KT
                dve.wait_ge(k_hi, n + 1)
                nc.vector.scalar_tensor_tensor(
                    out=k_out[n % 2][:, LO, :], in0=bank[n % 4][:, 0:CHUNK], scalar=bk[:, g:g + 1],
                    in1=k_out[n % 2][:, HI, :].bitcast(F32), op0=ALU.add, op1=ALU.subtract).then_inc(k_lo, 1)
                if n in (4, 8):
                    lo_w(1 + n // 4)

            def lo_v(r):
                rows = ROWS[r][1]
                dve.wait_ge(v_hi, r + 1)
                nc.vector.tensor_tensor(v_out[r % 2][0:rows, LO, :], v32[r % 2][0:rows, :],
                                        v_out[r % 2][0:rows, HI, :].bitcast(F32), ALU.subtract).then_inc(v_lo, 1)

            for r, (row, rows) in enumerate(ROWS):
                dve.wait_ge(full, NK + r + 1)
                wait(dve, v_lo, r - 1)
                nc.vector.tensor_tensor(v32[r % 2][0:rows, :], bank[(NK + r) % 4][0:rows, :], bv[0:rows, :],
                                        ALU.add).then_inc(v_sum, 1)
                if r:
                    lo_v(r - 1)
            lo_v(NR - 1)

        @block.tensor
        def _(pe):
            for n in range(NK):
                c, g = n // KT, n % KT
                if n == 0:
                    pe.wait_ge(w_lo, 1)
                if g == 0:
                    pe.wait_ge(c_lo, c + 1)
                if n >= 4:
                    pe.wait_ge(k_lo, n - 3)
                for i, (s, m) in enumerate(PASSES):
                    for k in range(KT):
                        mm = nc.tensor.matmul(bank[n % 4][:, 0:CHUNK], w_k[:, s, k, g * P:(g + 1) * P],
                                              ctx_s[:, m, k, c * CHUNK:(c + 1) * CHUNK],
                                              start=(i == 0 and k == 0), stop=(i == 2 and k == KT - 1))
                mm.then_inc(full, 1)
            pe.wait_ge(w_lo, 2)
            for r, (row, rows) in enumerate(ROWS):
                if r < 4:
                    pe.wait_ge(k_lo, NK - 3 + r)
                else:
                    pe.wait_ge(v_sum, r - 3)
                for i, (s, m) in enumerate(PASSES):
                    for k in range(KT):
                        mm = nc.tensor.matmul(bank[(NK + r) % 4][0:rows, :], ctx_s[:, s, k, row:row + rows],
                                              w_v[:, m, k, :],
                                              start=(i == 0 and k == 0), stop=(i == 2 and k == KT - 1))
                mm.then_inc(full, 1)


def attention_order():
    order = [(f"A{i}", 0) for i in range(KT)] + [("Q0", 0), ("Q1", 0), ("Q2", 0)]
    for b in range(BATCH):
        order += [("Q3", b), ("O3", b - 2), ("V3", b - 1)]
        order += [(f"A{i}", b + 1) for i in range(KT)] + [("O0", b - 1), ("Q0", b + 1), ("V0", b)]
        order += [("Q1", b + 1), ("O1", b - 1), ("V1", b)]
        order += [("Q2", b + 1), ("O2", b - 1), ("V2", b)]
    order += [("O3", LAST - 1), ("V3", LAST)] + [(f"O{i}", LAST) for i in range(TT)]
    return {x: n for n, x in enumerate(x for x in order if 0 <= x[1] < BATCH)}


ORDER = attention_order()
PER_SEQ = 16


def ordinal(what, b):
    if isinstance(b, int):
        return ORDER[(what, b)]
    middle = BATCH // 2
    return b * PER_SEQ + (ORDER[(what, middle)] - PER_SEQ * middle)


def bank_of(what, b):
    return ORDER[(what, b if isinstance(b, int) else BATCH // 2)] % 2


def attention(nc, x, mask, b_q, b_o, ident_dram, k_dram, v_dram, x2_dram, w_q, w_o, k_diag, v_diag):
    with ExitStack() as ctx:
        def sb(name, shape, dt=F32):
            return ctx.enter_context(nc.sbuf_tensor(name, shape, dt))

        def sem(name):
            return ctx.enter_context(nc.semaphore(name))

        ident = sb("ident", [P, P])
        bq = sb("bq_col", [P, KT])
        bo = sb("bo_row", [P, DM])
        x_sb = sb("x_sb", [P, TT, DM])
        stats = sb("stats", [P, TT, 6])
        mv = sb("mv", [P, TT, 2])
        var_eps = sb("var_eps", [P, TT])
        neg_mean = sb("neg_mean", [P, TT])
        rstd = sb("rstd", [P, TT])
        shift = sb("shift", [P, TT])
        minus_half = sb("minus_half", [P, TT])
        carrier = sb("carrier", [P, 2])
        xT = sb("xT", [P, 2, KT, SEQ], F32R)
        qT = sb("qT", [P, 2, 2, SEQ], F32R)
        prob = sb("prob", [P, KT, TT, GK])
        peak = sb("peak", [P, KT, TT * HG])
        total = sb("total", [P, KT, TT * HG])
        inv = sb("inv", [P, KT, TT * HG])
        pT = sb("pT", [P, 2, 2, 3, SEQ], F32R)
        aT = sb("aT", [P, 2, 2, KT, SEQ], F32R)
        res = sb("res", [P, TT, DM])
        mask_sb = sb("mask_sb", [P, 2, TT, KEYS], I32)
        bias = sb("bias", [P, 2, TT, KEYS])
        score = ctx.enter_context(nc.psum_tensor("score", [P, TT, 512], F32))
        work = [ctx.enter_context(nc.psum_tensor(f"work{i}", [P, 512], F32)) for i in range(2)]
        tbank = [ctx.enter_context(nc.psum_tensor(f"tbank{i}", [P, 512], F32)) for i in range(2)]

        const_in = sem("const_in")
        x_in = sem("x_in")
        mask_in, k_in, v_in = ([sem(f"{n}{i}") for i in range(2)] for n in ("mask_in", "k_in", "v_in"))
        res_in = [sem(f"res_in{t}") for t in range(TT)]
        x2_out = [sem(f"x2_out{t}") for t in range(TT)]
        half_set, ln_own, var_done, rstd_done, ln_done, xn_done = (
            sem(n) for n in ("half_set", "ln_own", "var_done", "rstd_done", "ln_done", "xn_done"))
        bias_done, res_ready = sem("bias_done"), sem("res_ready")
        work_full, work_free = sem("work_full"), sem("work_free")
        t_full, t_hi, t_lo = sem("t_full"), sem("t_hi"), sem("t_lo")
        x_hi, q_hi, a_hi = sem("x_hi"), sem("q_hi"), sem("a_hi")
        score_full, masked, peaked, shifted = (sem(n) for n in ("score_full", "masked", "peaked", "shifted"))
        exp_done, totalled, inverted, normed = (sem(n) for n in ("exp_done", "totalled", "inverted", "normed"))
        block = ctx.enter_context(nc.Block())

        def run(eng, start, body, end):
            start()
            body(0, 0)
            body(1, 1)
            with eng.Fori(1, BATCH // 2 - 1) as pair:
                body(pair * 2, 0)
                body(pair * 2 + 1, 1)
            body(BATCH - 2, 0)
            body(LAST, 1)
            end()

        def exists(b):
            return not isinstance(b, int) or 0 <= b < BATCH

        @block.sync
        def _(sp):
            def load_x(b):
                if exists(b):
                    if not (isinstance(b, int) and b == 0):
                        sp.wait_ge(work_full, ordinal("A3", b - 1) + 1)
                    sp.dma_start(x_sb[:, :, :], one(x, b).rearrange("o (t p) n -> (o p) t n", p=P)).then_inc(x_in, 16)

            def load_mask(b, par):
                if exists(b):
                    wait(sp, bias_done, b - 1)
                    sp.dma_start(mask_sb[:, par, :, :],
                                 one(mask, b).rearrange("o (t p) k -> (o p) t k", p=P)).then_inc(mask_in[par], 16)

            def load_k(b, par):
                if exists(b):
                    wait(sp, score_full, b * KT - KT)
                    for j in range(HG):
                        rows = slice(j * DK, (j + 1) * DK)
                        sp.dma_start(
                            k_diag[rows, par, :, j * KEYS:(j + 1) * KEYS].bitcast(F32),
                            one(k_dram, b)[:, rows, :, :, :].rearrange("o p t g k -> (o p) (t g) k").bitcast(F32),
                        ).then_inc(k_in[par], 16)

            def load_v(b, par):
                if exists(b):
                    if not (isinstance(b, int) and b < 2):
                        sp.wait_ge(work_full, ordinal("V3", b - 2) + 1)
                    seqs = v_dram.rearrange("(b k) (m d) -> b k m d", k=KEYS, d=P)
                    for t, row, key, n, j in value_pieces():
                        sp.dma_start(
                            v_diag[row:row + n, par, t, :, j * DK:(j + 1) * DK].bitcast(F32),
                            one(seqs, b)[:, key:key + n, :, j * DK:(j + 1) * DK]
                            .rearrange("o k m d -> (o k) m d").bitcast(F32),
                        ).then_inc(v_in[par], 16)

            def load_res(b, t):
                if exists(b):
                    wait(sp, x2_out[t], b * 16)
                    sp.dma_start(res[:, t, :], one(x, b)[:, t * P:(t + 1) * P, :].rearrange("o p n -> (o p) n")
                                 ).then_inc(res_in[t], 16)

            def store_x2(b, t):
                if exists(b):
                    sp.wait_ge(work_free, ordinal(f"O{t}", b) + 1)
                    sp.dma_start(one(x2_dram, b)[:, t * P:(t + 1) * P, :].rearrange("o p n -> (o p) n"),
                                 res[:, t, :]).then_inc(x2_out[t], 16)

            def start():
                load_x(0)
                sp.dma_start(ident[:, :], ident_dram).then_inc(const_in, 16)
                sp.dma_start(bq[:, :], b_q).then_inc(const_in, 16)
                load_mask(0, 0)
                load_k(0, 0)
                load_v(0, 0)
                sp.dma_start(bo[:, :], b_o.partition_broadcast(P)).then_inc(const_in, 16)
                load_x(1)

            def body(b, par):
                store_x2(b - 2, 3)
                for t in range(3):
                    load_res(b - 1, t)
                load_mask(b + 1, 1 - par)
                load_k(b + 1, 1 - par)
                load_v(b + 1, 1 - par)
                load_res(b - 1, 3)
                load_x(b + 2)
                for t in range(3):
                    store_x2(b - 1, t)

            def end():
                store_x2(LAST - 1, 3)
                for t in range(TT):
                    load_res(LAST, t)
                for t in range(TT):
                    store_x2(LAST, t)
                for t in range(TT):
                    sp.wait_ge(x2_out[t], 16 * BATCH)

            run(sp, start, body, end)

        @block.gpsimd
        def _(pool):
            def finish_ln(b):
                if exists(b):
                    pool.wait_ge(var_done, b * 2 + 2)
                    wait(pool, xn_done, b * TT)
                    nc.gpsimd.tensor_tensor(rstd[:, :], var_eps[:, :], minus_half[:, :], ALU.pow).then_inc(rstd_done, 1)
                    pool.wait_ge(rstd_done, b + 1)
                    nc.gpsimd.tensor_tensor(shift[:, :], neg_mean[:, :], rstd[:, :], ALU.mult).then_inc(ln_done, 1)

            def add_bo(b, t):
                if exists(b):
                    pool.wait_ge(res_in[t], b * 16 + 16)
                    nc.gpsimd.tensor_tensor(res[:, t, :], res[:, t, :], bo[:, :], ALU.add).then_inc(res_ready, 1)

            def norm(b, g):
                if exists(b):
                    pool.wait_ge(inverted, b * KT + (g + 1))
                    p = prob[:, g, :, :].rearrange("p t (h k) -> p (t h) k", k=KEYS)
                    nc.gpsimd.tensor_tensor(p, p, inv[:, g, :].unsqueeze(2).to_broadcast([P, TT * HG, KEYS]),
                                            ALU.mult).then_inc(normed, 1)

            def start():
                nc.gpsimd.memset(minus_half[:, :], -0.5).then_inc(half_set, 1)
                pool.wait_ge(half_set, 1)
                finish_ln(0)
                pool.wait_ge(const_in, 48)
                norm(0, 0)

            def body(b, par):
                add_bo(b - 2, 3)
                norm(b, 1)
                finish_ln(b + 1)
                add_bo(b - 1, 0)
                norm(b, 2)
                add_bo(b - 1, 1)
                norm(b, 3)
                add_bo(b - 1, 2)
                norm(b + 1, 0)

            def end():
                add_bo(LAST - 1, 3)
                for t in range(TT):
                    add_bo(LAST, t)

            run(pool, start, body, end)

        @block.scalar
        def _(act):
            def make_xn(b):
                if exists(b):
                    act.wait_ge(ln_done, b + 1)
                    for t in range(TT):
                        nc.scalar.activation(x_sb[:, t, :], x_sb[:, t, :], ACT.Identity,
                                             scale=rstd[:, t:t + 1], bias=shift[:, t:t + 1]).then_inc(xn_done, 1)

            def x_his(b):
                if exists(b):
                    for k in range(KT):
                        act.wait_ge(work_full, ordinal(f"A{k}", b) + 1)
                        if k == 0 and exists(b - 1):
                            act.wait_ge(work_full, ordinal("Q3", b - 1) + 1)
                        nc.scalar.activation(xT[:, HI, k, :], work[bank_of(f"A{k}", b)][:, :],
                                             ACT.Copy).then_inc(x_hi, 1)

            def q_his(b, g):
                if exists(b):
                    act.wait_ge(work_full, ordinal(f"Q{g}", b) + 1)
                    wait(act, score_full, b * KT + (g - 1))
                    nc.scalar.activation(qT[:, g % 2, HI, :], work[bank_of(f"Q{g}", b)][:, :], ACT.Identity,
                                         bias=bq[:, g:g + 1]).then_inc(q_hi, 1)

            def t_his(b, g, t):
                n = CUTS[t + 1] - CUTS[t]
                act.wait_ge(t_full, (b * KT + g) * 3 + (t + 1))
                if t == 0:
                    if g >= 2:
                        act.wait_ge(work_full, ordinal(f"V{g - 2}", b) + 1)
                    elif exists(b - 1):
                        act.wait_ge(work_full, ordinal(f"V{g + 2}", b - 1) + 1)
                nc.scalar.activation(pT[0:n, g % 2, HI, t, :], tbank[(g * 3 + t) % 2][0:n, :],
                                     ACT.Copy).then_inc(t_hi, 1)

            def exps(b, g):
                if exists(b):
                    act.wait_ge(shifted, b * KT + (g + 1))
                    nc.scalar.activation(prob[:, g, :, :], prob[:, g, :, :], ACT.Exp, scale=SCALE).then_inc(exp_done, 1)

            def a_his(b, par, g):
                if exists(b):
                    act.wait_ge(work_full, ordinal(f"V{g}", b) + 1)
                    if g == 0 and exists(b - 2):
                        act.wait_ge(work_full, ordinal("O3", b - 2) + 1)
                    nc.scalar.activation(aT[:, par, HI, g, :], work[bank_of(f"V{g}", b)][:, :],
                                         ACT.Copy).then_inc(a_hi, 1)

            def start():
                act.wait_ge(const_in, 48)
                make_xn(0)
                x_his(0)
                q_his(0, 0)
                q_his(0, 1)
                q_his(0, 2)
                exps(0, 0)
                exps(0, 1)

            def body(b, par):
                t_his(b, 0, 0)
                t_his(b, 0, 1)
                q_his(b, 3)
                t_his(b, 0, 2)
                exps(b, 2)
                a_his(b - 1, 1 - par, 3)
                make_xn(b + 1)

                t_his(b, 1, 0)
                t_his(b, 1, 1)
                x_his(b + 1)
                t_his(b, 1, 2)
                exps(b, 3)
                q_his(b + 1, 0)
                a_his(b, par, 0)

                for g in (2, 3):
                    t_his(b, g, 0)
                    t_his(b, g, 1)
                    q_his(b + 1, g - 1)
                    t_his(b, g, 2)
                    exps(b + 1, g - 2)
                    a_his(b, par, g - 1)

            def end():
                a_his(LAST, 1, 3)

            run(act, start, body, end)

        @block.vector
        def _(dve):
            def layernorm(b):
                if exists(b):
                    dve.wait_ge(x_in, b * 16 + 16)
                    wait(dve, ln_done, b)
                    for t in range(TT):
                        nc.vector.bn_stats(stats[:, t, :], x_sb[:, t, :]).then_inc(ln_own, 1)
                    dve.wait_ge(ln_own, b * 8 + 4)
                    nc.vector.tensor_copy(carrier[:, 1:2], carrier[:, 0:1])
                    for t in range(TT):
                        nc.vector.bn_aggr(mv[:, t, :], stats[:, t, :]).then_inc(ln_own, 1)
                    dve.wait_ge(ln_own, b * 8 + 8)
                    nc.vector.tensor_scalar(var_eps[:, :], mv[:, :, 1], EPS, None, ALU.add).then_inc(var_done, 1)
                    nc.vector.tensor_scalar(neg_mean[:, :], mv[:, :, 0], -1.0, None, ALU.mult).then_inc(var_done, 1)

            def make_bias(b, par):
                if exists(b):
                    dve.wait_ge(mask_in[par], by_parity(b, par) * 8 + 16)
                    nc.vector.tensor_scalar(bias[:, par, :, :], mask_sb[:, par, :, :], 0.0, MASKED,
                                            ALU.is_equal, ALU.mult).then_inc(bias_done, 1)

            def x_los(b):
                if exists(b):
                    for k in range(KT):
                        dve.wait_ge(x_hi, b * KT + (k + 1))
                        nc.vector.tensor_tensor(xT[:, LO, k, :], work[bank_of(f"A{k}", b)][:, :],
                                                xT[:, HI, k, :].bitcast(F32), ALU.subtract).then_inc(work_free, 1)

            def q_los(b, g):
                if exists(b):
                    dve.wait_ge(q_hi, b * KT + (g + 1))
                    nc.vector.scalar_tensor_tensor(
                        out=qT[:, g % 2, LO, :], in0=work[bank_of(f"Q{g}", b)][:, :], scalar=bq[:, g:g + 1],
                        in1=qT[:, g % 2, HI, :].bitcast(F32), op0=ALU.add, op1=ALU.subtract).then_inc(work_free, 1)

            def t_los(b, g, t):
                n = CUTS[t + 1] - CUTS[t]
                dve.wait_ge(t_hi, (b * KT + g) * 3 + (t + 1))
                nc.vector.tensor_tensor(pT[0:n, g % 2, LO, t, :], tbank[(g * 3 + t) % 2][0:n, :],
                                        pT[0:n, g % 2, HI, t, :].bitcast(F32), ALU.subtract).then_inc(t_lo, 1)

            def a_los(b, par, g):
                if exists(b):
                    dve.wait_ge(a_hi, b * KT + (g + 1))
                    nc.vector.tensor_tensor(aT[:, par, LO, g, :], work[bank_of(f"V{g}", b)][:, :],
                                            aT[:, par, HI, g, :].bitcast(F32), ALU.subtract).then_inc(work_free, 1)

            def mask_scores(b, par, g):
                if exists(b):
                    dve.wait_ge(score_full, b * KT + (g + 1))
                    if g == 0:
                        dve.wait_ge(bias_done, b + 1)
                    if exists(b - 1):
                        dve.wait_ge(t_full, (b * KT + g) * 3 - 9)
                    nc.vector.tensor_tensor(
                        prob[:, g, :, :].rearrange("p t (h k) -> p t h k", k=KEYS),
                        score[:, :, 0:GK].rearrange("p t (h k) -> p t h k", k=KEYS),
                        bias[:, par, :, :].unsqueeze(2).to_broadcast([P, TT, HG, KEYS]),
                        ALU.add).then_inc(masked, 1)

            def by_head(g):
                return prob[:, g, :, :].rearrange("p t (h k) -> p (t h) k", k=KEYS)

            def peaks(b, g):
                if exists(b):
                    dve.wait_ge(masked, b * KT + (g + 1))
                    nc.vector.tensor_reduce(peak[:, g, :], by_head(g), AX.X, ALU.max).then_inc(peaked, 1)

            def shift_scores(b, g):
                if exists(b):
                    dve.wait_ge(peaked, b * KT + (g + 1))
                    nc.vector.tensor_tensor(by_head(g), by_head(g),
                                            peak[:, g, :].unsqueeze(2).to_broadcast([P, TT * HG, KEYS]),
                                            ALU.subtract).then_inc(shifted, 1)

            def totals(b, g):
                if exists(b):
                    dve.wait_ge(exp_done, b * KT + (g + 1))
                    nc.vector.tensor_reduce(total[:, g, :], by_head(g), AX.X, ALU.add).then_inc(totalled, 1)
                    dve.wait_ge(totalled, b * KT + (g + 1))
                    nc.vector.reciprocal(inv[:, g, :], total[:, g, :]).then_inc(inverted, 1)

            def project(b, t):
                if exists(b):
                    dve.wait_ge(work_full, ordinal(f"O{t}", b) + 1)
                    dve.wait_ge(res_ready, b * TT + (t + 1))
                    nc.vector.tensor_tensor(res[:, t, :], work[bank_of(f"O{t}", b)][:, :], res[:, t, :],
                                            ALU.add).then_inc(work_free, 1)

            def start():
                nc.vector.memset(carrier[:, 0:1], 0.0)
                dve.wait_ge(const_in, 48)
                layernorm(0)
                make_bias(0, 0)
                x_los(0)
                q_los(0, 0)
                q_los(0, 1)
                mask_scores(0, 0, 0)
                q_los(0, 2)
                peaks(0, 0)
                shift_scores(0, 0)
                mask_scores(0, 0, 1)
                peaks(0, 1)
                shift_scores(0, 1)
                totals(0, 0)

            def body(b, par):
                mask_scores(b, par, 2)
                t_los(b, 0, 0)
                t_los(b, 0, 1)
                totals(b, 1)
                q_los(b, 3)
                peaks(b, 2)
                t_los(b, 0, 2)
                shift_scores(b, 2)
                project(b - 2, 3)
                layernorm(b + 1)
                make_bias(b + 1, 1 - par)
                a_los(b - 1, 1 - par, 3)

                mask_scores(b, par, 3)
                t_los(b, 1, 0)
                t_los(b, 1, 1)
                totals(b, 2)
                x_los(b + 1)
                peaks(b, 3)
                t_los(b, 1, 2)
                shift_scores(b, 3)
                project(b - 1, 0)
                q_los(b + 1, 0)
                a_los(b, par, 0)

                for g in (2, 3):
                    mask_scores(b + 1, 1 - par, g - 2)
                    t_los(b, g, 0)
                    t_los(b, g, 1)
                    if g == 2:
                        totals(b, 3)
                    else:
                        totals(b + 1, 0)
                    q_los(b + 1, g - 1)
                    peaks(b + 1, g - 2)
                    t_los(b, g, 2)
                    shift_scores(b + 1, g - 2)
                    project(b - 1, g - 1)
                    a_los(b, par, g - 1)

            def end():
                project(LAST - 1, 3)
                a_los(LAST, 1, 3)
                for t in range(TT):
                    project(LAST, t)

            run(dve, start, body, end)

        @block.tensor
        def _(pe):
            def free_bank(what, b):
                wait(pe, work_free, ordinal(what, b) - 1)
                return work[bank_of(what, b)]

            def transpose_x(b):
                if exists(b):
                    pe.wait_ge(xn_done, b * TT + TT)
                    for k in range(KT):
                        to = free_bank(f"A{k}", b)
                        for t in range(TT):
                            mm = nc.tensor.transpose(to[:, t * P:(t + 1) * P], x_sb[:, t, k * P:(k + 1) * P],
                                                     ident[:, :])
                        mm.then_inc(work_full, 1)

            def queries(b, g):
                if exists(b):
                    to = free_bank(f"Q{g}", b)
                    if g == 0:
                        pe.wait_ge(work_free, ordinal("A3", b) + 1)
                    for i, (s, m) in enumerate(PASSES):
                        for k in range(KT):
                            mm = nc.tensor.matmul(to[:, :], w_q[:, s, k, g * P:(g + 1) * P], xT[:, m, k, :],
                                                  start=(i == 0 and k == 0), stop=(i == 2 and k == KT - 1))
                    mm.then_inc(work_full, 1)

            def scores(b, par, g):
                if exists(b):
                    pe.wait_ge(work_free, ordinal(f"Q{g}", b) + 1)
                    if g == 0:
                        pe.wait_ge(k_in[par], by_parity(b, par) * (8 * HG) + 16 * HG)
                    wait(pe, masked, b * KT + g)
                    for t in range(TT):
                        for i, (s, m) in enumerate(PASSES):
                            mm = nc.tensor.matmul(score[:, t, 0:GK], qT[:, g % 2, s, t * P:(t + 1) * P],
                                                  k_diag[:, par, m * KT + g, :], start=(i == 0), stop=(i == 2))
                    mm.then_inc(score_full, 1)

            def transpose_p(b, g, t):
                n = (b * KT + g) * 3 + t
                if t == 0:
                    pe.wait_ge(normed, b * KT + (g + 1))
                wait(pe, t_lo, n - 1)
                for tt in range(TT):
                    mm = nc.tensor.transpose(tbank[(g * 3 + t) % 2][0:CUTS[t + 1] - CUTS[t], tt * P:(tt + 1) * P],
                                             prob[:, g, tt, CUTS[t]:CUTS[t + 1]], ident[:, :])
                mm.then_inc(t_full, 1)

            def weigh_values(b, par, g):
                if exists(b):
                    to = free_bank(f"V{g}", b)
                    pe.wait_ge(t_lo, (b * KT + g) * 3 + 3)
                    if g == 0:
                        pe.wait_ge(v_in[par], (by_parity(b, par) + 2) * (8 * len(value_pieces())))
                    for t in range(3):
                        n = CUTS[t + 1] - CUTS[t]
                        for i, (s, m) in enumerate(PASSES):
                            mm = nc.tensor.matmul(to[:, :], v_diag[0:n, par, t, s * KT + g, :],
                                                  pT[0:n, g % 2, m, t, :],
                                                  start=(t == 0 and i == 0), stop=(t == 2 and i == 2))
                    mm.then_inc(work_full, 1)

            def project(b, par, t):
                if exists(b):
                    to = free_bank(f"O{t}", b)
                    if t == 0:
                        pe.wait_ge(work_free, ordinal("V3", b) + 1)
                    for i, (s, m) in enumerate(PASSES):
                        for g in range(KT):
                            mm = nc.tensor.matmul(to[:, :], aT[:, par, s, g, t * P:(t + 1) * P], w_o[:, m, g, :],
                                                  start=(i == 0 and g == 0), stop=(i == 2 and g == KT - 1))
                    mm.then_inc(work_full, 1)

            def start():
                pe.wait_ge(const_in, 48)
                transpose_x(0)
                queries(0, 0)
                queries(0, 1)
                scores(0, 0, 0)
                queries(0, 2)
                scores(0, 0, 1)

            def body(b, par):
                scores(b, par, 2)
                transpose_p(b, 0, 0)
                transpose_p(b, 0, 1)
                queries(b, 3)
                transpose_p(b, 0, 2)
                project(b - 2, par, 3)
                weigh_values(b - 1, 1 - par, 3)

                scores(b, par, 3)
                transpose_p(b, 1, 0)
                transpose_p(b, 1, 1)
                transpose_x(b + 1)
                transpose_p(b, 1, 2)
                project(b - 1, 1 - par, 0)
                queries(b + 1, 0)
                weigh_values(b, par, 0)

                for g in (2, 3):
                    scores(b + 1, 1 - par, g - 2)
                    transpose_p(b, g, 0)
                    transpose_p(b, g, 1)
                    queries(b + 1, g - 1)
                    transpose_p(b, g, 2)
                    project(b - 1, 1 - par, g - 1)
                    weigh_values(b, par, g - 1)

            def end():
                project(LAST - 1, 0, 3)
                weigh_values(LAST, 1, 3)
                for t in range(TT):
                    project(LAST, 1, t)

            run(pe, start, body, end)


def feed_forward(nc, x2_dram, out, ident_dram, gamma, beta, q1, s1, b1, q2, s2, b2):
    with ExitStack() as ctx:
        def sb(name, shape, dt=F32):
            return ctx.enter_context(nc.sbuf_tensor(name, shape, dt))

        def sem(name):
            return ctx.enter_context(nc.semaphore(name))

        hT = [sb("hT0", [P, 2, KT, SEQ], F32R)]
        stage_at = nc.sbuf_base
        hT.append(sb("hT1", [P, 2, KT, SEQ], F32R))

        def staged(name, n, dt):
            return nc.alloc_sbuf_tensor_at(name, [P, 512], dt, offset=stage_at + 2048 * n)

        q1_sb = [staged(f"q1_sb{i}", 4 * i, I32) for i in range(2)]
        q2_sb = [staged(f"q2_sb{i}", 4 * i + 1, I32) for i in range(2)]
        w1_f = [staged(f"w1_f{i}", 4 * i + 2, F32) for i in range(2)]
        w2_f = [staged(f"w2_f{i}", 4 * i + 3, F32) for i in range(2)]
        w1 = sb("w1", [P, 2, KT, FF], F32R)
        w2 = sb("w2", [P, 2, NF, DM], F32R)
        ident = sb("ident3", [P, P])
        gam, bet = sb("gamma_col", [P, KT]), sb("beta_col", [P, KT])
        b1_in = sb("b1_in", [P, NF])
        b1_all, b1_half = sb("b1_all", [P, NF]), sb("b1_half", [P, NF])
        b2_half = sb("b2_half", [P, DM])
        x2 = sb("x2", [P, 2, TT, DM])
        h = sb("h", [P, TT, DM])
        stats, mv = sb("stats3", [P, TT, 6]), sb("mv3", [P, TT, 2])
        var_eps, rstds = sb("var_eps3", [P, 2, TT]), sb("rstds", [P, 2, TT])
        neg_mean, minus_half = sb("neg_mean3", [P, TT]), sb("minus_half3", [P, 2, TT])
        carrier = sb("carrier3", [P, 2])
        h_scale, h_shift = rstds[:, 1, :], sb("h_shift", [P, TT])
        u_scale, u_shift = sb("u_scale", [P, TT]), sb("u_shift", [P, TT])
        y = sb("y", [P, 2, SEQ])
        th = sb("th", [P, 2, SEQ])
        a = sb("a", [P, 2, 2, SEQ], F32R)
        acc = ctx.enter_context(nc.psum_tensor("acc", [P, TT, 512], F32))
        f_bank = [ctx.enter_context(nc.psum_tensor(f"f_bank{i}", [P, 512], F32)) for i in range(2)]
        h_bank = [ctx.enter_context(nc.psum_tensor(f"h_bank{i}", [P, 512], F32)) for i in range(2)]

        const_in, b2_done = sem("const_in3"), sem("b2_done")
        w_in = [sem(f"w_in3_{i}") for i in range(2)]
        w_f, w1_hi, w1_lo, w2_hi, w2_lo = (sem(n) for n in ("w_f", "w1_hi", "w1_lo", "w2_hi", "w2_lo"))
        b1_full, b1_sum, b1_done = sem("b1_full"), sem("b1_sum"), sem("b1_done")
        x2_in = [sem(f"x2_in{i}") for i in range(2)]
        out_kept = [sem(f"out_kept{i}") for i in range(2)]
        half_set, own, var_done, rstd_done, ln_done = (
            sem(n) for n in ("half_set3", "ln_own3", "var_done3", "rstd_done3", "ln_done3"))
        h_done, r_done, res_done = sem("h_done"), sem("r_done"), sem("res_done")
        h_full, h_hi, h_lo = sem("h_full"), sem("h_hi"), sem("h_lo")
        f_full, th_done, y_done, a_done, a_hi, a_lo = (
            sem(n) for n in ("f_full", "th_done", "y_done", "a_done", "a_hi3", "a_lo3"))
        g_done, acc_full, out_ready = sem("g_done"), sem("acc_full"), sem("out_ready")
        block = ctx.enter_context(nc.Block())

        NEXT_LN = 3
        NEXT_H = (6, 8, 10, 12)

        def run(eng, start, body, end):
            start()
            body(0, 0)
            body(1, 1)
            with eng.Fori(1, BATCH // 2 - 1) as pair:
                body(pair * 2, 0)
                body(pair * 2 + 1, 1)
            body(BATCH - 2, 0)
            body(LAST, 1)
            end()

        def exists(b):
            return not isinstance(b, int) or 0 <= b < BATCH

        def first(b):
            return isinstance(b, int) and b == 0

        @block.sync
        def _(sp):
            def load_x2(b, par):
                if exists(b):
                    if exists(b - 2):
                        sp.wait_ge(out_kept[par], by_parity(b, par) * (8 * TT))
                    sp.dma_start(x2[:, par, :, :], one(x2_dram, b).rearrange("o (t p) n -> (o p) t n", p=P)
                                 ).then_inc(x2_in[par], 16)

            def store(b, par):
                if exists(b):
                    for t in range(TT):
                        sp.wait_ge(out_ready, b * TT + (t + 1))
                        sp.dma_start(one(out, b)[:, t * P:(t + 1) * P, :].rearrange("o p n -> (o p) n"),
                                     x2[:, par, t, :]).then_inc(out_kept[par], 16)

            def load_w(f):
                i = f % 2
                if f >= 2:
                    sp.wait_ge(w1_lo, f - 1)
                    sp.wait_ge(w2_lo, f - 1)
                    sp.wait_ge(b1_full, f - 1)
                cols = slice(f * P, (f + 1) * P)
                sp.dma_start(q1_sb[i][:, :].rearrange("p (k n) -> p k n", n=P),
                             q1.rearrange("(k p) n -> p k n", p=P)[:, :, cols]).then_inc(w_in[i], 16)
                sp.dma_start(w1_f[i][:, :].rearrange("p (k n) -> p k n", n=P),
                             s1[:, cols].partition_broadcast(P)).then_inc(w_in[i], 16)
                sp.dma_start(q2_sb[i][:, :], q2[cols, :]).then_inc(w_in[i], 16)
                sp.dma_start(w2_f[i][:, :], s2[f, :].partition_broadcast(P)).then_inc(w_in[i], 16)

            def start():
                load_x2(0, 0)
                load_w(0)
                for to, of in ((ident, ident_dram), (gam, gamma), (bet, beta), (b1_in, b1)):
                    sp.dma_start(to[:, :], of).then_inc(const_in, 16)
                load_w(1)
                sp.dma_start(b2_half[:, :], b2.partition_broadcast(P)).then_inc(const_in, 16)
                load_x2(1, 1)
                for f in range(2, NF):
                    load_w(f)

            def body(b, par):
                if not first(b):
                    store(b - 1, 1 - par)
                    load_x2(b + 1, 1 - par)

            def end():
                store(LAST, 1)
                for i in range(2):
                    sp.wait_ge(out_kept[i], 8 * TT * BATCH)

            run(sp, start, body, end)

        @block.gpsimd
        def _(pool):
            def residual(b, par):
                if exists(b):
                    for t in range(TT):
                        pool.wait_ge(r_done, b * TT + (t + 1))
                        nc.gpsimd.tensor_tensor(x2[:, par, t, :], x2[:, par, t, :], b2_half[:, :],
                                                ALU.add).then_inc(res_done, 1)

            def finish_ln(b):
                if exists(b):
                    pool.wait_ge(var_done, b * 3 + 3)
                    wait(pool, r_done, b * TT)
                    nc.gpsimd.tensor_tensor(rstds[:, :, :], var_eps[:, :, :], minus_half[:, :, :],
                                            ALU.pow).then_inc(rstd_done, 1)
                    pool.wait_ge(rstd_done, b + 1)
                    nc.gpsimd.tensor_tensor(h_shift[:, :], neg_mean[:, :], h_scale, ALU.mult).then_inc(ln_done, 1)
                    nc.gpsimd.tensor_tensor(u_shift[:, :], neg_mean[:, :], rstds[:, 0, :], ALU.mult).then_inc(ln_done, 1)
                    nc.gpsimd.tensor_scalar(u_scale[:, :], rstds[:, 0, :], 1.0, None, ALU.add).then_inc(ln_done, 1)

            def start():
                nc.gpsimd.memset(minus_half[:, :, :], -0.5).then_inc(half_set, 1)
                pool.wait_ge(half_set, 1)
                finish_ln(0)
                pool.wait_ge(b2_done, 1)
                residual(0, 0)

            def body(b, par):
                finish_ln(b + 1)
                residual(b + 1, 1 - par)

            run(pool, start, body, lambda: None)

        @block.scalar
        def _(act):
            def make_h(b, par):
                if exists(b):
                    act.wait_ge(ln_done, b * 3 + 3)
                    if exists(b - 1):
                        act.wait_ge(h_full, b * KT)
                    for t in range(TT):
                        nc.scalar.activation(h[:, t, :], x2[:, par, t, :], ACT.Identity,
                                             scale=rstds[:, 1, t:t + 1], bias=h_shift[:, t:t + 1]).then_inc(h_done, 1)

            def make_r(b, par):
                if exists(b):
                    for t in range(TT):
                        act.wait_ge(h_done, b * TT + (t + 1))
                        nc.scalar.activation(x2[:, par, t, :], x2[:, par, t, :], ACT.Identity,
                                             scale=u_scale[:, t:t + 1], bias=u_shift[:, t:t + 1]).then_inc(r_done, 1)

            def h_his(b, par, k):
                if exists(b):
                    act.wait_ge(h_full, b * KT + (k + 1))
                    if isinstance(b, int) and b == 1:
                        act.wait_ge(w1_lo, NF)
                        act.wait_ge(w2_lo, NF)
                        act.wait_ge(b1_full, NF)
                    if exists(b - 2):
                        act.wait_ge(f_full, (b - 1) * NF)
                    nc.scalar.activation(hT[par][:, HI, k, :], h_bank[k % 2][:, :], ACT.Copy).then_inc(h_hi, 1)

            def split_w(f):
                act.wait_ge(w_f, 2 * f + 2)
                for k in range(KT):
                    nc.scalar.activation(w1[:, HI, k, f * P:(f + 1) * P], w1_f[f % 2][:, k * P:(k + 1) * P],
                                         ACT.Copy, scale=gam[:, k:k + 1]).then_inc(w1_hi, 1)
                nc.scalar.activation(w2[:, HI, f, :], w2_f[f % 2][:, :], ACT.Copy, scale=0.25).then_inc(w2_hi, 1)

            def silu(b, f):
                i = f % 2
                n = b * NF + f
                act.wait_ge(f_full, n + 1)
                if first(b):
                    act.wait_ge(b1_done, f + 1)
                wait(act, a_lo, n - 1)
                nc.scalar.activation(th[:, i, :], f_bank[i][:, :], ACT.Tanh, scale=0.5,
                                     bias=b1_half[:, f:f + 1]).then_inc(th_done, 1)
                nc.scalar.activation(y[:, i, :], f_bank[i][:, :], ACT.Identity,
                                     bias=b1_all[:, f:f + 1]).then_inc(y_done, 1)

            def a_his(b, f):
                n = b * NF + f
                act.wait_ge(a_done, n + 1)
                wait(act, g_done, n - 1)
                nc.scalar.activation(a[:, f % 2, HI, :], y[:, f % 2, :], ACT.Copy).then_inc(a_hi, 1)

            def start():
                act.wait_ge(const_in, 80)
                make_h(0, 0)
                make_r(0, 0)
                for k in range(KT):
                    h_his(0, 0, k)
                split_w(0)

            def body(b, par):
                for f in range(NF):
                    if first(b) and f + 1 < NF:
                        split_w(f + 1)
                    silu(b, f)
                    a_his(b, f)
                    if f == NEXT_LN + 1:
                        make_h(b + 1, 1 - par)
                    if f == NEXT_LN + 2:
                        make_r(b + 1, 1 - par)
                    if f in NEXT_H and not first(b):
                        h_his(b + 1, 1 - par, NEXT_H.index(f))
                if first(b):
                    for k in range(KT):
                        h_his(1, 1, k)

            run(act, start, body, lambda: None)

        @block.vector
        def _(dve):
            def layernorms(b, par):
                if exists(b):
                    dve.wait_ge(x2_in[par], by_parity(b, par) * 8 + 16)
                    wait(dve, ln_done, b * 3)
                    for t in range(TT):
                        nc.vector.bn_stats(stats[:, t, :], x2[:, par, t, :]).then_inc(own, 1)
                    dve.wait_ge(own, b * 8 + 4)
                    nc.vector.tensor_copy(carrier[:, 1:2], carrier[:, 0:1])
                    for t in range(TT):
                        nc.vector.bn_aggr(mv[:, t, :], stats[:, t, :]).then_inc(own, 1)
                    mean, var = mv[:, :, 0], mv[:, :, 1]
                    dve.wait_ge(own, b * 8 + 8)
                    nc.vector.tensor_scalar(var_eps[:, 0, :], var, EPS, None, ALU.add).then_inc(var_done, 1)
                    nc.vector.tensor_scalar(var_eps[:, 1, :], var, 1.0 + EPS, EPS * EPS,
                                            ALU.mult, ALU.add).then_inc(var_done, 1)
                    nc.vector.tensor_scalar(neg_mean[:, :], mean, -1.0, None, ALU.mult).then_inc(var_done, 1)

            def h_los(b, par, k):
                if exists(b):
                    dve.wait_ge(h_hi, b * KT + (k + 1))
                    nc.vector.tensor_tensor(hT[par][:, LO, k, :], h_bank[k % 2][:, :],
                                            hT[par][:, HI, k, :].bitcast(F32), ALU.subtract).then_inc(h_lo, 1)

            def dequantise(f):
                i = f % 2
                dve.wait_ge(w_in[i], 64 * (f // 2 + 1))
                for q, w in ((q1_sb[i], w1_f[i]), (q2_sb[i], w2_f[i])):
                    nc.vector.scalar_tensor_tensor(out=w[:, :], in0=q[:, :], scalar=-ZERO_POINT, in1=w[:, :],
                                                   op0=ALU.add, op1=ALU.mult).then_inc(w_f, 1)

            def split_w(f):
                i = f % 2
                dve.wait_ge(w1_hi, KT * (f + 1))
                for k in range(KT):
                    ins = nc.vector.scalar_tensor_tensor(
                        out=w1[:, LO, k, f * P:(f + 1) * P], in0=w1_f[i][:, k * P:(k + 1) * P],
                        scalar=gam[:, k:k + 1], in1=w1[:, HI, k, f * P:(f + 1) * P].bitcast(F32),
                        op0=ALU.mult, op1=ALU.subtract)
                ins.then_inc(w1_lo, 1)
                dve.wait_ge(w2_hi, f + 1)
                nc.vector.scalar_tensor_tensor(out=w2[:, LO, f, :], in0=w2_f[i][:, :], scalar=0.25,
                                               in1=w2[:, HI, f, :].bitcast(F32),
                                               op0=ALU.mult, op1=ALU.subtract).then_inc(w2_lo, 1)
                dve.wait_ge(b1_full, f + 1)
                nc.vector.tensor_tensor(b1_all[:, f:f + 1], h_bank[f % 2][:, f:f + 1], b1_in[:, f:f + 1],
                                        ALU.add).then_inc(b1_sum, 1)
                dve.wait_ge(b1_sum, f + 1)
                nc.vector.tensor_scalar(b1_half[:, f:f + 1], b1_all[:, f:f + 1], 0.5, None,
                                        ALU.mult).then_inc(b1_done, 1)

            def activate(b, f):
                i, n = f % 2, b * NF + f
                dve.wait_ge(th_done, n + 1)
                dve.wait_ge(y_done, n + 1)
                nc.vector.scalar_tensor_tensor(out=y[:, i, :], in0=th[:, i, :], scalar=1.0, in1=y[:, i, :],
                                               op0=ALU.add, op1=ALU.mult).then_inc(a_done, 1)
                dve.wait_ge(a_hi, n + 1)
                nc.vector.tensor_tensor(a[:, i, LO, :], y[:, i, :], a[:, i, HI, :].bitcast(F32),
                                        ALU.subtract).then_inc(a_lo, 1)

            def outputs(b, par):
                if exists(b):
                    for t in range(TT):
                        if t < TT - 1:
                            dve.wait_ge(acc_full, b * (TT - 1) + (t + 1))
                        else:
                            dve.wait_ge(g_done, b * NF + NF)
                        dve.wait_ge(res_done, b * TT + (t + 1))
                        nc.vector.tensor_tensor(x2[:, par, t, :], acc[:, t, :], x2[:, par, t, :],
                                                ALU.add).then_inc(out_ready, 1)

            def start():
                nc.vector.memset(carrier[:, 0:1], 0.0)
                dve.wait_ge(const_in, 80)
                layernorms(0, 0)
                dequantise(0)
                nc.vector.tensor_scalar(b2_half[:, :], b2_half[:, :], 0.5, None, ALU.mult).then_inc(b2_done, 1)
                for k in range(KT):
                    h_los(0, 0, k)
                split_w(0)

            def body(b, par):
                for f in range(NF):
                    if first(b) and f + 1 < NF:
                        dequantise(f + 1)
                        split_w(f + 1)
                    if f == 1:
                        outputs(b - 1, 1 - par)
                    activate(b, f)
                    if f == NEXT_LN:
                        layernorms(b + 1, 1 - par)
                    if f in NEXT_H and not first(b):
                        h_los(b + 1, 1 - par, NEXT_H.index(f))
                if first(b):
                    for k in range(KT):
                        h_los(1, 1, k)

            def end():
                outputs(LAST, 1)

            run(dve, start, body, end)

        @block.tensor
        def _(pe):
            def transpose_h(b, k):
                if exists(b):
                    if k == 0:
                        pe.wait_ge(h_done, b * TT + TT)
                        if isinstance(b, int) and b == 1:
                            pe.wait_ge(b1_done, NF)
                    wait(pe, h_lo, b * KT + (k - 1))
                    for t in range(TT):
                        mm = nc.tensor.transpose(h_bank[k % 2][:, t * P:(t + 1) * P], h[:, t, k * P:(k + 1) * P],
                                                 ident[:, :])
                    mm.then_inc(h_full, 1)

            def beta_bias(f):
                pe.wait_ge(w_f, 2 * f + 1)
                if f < 2:
                    pe.wait_ge(h_lo, KT - 1 + f)
                else:
                    pe.wait_ge(b1_sum, f - 1)
                for k in range(KT):
                    mm = nc.tensor.matmul(h_bank[f % 2][:, f:f + 1], w1_f[f % 2][:, k * P:(k + 1) * P],
                                          bet[:, k:k + 1], start=(k == 0), stop=(k == KT - 1))
                mm.then_inc(b1_full, 1)

            def fc1(b, par, f):
                n = b * NF + f
                if f == 0:
                    pe.wait_ge(h_lo, b * KT + KT)
                if first(b):
                    pe.wait_ge(w1_lo, f + 1)
                wait(pe, y_done, n - 1)
                for i, (s, m) in enumerate(PASSES):
                    for k in range(KT):
                        mm = nc.tensor.matmul(f_bank[f % 2][:, :], w1[:, s, k, f * P:(f + 1) * P],
                                              hT[par][:, m, k, :],
                                              start=(i == 0 and k == 0), stop=(i == 2 and k == KT - 1))
                mm.then_inc(f_full, 1)

            def fc2(b, f):
                n = b * NF + f
                pe.wait_ge(a_lo, n + 1)
                if first(b):
                    pe.wait_ge(w2_lo, f + 1)
                for t in range(TT):
                    if f == 0 and exists(b - 1):
                        pe.wait_ge(out_ready, b * TT + (t - 3))
                    for i, (s, m) in enumerate(PASSES):
                        mm = nc.tensor.matmul(acc[:, t, :], a[:, f % 2, s, t * P:(t + 1) * P], w2[:, m, f, :],
                                              start=(f == 0 and i == 0), stop=(f == NF - 1 and i == 2))
                    if f == NF - 1 and t < TT - 1:
                        mm.then_inc(acc_full, 1)
                mm.then_inc(g_done, 1)

            def start():
                pe.wait_ge(const_in, 80)
                for k in range(KT):
                    transpose_h(0, k)
                beta_bias(0)

            def body(b, par):
                for f in range(NF):
                    if first(b) and f + 1 < NF:
                        beta_bias(f + 1)
                    fc1(b, par, f)
                    if f:
                        fc2(b, f - 1)
                    elif exists(b - 1):
                        fc2(b - 1, NF - 1)
                    if f in NEXT_H and not first(b):
                        transpose_h(b + 1, NEXT_H.index(f))
                if first(b):
                    for k in range(KT):
                        transpose_h(1, k)

            def end():
                fc2(LAST, NF - 1)

            run(pe, start, body, end)


def xattn_ffn(nc, x, ctxT, mask, wqT, b_q, wkT, b_k, wvT, b_v, woT, b_o, ident, gamma, beta, q1, s1, b1, q2, s2, b2,
              out):
    k_dram = nc.dram_tensor("k_kept_dram", (BATCH, P, 2, KT, KEYS), F32R, kind="Internal").ap()
    v_dram = nc.dram_tensor("v_kept_dram", (CTX, 2 * DM), F32R, kind="Internal").ap()
    x2_dram = nc.dram_tensor("x2_kept_dram", (BATCH, SEQ, DM), F32, kind="Internal").ap()
    with ExitStack() as ctx:
        w_q = ctx.enter_context(nc.sbuf_tensor("w_q", [P, 2, KT, DM], F32R))
        w_o = ctx.enter_context(nc.sbuf_tensor("w_o", [P, 2, KT, DM], F32R))
        k_diag = ctx.enter_context(nc.sbuf_tensor("k_diag", [P, 2, 2 * KT, GK], F32R))
        v_diag = ctx.enter_context(nc.sbuf_tensor("v_diag", [P, 2, 3, 2 * KT, P], F32R))
        keys_and_values(nc, ctx, ctxT, (wkT, wvT, wqT, woT), b_k, b_v, k_dram, v_dram, w_q, w_o, k_diag, v_diag)
        attention(nc, x, mask, b_q, b_o, ident, k_dram, v_dram, x2_dram, w_q, w_o, k_diag, v_diag)
    feed_forward(nc, x2_dram, out, ident, gamma, beta, q1, s1, b1, q2, s2, b2)


def kernel(x, ctx_1024, mask_Bx1xSxS2_ik0, L0_xattn_w_q, L0_xattn_b_q, L0_xattn_w_k, L0_xattn_b_k, L0_xattn_w_v,
           L0_xattn_b_v, L0_xattn_w_out, L0_xattn_b_out, L0_ffn_ln_gamma, L0_ffn_ln_beta, L0_ffn_fc1_q,
           L0_ffn_fc1_scales, L0_ffn_fc1_bias, L0_ffn_fc2_q, L0_ffn_fc2_scales, L0_ffn_fc2_bias):
    import numpy as np
    import concourse.bacc as bacc
    from concourse.bass_utils import run_bass_kernel_spmd

    def column(v):
        return np.asarray(v).reshape(-1, P).T

    arrays = {
        "x": x,
        "ctxT": np.asarray(ctx_1024).reshape(CTX, DM).T,
        "mask": np.asarray(mask_Bx1xSxS2_ik0).reshape(BATCH, SEQ, KEYS),
        "wqT": np.asarray(L0_xattn_w_q).T,
        "b_q": column(L0_xattn_b_q),
        "wkT": np.asarray(L0_xattn_w_k).T,
        "b_k": column(L0_xattn_b_k),
        "wvT": np.asarray(L0_xattn_w_v).T,
        "b_v": L0_xattn_b_v,
        "woT": np.asarray(L0_xattn_w_out).T,
        "b_o": L0_xattn_b_out,
        "identity": np.eye(P, dtype=np.float32),
        "gamma": column(L0_ffn_ln_gamma),
        "beta": column(L0_ffn_ln_beta),
        "fc1_q": L0_ffn_fc1_q,
        "fc1_scales": L0_ffn_fc1_scales,
        "fc1_bias": column(L0_ffn_fc1_bias),
        "fc2_q": L0_ffn_fc2_q,
        "fc2_scales": L0_ffn_fc2_scales,
        "fc2_bias": L0_ffn_fc2_bias,
    }
    nc = bacc.Bacc("TRN2", target_bir_lowering=False, num_devices=1)
    given, args = {}, []
    for name, a in arrays.items():
        a = np.ascontiguousarray(a)
        given[f"in_{name}"] = a
        args.append(nc.dram_tensor(f"in_{name}", a.shape, mybir.dt.from_np(a.dtype), kind="ExternalInput").ap())
    out = nc.dram_tensor("out_x", (BATCH, SEQ, DM), F32, kind="ExternalOutput").ap()
    xattn_ffn(nc, *args, out)
    return run_bass_kernel_spmd(nc, [given], core_ids=[0]).results[0]["out_x"]
```

```python
from contextlib import ExitStack

import concourse.bass as bass
from concourse import mybir

F32 = mybir.dt.float32
F32R = mybir.dt.float32r
I32 = mybir.dt.int32
ALU = mybir.AluOpType
ACT = mybir.ActivationFunctionType
AX = mybir.AxisListType
RMAX = bass.bass_isa.ReduceOp.max

P = 128
HI, LO = 0, 1
PASSES = ((HI, HI), (HI, LO), (LO, HI))

BATCH, SEQ, DM = 16, 512, 512
KEYS = 77
HEADS, DK = 16, 32
FF = 2048
EPS = 1e-5
ZERO_POINT = 128.0
SCALE = float(DK) ** -0.5
MASKED = -1.0e30

TT = SEQ // P
KT = DM // P
HG = P // DK
GK = HG * KEYS
NF = FF // P
CUTS = (0, 103, 206, GK)
CTX = BATCH * KEYS
CHUNK_B = 4
CHUNK = CHUNK_B * KEYS
LAST = BATCH - 1


LOADS = 4


class AttentionHead:

    def __init__(self, buffers, semaphores, steps, under_stage_1):
        self.ident, self.bq, self.bo, self.x_sb = buffers
        self.const_in, self.bq_done, self.xn_done = semaphores
        self.load_x, self.token_stats, self.layernorm, self.finish_ln, self.make_xn = steps
        self.on_sync, self.on_vector, self.on_gpsimd, self.on_scalar = under_stage_1


def value_pieces():
    out = []
    for t in range(3):
        for j in range(HG):
            a, b = max(CUTS[t], j * KEYS), min(CUTS[t + 1], (j + 1) * KEYS)
            if a < b:
                out.append((t, a - CUTS[t], a - j * KEYS, b - a, j))
    return out


def wait(eng, sem, value):
    if isinstance(value, int) and value <= 0:
        return
    eng.wait_ge(sem, value)


def by_parity(b, par):
    return b - par if par else b


def one(ap, b):
    return ap[b:b + 1] if isinstance(b, int) else ap[bass.ds(b, 1)]


def attention_head(nc, outer, x, ident_dram, b_q, b_o):
    def sb(name, shape, dt=F32):
        return outer.enter_context(nc.sbuf_tensor(name, shape, dt))

    def sem(name):
        return outer.enter_context(nc.semaphore(name))

    ident = sb("ident", [P, P])
    bq_in = sb("bq_in", [P, KT])
    bq = sb("bq_col", [P, KT])
    bo = sb("bo_row", [P, DM])
    x_sb = sb("x_sb", [P, TT, DM])
    stats = sb("stats", [P, TT, 6])
    mv = sb("mv", [P, TT, 2])
    var_eps = sb("var_eps", [P, TT])
    neg_mean = sb("neg_mean", [P, TT])
    rstd = sb("rstd", [P, TT])
    shift = sb("shift", [P, TT])
    minus_half = sb("minus_half", [P, TT])
    carrier = sb("carrier", [P, 2])
    const_in, bq_done = sem("const_in"), sem("bq_done")
    x_in = sem("x_in")
    half_set, ln_own, var_done, rstd_done, ln_done, xn_done = (
        sem(n) for n in ("half_set", "ln_own", "var_done", "rstd_done", "ln_done", "xn_done"))

    def exists(b):
        return not isinstance(b, int) or 0 <= b < BATCH

    def load_x(sp, b):
        sp.dma_start(x_sb[:, :, :], one(x, b).rearrange("o (t p) n -> (o p) t n", p=P)).then_inc(x_in, 16)

    def token_stats(dve, b, tiles):
        if exists(b):
            if tiles[0] == 0:
                dve.wait_ge(x_in, b * 16 + 16)
                wait(dve, ln_done, b)
            for t in tiles:
                nc.vector.bn_stats(stats[:, t, :], x_sb[:, t, :]).then_inc(ln_own, 1)

    def layernorm(dve, b):
        if exists(b):
            dve.wait_ge(ln_own, b * 8 + 4)
            nc.vector.tensor_copy(carrier[:, 1:2], carrier[:, 0:1])
            for t in range(TT):
                nc.vector.bn_aggr(mv[:, t, :], stats[:, t, :]).then_inc(ln_own, 1)
            dve.wait_ge(ln_own, b * 8 + 8)
            nc.vector.tensor_scalar(var_eps[:, :], mv[:, :, 1], EPS, None, ALU.add).then_inc(var_done, 1)
            nc.vector.tensor_scalar(neg_mean[:, :], mv[:, :, 0], -1.0, None, ALU.mult).then_inc(var_done, 1)

    def finish_ln(pool, b):
        if exists(b):
            pool.wait_ge(var_done, b * 2 + 2)
            wait(pool, xn_done, b * TT)
            nc.gpsimd.tensor_tensor(rstd[:, :], var_eps[:, :], minus_half[:, :], ALU.pow).then_inc(rstd_done, 1)
            pool.wait_ge(rstd_done, b + 1)
            nc.gpsimd.tensor_tensor(shift[:, :], neg_mean[:, :], rstd[:, :], ALU.mult).then_inc(ln_done, 1)

    def make_xn(act, b, tiles):
        if exists(b):
            act.wait_ge(ln_done, b + 1)
            for t in tiles:
                nc.scalar.activation(x_sb[:, t, :], x_sb[:, t, :], ACT.Identity,
                                     scale=rstd[:, t:t + 1], bias=shift[:, t:t + 1]).then_inc(xn_done, 1)

    def on_sync(sp):
        load_x(sp, 0)
        sp.dma_start(ident[:, :], ident_dram).then_inc(const_in, 16)
        sp.dma_start(bq_in[:, :], b_q).then_inc(const_in, 16)
        sp.dma_start(bo[:, :], b_o.partition_broadcast(P)).then_inc(const_in, 16)

    def on_vector(dve):
        nc.vector.memset(carrier[:, 0:1], 0.0)
        token_stats(dve, 0, range(TT))
        layernorm(dve, 0)
        dve.wait_ge(const_in, 48)
        nc.vector.tensor_scalar(bq[:, :], bq_in[:, :], SCALE, None, ALU.mult).then_inc(bq_done, 1)

    def on_gpsimd(pool):
        nc.gpsimd.memset(minus_half[:, :], -0.5).then_inc(half_set, 1)
        pool.wait_ge(half_set, 1)
        finish_ln(pool, 0)

    def on_scalar(act):
        make_xn(act, 0, range(TT))

    return AttentionHead((ident, bq, bo, x_sb), (const_in, bq_done, xn_done),
                         (load_x, token_stats, layernorm, finish_ln, make_xn),
                         (on_sync, on_vector, on_gpsimd, on_scalar))


def keys_and_values(nc, head, ctxT, wT, b_k, b_v, k_dram, v_dram, w_q, w_o, k_diag, v_diag):
    ROWS = [(r, min(P, CTX - r)) for r in range(0, CTX, P)]
    NR = len(ROWS)
    NC = BATCH // CHUNK_B
    NB = 8
    NKO = 3
    NVO = 4
    with ExitStack() as ctx:
        def sb(name, shape, dt=F32):
            return ctx.enter_context(nc.sbuf_tensor(name, shape, dt))

        def sem(name):
            return ctx.enter_context(nc.semaphore(name))

        raw = [sb(f"w_raw{i}", [P, KT, DM]) for i in range(2)]
        ctx_raw = [sb(f"ctx_raw{i}", [P, KT, CHUNK]) for i in range(2)]
        w_k = sb("w_k", [P, 2, KT, DM], F32R)
        w_v = sb("w_v", [P, 2, KT, DM], F32R)
        ctx_s = sb("ctx_split", [P, 2, KT, CTX], F32R)
        bk = sb("bk_col", [P, KT])
        bv = sb("bv_row", [P, DM])
        k_out = [sb(f"k_out{i}", [P, 2, CHUNK], F32R) for i in range(NKO)]
        v32 = [raw[i][:, 0, :] for i in range(2)]
        v_out = [sb(f"v_out{i}", [P, 2, DM], F32R) for i in range(NVO)]
        bank = [ctx.enter_context(nc.psum_tensor(f"kv_bank{i}", [P, 512], F32)) for i in range(NB)]

        split_to = [w_k, w_v, w_q, w_o]
        factor = [1.0, 1.0, SCALE, 1.0]
        w_in = [sem(f"w_in{i}") for i in range(4)]
        c_in = [sem(f"ctx_in{i}") for i in range(NC)]
        bias_in = sem("kv_bias_in")
        w_hi, w_lo = sem("kv_w_hi"), sem("kv_w_lo")
        c_hi, c_lo = sem("ctx_hi"), sem("ctx_lo")
        full = sem("kv_full")
        k_hi, k_lo = sem("k_hi"), sem("k_lo")
        v_sum, v_hi, v_lo = sem("v_sum"), sem("v_hi"), sem("v_lo")
        k_kept = [sem(f"k_kept{i}") for i in range(NKO)]
        v_kept = [sem(f"v_kept{i}") for i in range(NVO)]
        block = ctx.enter_context(nc.Block())
        NK = NC * KT

        @block.sync
        def _(sp):
            def load_w(i):
                sp.dma_start(raw[i % 2][:, :, :], wT[i].rearrange("(k p) n -> p k n", p=P)).then_inc(w_in[i], 16)

            def load_ctx(c):
                sp.dma_start(ctx_raw[c % 2][:, :, :],
                             ctxT.rearrange("(k p) n -> p k n", p=P)[:, :, c * CHUNK:(c + 1) * CHUNK]
                             ).then_inc(c_in[c], 16)

            load_w(0)
            load_ctx(0)
            sp.dma_start(bk[:, :], b_k).then_inc(bias_in, 16)
            sp.dma_start(bv[:, :], b_v.partition_broadcast(P)).then_inc(bias_in, 16)
            load_ctx(1)
            load_w(1)
            for c in range(2, NC):
                sp.wait_ge(c_lo, c - 1)
                load_ctx(c)
            for i in range(2, 4):
                sp.wait_ge(w_lo, i - 1)
                load_w(i)
            head.on_sync(sp)
            for n in range(NK):
                c, g = n // KT, n % KT
                sp.wait_ge(k_lo, n + 1)
                for part in (HI, LO):
                    sp.dma_start(
                        k_dram[c * CHUNK_B:(c + 1) * CHUNK_B, :, part, g, :].rearrange("b p k -> p b k").bitcast(F32),
                        k_out[n % NKO][:, part, :].rearrange("p (b k) -> p b k", k=KEYS).bitcast(F32),
                    ).then_inc(k_kept[n % NKO], 16)
            for r, (row, rows) in enumerate(ROWS):
                sp.wait_ge(v_lo, r + 1)
                sp.dma_start(v_dram[row:row + rows, :].bitcast(F32),
                             v_out[r % NVO][0:rows, :, :].rearrange("p t n -> p (t n)").bitcast(F32)
                             ).then_inc(v_kept[r % NVO], 16)
            for i in range(NKO):
                sp.wait_ge(k_kept[i], 32 * len(range(i, NK, NKO)))
            for i in range(NVO):
                sp.wait_ge(v_kept[i], 16 * len(range(i, NR, NVO)))

        @block.gpsimd
        def _(pool):
            nc.gpsimd.memset(k_diag[:, :, :, :].bitcast(F32), 0.0)
            nc.gpsimd.memset(v_diag[:, :, :, :, :].bitcast(F32), 0.0)
            head.on_gpsimd(pool)

        @block.scalar
        def _(act):
            def hi_w(i):
                act.wait_ge(w_in[i], 16)
                nc.scalar.activation(split_to[i][:, HI, :, :], raw[i % 2][:, :, :], ACT.Copy,
                                     scale=factor[i]).then_inc(w_hi, 1)

            def hi_ctx(c):
                act.wait_ge(c_in[c], 16)
                nc.scalar.activation(ctx_s[:, HI, :, c * CHUNK:(c + 1) * CHUNK], ctx_raw[c % 2][:, :, :],
                                     ACT.Copy).then_inc(c_hi, 1)

            hi_w(0)
            hi_ctx(0)
            hi_ctx(1)
            hi_w(1)
            for c in range(2, NC):
                hi_ctx(c)
            act.wait_ge(bias_in, 32)
            for n in range(NK):
                c, g = n // KT, n % KT
                act.wait_ge(full, n + 1)
                if n >= NKO:
                    act.wait_ge(k_kept[n % NKO], 32 * (n // NKO))
                nc.scalar.activation(k_out[n % NKO][:, HI, :], bank[n % NB][:, 0:CHUNK], ACT.Identity,
                                     bias=bk[:, g:g + 1]).then_inc(k_hi, 1)
                if n in (4, 8):
                    hi_w(1 + n // 4)
            head.on_scalar(act)
            for r, (row, rows) in enumerate(ROWS):
                act.wait_ge(v_sum, r + 1)
                if r >= NVO:
                    act.wait_ge(v_kept[r % NVO], 16 * (r // NVO))
                nc.scalar.activation(v_out[r % NVO][0:rows, HI, :], v32[r % 2][0:rows, :], ACT.Copy).then_inc(v_hi, 1)

        @block.vector
        def _(dve):
            def lo_w(i):
                dve.wait_ge(w_hi, i + 1)
                nc.vector.scalar_tensor_tensor(
                    out=split_to[i][:, LO, :, :], in0=raw[i % 2][:, :, :], scalar=factor[i],
                    in1=split_to[i][:, HI, :, :].bitcast(F32), op0=ALU.mult, op1=ALU.subtract).then_inc(w_lo, 1)

            def lo_ctx(c):
                dve.wait_ge(c_hi, c + 1)
                cols = slice(c * CHUNK, (c + 1) * CHUNK)
                nc.vector.tensor_tensor(ctx_s[:, LO, :, cols], ctx_raw[c % 2][:, :, :],
                                        ctx_s[:, HI, :, cols].bitcast(F32), ALU.subtract).then_inc(c_lo, 1)

            lo_w(0)
            lo_ctx(0)
            lo_ctx(1)
            lo_w(1)
            for c in range(2, NC):
                lo_ctx(c)
            for n in range(NK):
                g = n % KT
                dve.wait_ge(k_hi, n + 1)
                nc.vector.scalar_tensor_tensor(
                    out=k_out[n % NKO][:, LO, :], in0=bank[n % NB][:, 0:CHUNK], scalar=bk[:, g:g + 1],
                    in1=k_out[n % NKO][:, HI, :].bitcast(F32), op0=ALU.add, op1=ALU.subtract).then_inc(k_lo, 1)
                if n in (4, 8):
                    lo_w(1 + n // 4)
                if n == NK - 2:
                    head.on_vector(dve)

            def lo_v(r):
                rows = ROWS[r][1]
                dve.wait_ge(v_hi, r + 1)
                nc.vector.tensor_tensor(v_out[r % NVO][0:rows, LO, :], v32[r % 2][0:rows, :],
                                        v_out[r % NVO][0:rows, HI, :].bitcast(F32), ALU.subtract).then_inc(v_lo, 1)

            for r, (row, rows) in enumerate(ROWS):
                dve.wait_ge(full, NK + r + 1)
                wait(dve, v_lo, r - 1)
                nc.vector.tensor_tensor(v32[r % 2][0:rows, :], bank[(NK + r) % NB][0:rows, :], bv[0:rows, :],
                                        ALU.add).then_inc(v_sum, 1)
                if r:
                    lo_v(r - 1)
            lo_v(NR - 1)

        @block.tensor
        def _(pe):
            for n in range(NK):
                c, g = n // KT, n % KT
                if n == 0:
                    pe.wait_ge(w_lo, 1)
                if g == 0:
                    pe.wait_ge(c_lo, c + 1)
                if n >= NB:
                    pe.wait_ge(k_lo, n - NB + 1)
                for i, (s, m) in enumerate(PASSES):
                    for k in range(KT):
                        mm = nc.tensor.matmul(bank[n % NB][:, 0:CHUNK], w_k[:, s, k, g * P:(g + 1) * P],
                                              ctx_s[:, m, k, c * CHUNK:(c + 1) * CHUNK],
                                              start=(i == 0 and k == 0), stop=(i == 2 and k == KT - 1))
                mm.then_inc(full, 1)
            pe.wait_ge(w_lo, 2)
            for r, (row, rows) in enumerate(ROWS):
                if r < NB:
                    pe.wait_ge(k_lo, NK - NB + 1 + r)
                else:
                    pe.wait_ge(v_sum, r - NB + 1)
                for i, (s, m) in enumerate(PASSES):
                    for k in range(KT):
                        mm = nc.tensor.matmul(bank[(NK + r) % NB][0:rows, :], ctx_s[:, s, k, row:row + rows],
                                              w_v[:, m, k, :],
                                              start=(i == 0 and k == 0), stop=(i == 2 and k == KT - 1))
                mm.then_inc(full, 1)


def attention_order():
    work = [(f"Q{g}", 0) for g in range(KT)]
    tile = [(f"A{k}", b) for b in range(2) for k in range(KT)]
    for b in range(BATCH):
        work += [("Q0", b + 1), ("O3", b - 2), ("V3", b - 1)]
        for g in range(1, KT):
            work += [(f"Q{g}", b + 1), (f"O{g - 1}", b - 1), (f"V{g - 1}", b)]
        tile += [(f"T{g}{t}", b) for g in range(KT) for t in range(3)] + [(f"A{k}", b + 2) for k in range(KT)]
    work += [("O3", LAST - 1), ("V3", LAST)] + [(f"O{t}", LAST) for t in range(TT)]
    orders = {}
    for ring in (work, tile):
        orders.update({x: n for n, x in enumerate(x for x in ring if 0 <= x[1] < BATCH)})
    return orders


ORDER = attention_order()
PER_SEQ = {"Q": 12, "V": 12, "O": 12, "A": 16, "T": 16}


def ordinal(what, b):
    if isinstance(b, int):
        return ORDER[(what, b)]
    middle = BATCH // 2
    return b * PER_SEQ[what[0]] + (ORDER[(what, middle)] - PER_SEQ[what[0]] * middle)


def bank_of(what, b):
    return ORDER[(what, b if isinstance(b, int) else BATCH // 2)] % 2


def attention(nc, head, x, mask, k_dram, v_dram, x2_dram, w_q, w_o, k_diag, v_diag):
    with ExitStack() as ctx:
        def sb(name, shape, dt=F32):
            return ctx.enter_context(nc.sbuf_tensor(name, shape, dt))

        def sem(name):
            return ctx.enter_context(nc.semaphore(name))

        ident, bq, bo, x_sb = head.ident, head.bq, head.bo, head.x_sb
        bq_done, xn_done = head.bq_done, head.xn_done
        xT = sb("xT", [P, 2, KT, SEQ], F32R)
        qT = sb("qT", [P, 2, 2, SEQ], F32R)
        prob = sb("prob", [P, KT, TT, GK])
        neg_peak = sb("neg_peak", [P, KT, TT * HG])
        total = sb("total", [P, KT, TT * HG])
        inv = sb("inv", [P, KT, TT * HG])
        pT = sb("pT", [P, 2, 2, 3, SEQ], F32R)
        aT = sb("aT", [P, 2, 2, KT, SEQ], F32R)
        res = sb("res", [P, TT, DM])
        mask_sb = sb("mask_sb", [P, 2, TT, KEYS], I32)
        bias = sb("bias", [P, 2, TT, KEYS])
        score = ctx.enter_context(nc.psum_tensor("score", [P, TT, 512], F32))
        work = [ctx.enter_context(nc.psum_tensor(f"work{i}", [P, 512], F32)) for i in range(2)]
        tbank = [ctx.enter_context(nc.psum_tensor(f"tbank{i}", [P, 512], F32)) for i in range(2)]

        mask_in, k_in, v_in = ([sem(f"{n}{i}") for i in range(2)] for n in ("mask_in", "k_in", "v_in"))
        res_in = [sem(f"res_in{t}") for t in range(TT)]
        x2_out = [sem(f"x2_out{t}") for t in range(TT)]
        bias_done, res_ready = sem("bias_done"), sem("res_ready")
        work_full, work_free = sem("work_full"), sem("work_free")
        t_full, t_hi, t_lo = sem("t_full"), sem("t_hi"), sem("t_lo")
        x_hi, q_hi, a_hi = sem("x_hi"), sem("q_hi"), sem("a_hi")
        score_full, masked, peaked = (sem(n) for n in ("score_full", "masked", "peaked"))
        exp_done, totalled, inverted, normed = (sem(n) for n in ("exp_done", "totalled", "inverted", "normed"))
        block = ctx.enter_context(nc.Block())

        def run(eng, start, body, end):
            start()
            body(0, 0)
            body(1, 1)
            with eng.Fori(1, BATCH // 2 - 1) as pair:
                body(pair * 2, 0)
                body(pair * 2 + 1, 1)
            body(BATCH - 2, 0)
            body(LAST, 1)
            end()

        def exists(b):
            return not isinstance(b, int) or 0 <= b < BATCH

        @block.sync
        def _(sp):
            def load_x(b):
                if exists(b):
                    sp.wait_ge(t_full, ordinal("A3", b - 1) + 1)
                    head.load_x(sp, b)

            def load_mask(b, par):
                if exists(b):
                    wait(sp, bias_done, b - 1)
                    sp.dma_start(mask_sb[:, par, :, :],
                                 one(mask, b).rearrange("o (t p) k -> (o p) t k", p=P)).then_inc(mask_in[par], 16)

            def load_k(b, par):
                if exists(b):
                    wait(sp, score_full, b * KT - KT)
                    for j in range(HG):
                        rows = slice(j * DK, (j + 1) * DK)
                        sp.dma_start(
                            k_diag[rows, par, :, j * KEYS:(j + 1) * KEYS].bitcast(F32),
                            one(k_dram, b)[:, rows, :, :, :].rearrange("o p t g k -> (o p) (t g) k").bitcast(F32),
                        ).then_inc(k_in[par], 16)

            def load_v(b, par):
                if exists(b):
                    if not (isinstance(b, int) and b < 2):
                        sp.wait_ge(work_full, ordinal("V3", b - 2) + 1)
                    seqs = v_dram.rearrange("(b k) (m d) -> b k m d", k=KEYS, d=P)
                    for t, row, key, n, j in value_pieces():
                        sp.dma_start(
                            v_diag[row:row + n, par, t, :, j * DK:(j + 1) * DK].bitcast(F32),
                            one(seqs, b)[:, key:key + n, :, j * DK:(j + 1) * DK]
                            .rearrange("o k m d -> (o k) m d").bitcast(F32),
                        ).then_inc(v_in[par], 16)

            def load_res(b, t):
                if exists(b):
                    wait(sp, x2_out[t], b * 16)
                    sp.dma_start(res[:, t, :], one(x, b)[:, t * P:(t + 1) * P, :].rearrange("o p n -> (o p) n")
                                 ).then_inc(res_in[t], 16)

            def store_x2(b, t):
                if exists(b):
                    sp.wait_ge(work_free, ordinal(f"O{t}", b) + 1)
                    sp.dma_start(one(x2_dram, b)[:, t * P:(t + 1) * P, :].rearrange("o p n -> (o p) n"),
                                 res[:, t, :]).then_inc(x2_out[t], 16)

            def start():
                load_k(0, 0)
                load_mask(0, 0)
                load_x(1)
                load_k(1, 1)
                load_mask(1, 1)
                load_v(0, 0)

            def body(b, par):
                load_res(b - 1, 0)
                load_x(b + 2)
                load_res(b - 1, 1)
                load_res(b - 1, 2)
                load_k(b + 2, par)
                store_x2(b - 2, 3)
                load_v(b + 1, 1 - par)
                load_res(b - 1, 3)
                load_mask(b + 2, par)
                for t in range(3):
                    store_x2(b - 1, t)

            def end():
                store_x2(LAST - 1, 3)
                for t in range(TT):
                    load_res(LAST, t)
                for t in range(TT):
                    store_x2(LAST, t)
                for t in range(TT):
                    sp.wait_ge(x2_out[t], 16 * BATCH)

            run(sp, start, body, end)

        @block.gpsimd
        def _(pool):
            def add_bo(b, t):
                if exists(b):
                    pool.wait_ge(res_in[t], b * 16 + 16)
                    nc.gpsimd.tensor_tensor(res[:, t, :], res[:, t, :], bo[:, :], ALU.add).then_inc(res_ready, 1)

            def norm(b, g):
                if exists(b):
                    pool.wait_ge(inverted, b * KT + (g + 1))
                    p = prob[:, g, :, :].rearrange("p t (h k) -> p (t h) k", k=KEYS)
                    nc.gpsimd.tensor_tensor(p, p, inv[:, g, :].unsqueeze(2).to_broadcast([P, TT * HG, KEYS]),
                                            ALU.mult).then_inc(normed, 1)

            def start():
                head.finish_ln(pool, 1)
                norm(0, 0)

            def body(b, par):
                norm(b, 1)
                add_bo(b - 1, 0)
                norm(b, 2)
                add_bo(b - 1, 1)
                norm(b, 3)
                head.finish_ln(pool, b + 2)
                add_bo(b - 1, 2)
                norm(b + 1, 0)
                add_bo(b - 1, 3)

            def end():
                for t in range(TT):
                    add_bo(LAST, t)

            run(pool, start, body, end)

        @block.scalar
        def _(act):
            def x_his(b, k):
                if exists(b):
                    act.wait_ge(t_full, ordinal(f"A{k}", b) + 1)
                    if k == 0 and exists(b - 1):
                        act.wait_ge(work_full, ordinal("Q3", b - 1) + 1)
                    nc.scalar.activation(xT[:, HI, k, :], tbank[bank_of(f"A{k}", b)][:, :],
                                         ACT.Copy).then_inc(x_hi, 1)

            def q_his(b, g):
                if exists(b):
                    act.wait_ge(work_full, ordinal(f"Q{g}", b) + 1)
                    wait(act, score_full, b * KT + (g - 1))
                    nc.scalar.activation(qT[:, g % 2, HI, :], work[bank_of(f"Q{g}", b)][:, :], ACT.Identity,
                                         bias=bq[:, g:g + 1]).then_inc(q_hi, 1)

            def t_his(b, g, t):
                n = CUTS[t + 1] - CUTS[t]
                act.wait_ge(t_full, ordinal(f"T{g}{t}", b) + 1)
                if t == 0:
                    if g >= 2:
                        act.wait_ge(work_full, ordinal(f"V{g - 2}", b) + 1)
                    elif exists(b - 1):
                        act.wait_ge(work_full, ordinal(f"V{g + 2}", b - 1) + 1)
                nc.scalar.activation(pT[0:n, g % 2, HI, t, :], tbank[bank_of(f"T{g}{t}", b)][0:n, :],
                                     ACT.Copy).then_inc(t_hi, 1)

            def exps(b, g, t):
                if exists(b):
                    if t == 0:
                        act.wait_ge(peaked, b * KT + (g + 1))
                    for j in range(HG):
                        tile = prob[:, g, t, j * KEYS:(j + 1) * KEYS]
                        ins = nc.scalar.activation(tile, tile, ACT.Exp, scale=1.0,
                                                   bias=neg_peak[:, g, t * HG + j:t * HG + j + 1])
                    if t == TT - 1:
                        ins.then_inc(exp_done, 1)

            def a_his(b, par, g):
                if exists(b):
                    act.wait_ge(work_full, ordinal(f"V{g}", b) + 1)
                    if g == 0 and exists(b - 2):
                        act.wait_ge(work_full, ordinal("O3", b - 2) + 1)
                    nc.scalar.activation(aT[:, par, HI, g, :], work[bank_of(f"V{g}", b)][:, :],
                                         ACT.Copy).then_inc(a_hi, 1)

            def start():
                for k in range(KT):
                    x_his(0, k)
                act.wait_ge(bq_done, 1)
                for g in range(KT):
                    q_his(0, g)
                head.make_xn(act, 1, range(TT))
                for t in range(TT):
                    exps(0, 0, t)
                for k in range(KT):
                    x_his(1, k)
                for t in range(TT):
                    exps(0, 1, t)

            def body(b, par):
                for g in range(KT):
                    eb, eg = (b, g + 2) if g < 2 else (b + 1, g - 2)
                    t_his(b, g, 0)
                    t_his(b, g, 1)
                    exps(eb, eg, 0)
                    exps(eb, eg, 1)
                    t_his(b, g, 2)
                    exps(eb, eg, 2)
                    q_his(b + 1, g)
                    if g == 2:
                        head.make_xn(act, b + 2, (0, 1))
                    exps(eb, eg, 3)
                    if g == 2:
                        head.make_xn(act, b + 2, (2, 3))
                    if g == 3:
                        for k in range(KT):
                            x_his(b + 2, k)
                    if g == 0:
                        a_his(b - 1, 1 - par, 3)
                    else:
                        a_his(b, par, g - 1)

            def end():
                a_his(LAST, 1, 3)

            run(act, start, body, end)

        @block.vector
        def _(dve):
            def make_bias(b, par):
                if exists(b):
                    dve.wait_ge(mask_in[par], by_parity(b, par) * 8 + 16)
                    nc.vector.tensor_scalar(bias[:, par, :, :], mask_sb[:, par, :, :], 0.0, MASKED,
                                            ALU.is_equal, ALU.mult).then_inc(bias_done, 1)

            def x_los(b, k):
                if exists(b):
                    dve.wait_ge(x_hi, b * KT + (k + 1))
                    nc.vector.tensor_tensor(xT[:, LO, k, :], tbank[bank_of(f"A{k}", b)][:, :],
                                            xT[:, HI, k, :].bitcast(F32), ALU.subtract).then_inc(t_lo, 1)

            def q_los(b, g):
                if exists(b):
                    dve.wait_ge(q_hi, b * KT + (g + 1))
                    nc.vector.scalar_tensor_tensor(
                        out=qT[:, g % 2, LO, :], in0=work[bank_of(f"Q{g}", b)][:, :], scalar=bq[:, g:g + 1],
                        in1=qT[:, g % 2, HI, :].bitcast(F32), op0=ALU.add, op1=ALU.subtract).then_inc(work_free, 1)

            def t_los(b, g, t):
                n = CUTS[t + 1] - CUTS[t]
                dve.wait_ge(t_hi, (b * KT + g) * 3 + (t + 1))
                nc.vector.tensor_tensor(pT[0:n, g % 2, LO, t, :], tbank[bank_of(f"T{g}{t}", b)][0:n, :],
                                        pT[0:n, g % 2, HI, t, :].bitcast(F32), ALU.subtract).then_inc(t_lo, 1)

            def a_los(b, par, g):
                if exists(b):
                    dve.wait_ge(a_hi, b * KT + (g + 1))
                    nc.vector.tensor_tensor(aT[:, par, LO, g, :], work[bank_of(f"V{g}", b)][:, :],
                                            aT[:, par, HI, g, :].bitcast(F32), ALU.subtract).then_inc(work_free, 1)

            def mask_scores(b, par, g):
                if exists(b):
                    dve.wait_ge(score_full, b * KT + (g + 1))
                    if g == 0:
                        dve.wait_ge(bias_done, b + 1)
                    if exists(b - 1):
                        dve.wait_ge(t_full, ordinal(f"T{g}2", b - 1) + 1)
                    nc.vector.tensor_tensor(
                        prob[:, g, :, :].rearrange("p t (h k) -> p t h k", k=KEYS),
                        score[:, :, 0:GK].rearrange("p t (h k) -> p t h k", k=KEYS),
                        bias[:, par, :, :].unsqueeze(2).to_broadcast([P, TT, HG, KEYS]),
                        ALU.add).then_inc(masked, 1)

            def by_head(g):
                return prob[:, g, :, :].rearrange("p t (h k) -> p (t h) k", k=KEYS)

            def peaks(b, g):
                if exists(b):
                    dve.wait_ge(masked, b * KT + (g + 1))
                    nc.vector.tensor_reduce(neg_peak[:, g, :], by_head(g), AX.X, ALU.max,
                                            negate=True).then_inc(peaked, 1)

            def totals(b, g):
                if exists(b):
                    dve.wait_ge(exp_done, b * KT + (g + 1))
                    nc.vector.tensor_reduce(total[:, g, :], by_head(g), AX.X, ALU.add).then_inc(totalled, 1)
                    dve.wait_ge(totalled, b * KT + (g + 1))
                    nc.vector.reciprocal(inv[:, g, :], total[:, g, :]).then_inc(inverted, 1)

            def project(b, t):
                if exists(b):
                    dve.wait_ge(work_full, ordinal(f"O{t}", b) + 1)
                    dve.wait_ge(res_ready, b * TT + (t + 1))
                    nc.vector.tensor_tensor(res[:, t, :], work[bank_of(f"O{t}", b)][:, :], res[:, t, :],
                                            ALU.add).then_inc(work_free, 1)

            def start():
                for k in range(KT):
                    x_los(0, k)
                dve.wait_ge(bq_done, 1)
                q_los(0, 0)
                q_los(0, 1)
                make_bias(0, 0)
                mask_scores(0, 0, 0)
                q_los(0, 2)
                peaks(0, 0)
                mask_scores(0, 0, 1)
                q_los(0, 3)
                head.token_stats(dve, 1, range(TT))
                head.layernorm(dve, 1)
                peaks(0, 1)
                mask_scores(0, 0, 2)
                peaks(0, 2)
                for k in range(KT):
                    x_los(1, k)
                totals(0, 0)
                totals(0, 1)

            def body(b, par):
                for g in range(KT):
                    t_los(b, g, 0)
                    t_los(b, g, 1)
                    if g == 0:
                        mask_scores(b, par, 3)
                    else:
                        mask_scores(b + 1, 1 - par, g - 1)
                    t_los(b, g, 2)
                    if g == 0:
                        peaks(b, 3)
                    else:
                        peaks(b + 1, g - 1)
                    q_los(b + 1, g)
                    if g == 3:
                        x_los(b + 2, 0)
                        x_los(b + 2, 1)
                    if g == 0:
                        project(b - 2, 3)
                        make_bias(b + 1, 1 - par)
                        head.token_stats(dve, b + 2, (0, 1))
                        totals(b, 2)
                        a_los(b - 1, 1 - par, 3)
                    else:
                        project(b - 1, g - 1)
                        if g == 1:
                            head.token_stats(dve, b + 2, (2, 3))
                            totals(b, 3)
                            head.layernorm(dve, b + 2)
                        else:
                            totals(b + 1, g - 2)
                        if g == 3:
                            x_los(b + 2, 2)
                            x_los(b + 2, 3)
                        a_los(b, par, g - 1)

            def end():
                project(LAST - 1, 3)
                a_los(LAST, 1, 3)
                for t in range(TT):
                    project(LAST, t)

            run(dve, start, body, end)

        @block.tensor
        def _(pe):
            def free_bank(what, b):
                wait(pe, work_free, ordinal(what, b) - 1)
                return work[bank_of(what, b)]

            def free_tile_bank(what, b):
                wait(pe, t_lo, ordinal(what, b) - 1)
                return tbank[bank_of(what, b)]

            def transpose_x(b, k):
                if exists(b):
                    if k == 0:
                        pe.wait_ge(xn_done, b * TT + TT)
                    to = free_tile_bank(f"A{k}", b)
                    for t in range(TT):
                        mm = nc.tensor.transpose(to[:, t * P:(t + 1) * P], x_sb[:, t, k * P:(k + 1) * P],
                                                 ident[:, :])
                    mm.then_inc(t_full, 1)

            def queries(b, g):
                if exists(b):
                    to = free_bank(f"Q{g}", b)
                    if g == 0:
                        pe.wait_ge(t_lo, ordinal("A3", b) + 1)
                    for i, (s, m) in enumerate(PASSES):
                        for k in range(KT):
                            mm = nc.tensor.matmul(to[:, :], w_q[:, s, k, g * P:(g + 1) * P], xT[:, m, k, :],
                                                  start=(i == 0 and k == 0), stop=(i == 2 and k == KT - 1))
                    mm.then_inc(work_full, 1)

            def scores(b, par, g):
                if exists(b):
                    pe.wait_ge(work_free, ordinal(f"Q{g}", b) + 1)
                    if g == 0:
                        pe.wait_ge(k_in[par], by_parity(b, par) * (8 * HG) + 16 * HG)
                    wait(pe, masked, b * KT + g)
                    for t in range(TT):
                        for i, (s, m) in enumerate(PASSES):
                            mm = nc.tensor.matmul(score[:, t, 0:GK], qT[:, g % 2, s, t * P:(t + 1) * P],
                                                  k_diag[:, par, m * KT + g, :], start=(i == 0), stop=(i == 2))
                    mm.then_inc(score_full, 1)

            def transpose_p(b, g, t):
                if t == 0:
                    pe.wait_ge(normed, b * KT + (g + 1))
                to = free_tile_bank(f"T{g}{t}", b)
                for tt in range(TT):
                    mm = nc.tensor.transpose(to[0:CUTS[t + 1] - CUTS[t], tt * P:(tt + 1) * P],
                                             prob[:, g, tt, CUTS[t]:CUTS[t + 1]], ident[:, :])
                mm.then_inc(t_full, 1)

            def weigh_values(b, par, g):
                if exists(b):
                    to = free_bank(f"V{g}", b)
                    pe.wait_ge(t_lo, ordinal(f"T{g}2", b) + 1)
                    if g == 0:
                        pe.wait_ge(v_in[par], (by_parity(b, par) + 2) * (8 * len(value_pieces())))
                    for t in range(3):
                        n = CUTS[t + 1] - CUTS[t]
                        for i, (s, m) in enumerate(PASSES):
                            mm = nc.tensor.matmul(to[:, :], v_diag[0:n, par, t, s * KT + g, :],
                                                  pT[0:n, g % 2, m, t, :],
                                                  start=(t == 0 and i == 0), stop=(t == 2 and i == 2))
                    mm.then_inc(work_full, 1)

            def project(b, par, t):
                if exists(b):
                    to = free_bank(f"O{t}", b)
                    if t == 0:
                        pe.wait_ge(work_free, ordinal("V3", b) + 1)
                    for i, (s, m) in enumerate(PASSES):
                        for g in range(KT):
                            mm = nc.tensor.matmul(to[:, :], aT[:, par, s, g, t * P:(t + 1) * P], w_o[:, m, g, :],
                                                  start=(i == 0 and g == 0), stop=(i == 2 and g == KT - 1))
                    mm.then_inc(work_full, 1)

            def start():
                pe.wait_ge(head.const_in, 48)
                for k in range(KT):
                    transpose_x(0, k)
                queries(0, 0)
                queries(0, 1)
                scores(0, 0, 0)
                queries(0, 2)
                scores(0, 0, 1)
                queries(0, 3)
                scores(0, 0, 2)
                for k in range(KT):
                    transpose_x(1, k)

            def body(b, par):
                for g in range(KT):
                    transpose_p(b, g, 0)
                    transpose_p(b, g, 1)
                    if g == 0:
                        scores(b, par, 3)
                    else:
                        scores(b + 1, 1 - par, g - 1)
                    transpose_p(b, g, 2)
                    queries(b + 1, g)
                    if g == 0:
                        project(b - 2, par, 3)
                        weigh_values(b - 1, 1 - par, 3)
                    else:
                        if g == 3:
                            transpose_x(b + 2, 0)
                            transpose_x(b + 2, 1)
                        project(b - 1, 1 - par, g - 1)
                        if g == 3:
                            transpose_x(b + 2, 2)
                            transpose_x(b + 2, 3)
                        weigh_values(b, par, g - 1)

            def end():
                project(LAST - 1, 0, 3)
                weigh_values(LAST, 1, 3)
                for t in range(TT):
                    project(LAST, 1, t)

            run(pe, start, body, end)


def feed_forward(nc, x2_dram, out, ident_dram, gamma, beta, q1, s1, b1, q2, s2, b2):
    with ExitStack() as ctx:
        def sb(name, shape, dt=F32):
            return ctx.enter_context(nc.sbuf_tensor(name, shape, dt))

        def sem(name):
            return ctx.enter_context(nc.semaphore(name))

        ident = sb("ident3", [P, P])
        w1_at = nc.sbuf_base
        w1_lo = sb("w1_lo", [P, KT, FF], F32R)
        w1_codes = nc.alloc_sbuf_tensor_at("w1_codes", [P, KT, FF], I32, offset=w1_at)
        w1_f = nc.alloc_sbuf_tensor_at("w1_f", [P, KT, FF], F32, offset=w1_at)
        w2_at = nc.sbuf_base
        w2 = sb("w2", [P, 2, NF, DM], F32R)
        w2_codes = nc.alloc_sbuf_tensor_at("w2_codes", [P, 2, NF, DM], I32, offset=w2_at)
        w2_f = nc.alloc_sbuf_tensor_at("w2_f", [P, 2, NF, DM], F32, offset=w2_at)
        w1_hi = sb("w1_hi", [P, KT, FF], F32R)
        lo_peak = sb("lo_peak", [P, NF * KT])
        row_peak, any_peak = sb("row_peak", [P, 1]), sb("any_peak", [P, 1])
        lo_used = sb("lo_used", [P, 1], I32)
        hT = [sb(f"hT{i}", [P, 2, KT, SEQ], F32R) for i in range(2)]
        gam, bet = sb("gamma_col", [P, KT]), sb("beta_col", [P, KT])
        s1_col = sb("s1_col", [P, KT, NF])
        b1_col = sb("b1_col", [P, NF])
        b2_half = sb("b2_half", [P, DM])
        x2 = sb("x2", [P, 2, TT, DM])
        h = sb("h", [P, TT, DM])
        h_f = sb("h_f", [P, 2, SEQ])
        stats, mv = sb("stats3", [P, TT, 6]), sb("mv3", [P, TT, 2])
        var_eps, rstds = sb("var_eps3", [P, 2, TT]), sb("rstds", [P, 2, TT])
        neg_mean, minus_half = sb("neg_mean3", [P, TT]), sb("minus_half3", [P, 2, TT])
        carrier = sb("carrier3", [P, 2])
        h_scale, h_shift = rstds[:, 1, :], sb("h_shift", [P, TT])
        u_scale, u_shift = sb("u_scale", [P, TT]), sb("u_shift", [P, TT])
        y = sb("y", [P, 2, SEQ])
        th = sb("th", [P, 2, SEQ])
        a = sb("a", [P, 2, 2, SEQ], F32R)
        acc = ctx.enter_context(nc.psum_tensor("acc", [P, TT, 512], F32))
        g_bank = [ctx.enter_context(nc.psum_tensor(f"g_bank{k}", [P, 512], F32)) for k in range(KT)]

        const_in, b2_done = sem("const_in3"), sem("b2_done")
        w_in = [sem(f"w_in3_{i}") for i in range(LOADS)]
        c_f, w_f, w2_hi, w2_lo = (sem(n) for n in ("c_f", "w_f", "w2_hi", "w2_lo"))
        c_hi, c_lo, peaked, all_peaked, lo_known = (
            sem(n) for n in ("c_hi", "c_lo", "lo_peaked", "lo_all_peaked", "lo_known"))
        any_peaked = sem("lo_any_peaked")
        x2_in = [sem(f"x2_in{i}") for i in range(2)]
        out_kept = [sem(f"out_kept{i}") for i in range(2)]
        half_set, own, var_done, rstd_done, ln_done = (
            sem(n) for n in ("half_set3", "ln_own3", "var_done3", "rstd_done3", "ln_done3"))
        h_done, r_done, res_done = sem("h_done"), sem("r_done"), sem("res_done")
        h_full, h_scaled, h_hi, h_lo = sem("h_full"), sem("h_scaled"), sem("h_hi"), sem("h_lo")
        g_full, y_begun, added, th_done, a_done, a_hi, a_lo = (
            sem(n) for n in ("g_full", "y_begun", "added", "th_done", "a_done", "a_hi3", "a_lo3"))
        f2_done, acc_full, out_ready = sem("f2_done"), sem("acc_full"), sem("out_ready")
        block = ctx.enter_context(nc.Block())

        AHEAD = 2
        ADDS = KT - 1
        NEXT_STATS = {4: 0, 5: 1, 6: 2, 7: 3}
        NEXT_ROWS = {8: (0, 1), 9: (2, 3)}
        NEXT_H = {10: 0, 11: 1, 12: 2, 13: 3}
        NEXT_RES = {12: (0, 1), 13: (2, 3)}
        H_EARLY = (0, 1)

        def run(eng, start, body, end):
            start()
            body(0, 0)
            body(1, 1)
            with eng.Fori(1, BATCH // 2 - 1) as pair:
                body(pair * 2, 0)
                body(pair * 2 + 1, 1)
            body(BATCH - 2, 0)
            body(LAST, 1)
            end()

        def exists(b):
            return not isinstance(b, int) or 0 <= b < BATCH

        def first(b):
            return isinstance(b, int) and b == 0

        def back(b, f, steps):
            return (b, f - steps) if f >= steps else (b - 1, f - steps + NF)

        @block.sync
        def _(sp):
            def load_x2(b, par):
                if exists(b):
                    if exists(b - 2):
                        sp.wait_ge(out_kept[par], by_parity(b, par) * (8 * TT))
                    sp.dma_start(x2[:, par, :, :], one(x2_dram, b).rearrange("o (t p) n -> (o p) t n", p=P)
                                 ).then_inc(x2_in[par], 16)

            def store(b, par):
                if exists(b):
                    for t in range(TT):
                        sp.wait_ge(out_ready, b * TT + (t + 1))
                        sp.dma_start(one(out, b)[:, t * P:(t + 1) * P, :].rearrange("o p n -> (o p) n"),
                                     x2[:, par, t, :]).then_inc(out_kept[par], 16)

            def load_w(f):
                if f >= LOADS:
                    sp.wait_ge(w2_lo, f - LOADS + 1)
                cols = slice(f * P, (f + 1) * P)
                sp.dma_start(w1_codes[:, :, cols], q1.rearrange("(k p) n -> p k n", p=P)[:, :, cols]
                             ).then_inc(w_in[f % LOADS], 16)
                sp.dma_start(w2_codes[:, LO, f, :], q2[cols, :]).then_inc(w_in[f % LOADS], 16)
                sp.dma_start(w2_f[:, HI, f, :], s2[f, :].partition_broadcast(P)).then_inc(w_in[f % LOADS], 16)

            def start():
                load_x2(0, 0)
                load_w(0)
                for to, of in ((ident, ident_dram), (gam, gamma), (bet, beta), (b1_col, b1)):
                    sp.dma_start(to[:, :], of).then_inc(const_in, 16)
                sp.dma_start(s1_col[:, :, :], s1).then_inc(const_in, 16)
                load_w(1)
                sp.dma_start(b2_half[:, :], b2.partition_broadcast(P)).then_inc(const_in, 16)
                load_w(2)
                load_x2(1, 1)
                for f in range(3, NF):
                    load_w(f)

            def body(b, par):
                if not first(b):
                    store(b - 1, 1 - par)
                    load_x2(b + 1, 1 - par)

            def end():
                store(LAST, 1)
                for i in range(2):
                    sp.wait_ge(out_kept[i], 8 * TT * BATCH)

            run(sp, start, body, end)

        @block.gpsimd
        def _(pool):
            def residual(b, par, tiles):
                if exists(b):
                    for t in tiles:
                        pool.wait_ge(r_done, b * TT + (t + 1))
                        nc.gpsimd.tensor_tensor(x2[:, par, t, :], x2[:, par, t, :], b2_half[:, :],
                                                ALU.add).then_inc(res_done, 1)

            def finish_ln(b):
                if exists(b):
                    pool.wait_ge(var_done, b * 3 + 3)
                    wait(pool, r_done, b * TT)
                    nc.gpsimd.tensor_tensor(rstds[:, :, :], var_eps[:, :, :], minus_half[:, :, :],
                                            ALU.pow).then_inc(rstd_done, 1)
                    pool.wait_ge(rstd_done, b + 1)
                    nc.gpsimd.tensor_tensor(h_shift[:, :], neg_mean[:, :], h_scale, ALU.mult).then_inc(ln_done, 1)
                    nc.gpsimd.tensor_tensor(u_shift[:, :], neg_mean[:, :], rstds[:, 0, :], ALU.mult).then_inc(ln_done, 1)
                    nc.gpsimd.tensor_scalar(u_scale[:, :], rstds[:, 0, :], 1.0, None, ALU.add).then_inc(ln_done, 1)

            def code_lo(f):
                cols = slice(f * P, (f + 1) * P)
                pool.wait_ge(c_hi, f + 1)
                nc.gpsimd.tensor_tensor(w1_lo[:, :, cols], w1_f[:, :, cols], w1_hi[:, :, cols].bitcast(F32),
                                        ALU.subtract).then_inc(c_lo, 1)

            def h_los(b, par, k):
                if exists(b):
                    pool.wait_ge(h_hi, b * KT + (k + 1))
                    nc.gpsimd.tensor_tensor(hT[par][:, LO, k, :], h_f[:, k % 2, :],
                                            hT[par][:, HI, k, :].bitcast(F32), ALU.subtract).then_inc(h_lo, 1)

            def a_los(b, f):
                if exists(b):
                    pool.wait_ge(a_hi, b * NF + (f + 1))
                    nc.gpsimd.tensor_tensor(a[:, f % 2, LO, :], y[:, f % 2, :], a[:, f % 2, HI, :].bitcast(F32),
                                            ALU.subtract).then_inc(a_lo, 1)

            def start():
                nc.gpsimd.memset(minus_half[:, :, :], -0.5).then_inc(half_set, 1)
                pool.wait_ge(half_set, 1)
                finish_ln(0)
                code_lo(0)
                for k in range(KT):
                    h_los(0, 0, k)
                code_lo(1)
                pool.wait_ge(b2_done, 1)

            def body(b, par):
                for f in range(NF):
                    if f - 1 in NEXT_H and NEXT_H[f - 1] not in H_EARLY:
                        h_los(b + 1, 1 - par, NEXT_H[f - 1])
                    if f == min(NEXT_ROWS):
                        finish_ln(b + 1)
                    a_los(*back(b, f, 1))
                    if first(b) and f + AHEAD < NF:
                        code_lo(f + AHEAD)
                    if first(b) and f in (4, 5):
                        residual(0, 0, (2 * (f - 4), 2 * (f - 4) + 1))
                    if f in NEXT_H and NEXT_H[f] in H_EARLY:
                        h_los(b + 1, 1 - par, NEXT_H[f])
                    if f - 2 in NEXT_RES:
                        residual(b + 1, 1 - par, NEXT_RES[f - 2])
                if first(b):
                    pool.wait_ge(all_peaked, 1)
                    nc.gpsimd.partition_all_reduce(any_peak[:, :], row_peak[:, :], P, RMAX).then_inc(any_peaked, 1)

            def end():
                a_los(LAST, NF - 1)

            run(pool, start, body, end)

        @block.scalar
        def _(act):
            def make_h(b, par, tiles):
                if exists(b):
                    if tiles[0] == 0:
                        act.wait_ge(ln_done, b * 3 + 3)
                        if exists(b - 1):
                            act.wait_ge(h_full, b * KT)
                    for t in tiles:
                        nc.scalar.activation(h[:, t, :], x2[:, par, t, :], ACT.Identity,
                                             scale=rstds[:, 1, t:t + 1], bias=h_shift[:, t:t + 1]).then_inc(h_done, 1)

            def make_r(b, par, tiles):
                if exists(b):
                    for t in tiles:
                        act.wait_ge(h_done, b * TT + (t + 1))
                        nc.scalar.activation(x2[:, par, t, :], x2[:, par, t, :], ACT.Identity,
                                             scale=u_scale[:, t:t + 1], bias=u_shift[:, t:t + 1]).then_inc(r_done, 1)

            def h_his(b, par, k):
                if exists(b):
                    act.wait_ge(h_full, b * KT + (k + 1))
                    wait(act, h_lo, b * KT + (k - 1))
                    nc.scalar.activation(h_f[:, k % 2, :], g_bank[k][:, :], ACT.Identity,
                                         scale=gam[:, k:k + 1], bias=bet[:, k:k + 1]).then_inc(h_scaled, 1)
                    act.wait_ge(h_scaled, b * KT + (k + 1))
                    if k == 0 and exists(b - 2):
                        act.wait_ge(g_full, (b - 1) * (NF * KT))
                    nc.scalar.activation(hT[par][:, HI, k, :], h_f[:, k % 2, :], ACT.Copy).then_inc(h_hi, 1)

            def split_w(f):
                act.wait_ge(c_f, f + 1)
                cols = slice(f * P, (f + 1) * P)
                nc.scalar.activation(w1_hi[:, :, cols], w1_f[:, :, cols], ACT.Copy).then_inc(c_hi, 1)
                act.wait_ge(w_f, f + 1)
                nc.scalar.activation(w2[:, HI, f, :], w2_f[:, LO, f, :], ACT.Copy,
                                     scale=0.25).then_inc(w2_hi, 1)

            def begin(b, f):
                n = b * NF + f
                act.wait_ge(g_full, n * KT + 1)
                wait(act, a_lo, n - 1)
                nc.scalar.activation(y[:, f % 2, :], g_bank[0][:, :], ACT.Identity, scale=s1_col[:, 0, f:f + 1],
                                     bias=b1_col[:, f:f + 1]).then_inc(y_begun, 1)

            def tanh(b, f):
                if exists(b):
                    act.wait_ge(added, (b * NF + (f + 1)) * ADDS)
                    nc.scalar.activation(th[:, f % 2, :], y[:, f % 2, :], ACT.Tanh, scale=0.5).then_inc(th_done, 1)

            def a_his(b, f):
                if exists(b):
                    n = b * NF + f
                    act.wait_ge(a_done, n + 1)
                    wait(act, f2_done, n - 1)
                    nc.scalar.activation(a[:, f % 2, HI, :], y[:, f % 2, :], ACT.Copy).then_inc(a_hi, 1)

            def start():
                act.wait_ge(const_in, 96)
                make_h(0, 0, range(TT))
                split_w(0)
                for k in range(KT):
                    h_his(0, 0, k)
                split_w(1)
                make_r(0, 0, range(TT))

            def body(b, par):
                for f in range(NF):
                    if f - 1 in NEXT_H and NEXT_H[f - 1] not in H_EARLY:
                        h_his(b + 1, 1 - par, NEXT_H[f - 1])
                    begin(b, f)
                    tanh(*back(b, f, 1))
                    a_his(*back(b, f, 1))
                    if f in NEXT_H and NEXT_H[f] in H_EARLY:
                        h_his(b + 1, 1 - par, NEXT_H[f])
                    if first(b) and f + AHEAD < NF:
                        split_w(f + AHEAD)
                    if f in NEXT_ROWS:
                        make_h(b + 1, 1 - par, NEXT_ROWS[f])
                    if f in NEXT_RES:
                        make_r(b + 1, 1 - par, NEXT_RES[f])

            def end():
                tanh(LAST, NF - 1)
                a_his(LAST, NF - 1)

            run(act, start, body, end)

        @block.vector
        def _(dve):
            def token_stats(b, par, tiles):
                if exists(b):
                    if tiles[0] == 0:
                        dve.wait_ge(x2_in[par], by_parity(b, par) * 8 + 16)
                        wait(dve, ln_done, b * 3)
                    for t in tiles:
                        nc.vector.bn_stats(stats[:, t, :], x2[:, par, t, :]).then_inc(own, 1)

            def layernorms(b):
                if exists(b):
                    dve.wait_ge(own, b * 8 + 4)
                    nc.vector.tensor_copy(carrier[:, 1:2], carrier[:, 0:1])
                    for t in range(TT):
                        nc.vector.bn_aggr(mv[:, t, :], stats[:, t, :]).then_inc(own, 1)
                    mean, var = mv[:, :, 0], mv[:, :, 1]
                    dve.wait_ge(own, b * 8 + 8)
                    nc.vector.tensor_scalar(var_eps[:, 0, :], var, EPS, None, ALU.add).then_inc(var_done, 1)
                    nc.vector.tensor_scalar(var_eps[:, 1, :], var, 1.0 + EPS, EPS * EPS,
                                            ALU.mult, ALU.add).then_inc(var_done, 1)
                    nc.vector.tensor_scalar(neg_mean[:, :], mean, -1.0, None, ALU.mult).then_inc(var_done, 1)

            def dequantise(f):
                cols = slice(f * P, (f + 1) * P)
                dve.wait_ge(w_in[f % LOADS], 48 * (f // LOADS + 1))
                nc.vector.tensor_scalar(w1_f[:, :, cols], w1_codes[:, :, cols], -ZERO_POINT, None,
                                        ALU.add).then_inc(c_f, 1)
                nc.vector.scalar_tensor_tensor(out=w2_f[:, LO, f, :], in0=w2_codes[:, LO, f, :], scalar=-ZERO_POINT,
                                               in1=w2_f[:, HI, f, :], op0=ALU.add, op1=ALU.mult).then_inc(w_f, 1)

            def split_w(f):
                dve.wait_ge(w2_hi, f + 1)
                nc.vector.scalar_tensor_tensor(out=w2[:, LO, f, :], in0=w2_f[:, LO, f, :], scalar=0.25,
                                               in1=w2[:, HI, f, :].bitcast(F32),
                                               op0=ALU.mult, op1=ALU.subtract).then_inc(w2_lo, 1)

            def peak_of_lo(f):
                dve.wait_ge(c_lo, f + 1)
                nc.vector.tensor_reduce(lo_peak[:, f * KT:(f + 1) * KT],
                                        w1_lo[:, :, f * P:(f + 1) * P].bitcast(F32), AX.X, ALU.max,
                                        apply_absolute_value=True).then_inc(peaked, 1)

            def gather_peaks():
                dve.wait_ge(peaked, NF)
                nc.vector.tensor_reduce(row_peak[:, :], lo_peak[:, :], AX.X, ALU.max).then_inc(all_peaked, 1)

            def know_lo():
                dve.wait_ge(any_peaked, 1)
                nc.vector.tensor_scalar(lo_used[:, :], any_peak[:, :], 0.0, None, ALU.not_equal).then_inc(lo_known, 1)

            def add_group(b, f, k):
                n = b * NF + f
                dve.wait_ge(g_full, n * KT + (k + 1))
                if k == 1:
                    dve.wait_ge(y_begun, n + 1)
                else:
                    dve.wait_ge(added, n * ADDS + (k - 1))
                nc.vector.scalar_tensor_tensor(out=y[:, f % 2, :], in0=g_bank[k][:, :], scalar=s1_col[:, k, f:f + 1],
                                               in1=y[:, f % 2, :], op0=ALU.mult, op1=ALU.add).then_inc(added, 1)

            def activate(b, f):
                if exists(b):
                    dve.wait_ge(th_done, b * NF + (f + 1))
                    nc.vector.scalar_tensor_tensor(out=y[:, f % 2, :], in0=th[:, f % 2, :], scalar=1.0,
                                                   in1=y[:, f % 2, :], op0=ALU.add, op1=ALU.mult).then_inc(a_done, 1)

            def outputs(b, par, tiles):
                if exists(b):
                    for t in tiles:
                        if t < TT - 1:
                            dve.wait_ge(acc_full, b * (TT - 1) + (t + 1))
                        else:
                            dve.wait_ge(f2_done, b * NF + NF)
                        dve.wait_ge(res_done, b * TT + (t + 1))
                        nc.vector.tensor_tensor(x2[:, par, t, :], acc[:, t, :], x2[:, par, t, :],
                                                ALU.add).then_inc(out_ready, 1)

            def start():
                nc.vector.memset(carrier[:, 0:1], 0.0)
                dve.wait_ge(const_in, 96)
                token_stats(0, 0, range(TT))
                layernorms(0)
                nc.vector.tensor_scalar(b2_half[:, :], b2_half[:, :], 0.5, None, ALU.mult).then_inc(b2_done, 1)
                for f in range(AHEAD + 1):
                    dequantise(f)
                for f in range(AHEAD):
                    split_w(f)
                    peak_of_lo(f)

            def body(b, par):
                for f in range(NF):
                    if f == 2:
                        outputs(b - 1, 1 - par, (2,))
                    add_group(b, f, 1)
                    if f == 2:
                        outputs(b - 1, 1 - par, (3,))
                    activate(*back(b, f, 1))
                    add_group(b, f, 2)
                    if f == 1:
                        outputs(b - 1, 1 - par, (0, 1))
                    add_group(b, f, 3)
                    if first(b) and f + AHEAD < NF:
                        split_w(f + AHEAD)
                        peak_of_lo(f + AHEAD)
                        if f + AHEAD + 1 < NF:
                            dequantise(f + AHEAD + 1)
                    if first(b) and f == NF - AHEAD:
                        gather_peaks()
                    if first(b) and f == NF - 1:
                        know_lo()
                    if f in NEXT_STATS:
                        token_stats(b + 1, 1 - par, (NEXT_STATS[f],))
                    if f == max(NEXT_STATS):
                        layernorms(b + 1)

            def end():
                activate(LAST, NF - 1)
                outputs(LAST, 1, range(TT))

            run(dve, start, body, end)

        @block.tensor
        def _(pe):
            def transpose_h(b, k):
                if exists(b):
                    if k == 0:
                        pe.wait_ge(h_done, b * TT + TT)
                    for t in range(TT):
                        mm = nc.tensor.transpose(g_bank[k][:, t * P:(t + 1) * P], h[:, t, k * P:(k + 1) * P],
                                                 ident[:, :])
                    mm.then_inc(h_full, 1)

            def group_used(b, f, k):
                if k == 0:
                    wait(pe, y_begun, b * NF + (f + 1))
                else:
                    wait(pe, added, (b * NF + f) * ADDS + k)

            def fc1(b, par, f, lo):
                if f == 0:
                    pe.wait_ge(h_lo, b * KT + KT)
                if first(b):
                    pe.wait_ge(c_lo, f + 1)
                cols = slice(f * P, (f + 1) * P)
                for k in range(KT):
                    group_used(*back(b, f, 1), k)
                    if f and NEXT_H.get(f - 1) == k and exists(b + 1):
                        pe.wait_ge(h_scaled, (b + 1) * KT + (k + 1))
                    nc.tensor.matmul(g_bank[k][:, :], w1_hi[:, k, cols], hT[par][:, HI, k, :], start=True, stop=False)
                    if lo:
                        nc.tensor.matmul(g_bank[k][:, :], w1_lo[:, k, cols], hT[par][:, HI, k, :],
                                         start=False, stop=False)
                    nc.tensor.matmul(g_bank[k][:, :], w1_hi[:, k, cols], hT[par][:, LO, k, :],
                                     start=False, stop=True).then_inc(g_full, 1)

            def fc2(b, f):
                if not exists(b):
                    return
                n = b * NF + f
                pe.wait_ge(a_lo, n + 1)
                if first(b):
                    pe.wait_ge(w2_lo, f + 1)
                for t in range(TT):
                    if f == 0 and exists(b - 1):
                        pe.wait_ge(out_ready, b * TT + (t - 3))
                    for i, (s, m) in enumerate(PASSES):
                        mm = nc.tensor.matmul(acc[:, t, :], a[:, f % 2, s, t * P:(t + 1) * P], w2[:, m, f, :],
                                              start=(f == 0 and i == 0), stop=(f == NF - 1 and i == 2))
                    if f == NF - 1 and t < TT - 1:
                        mm.then_inc(acc_full, 1)
                mm.then_inc(f2_done, 1)

            def next_h(b, f):
                if exists(b + 1):
                    group_used(b, f, NEXT_H[f])
                    transpose_h(b + 1, NEXT_H[f])

            def start():
                pe.wait_ge(const_in, 96)
                for k in range(KT):
                    transpose_h(0, k)

            def body(b, par, lo):
                for f in range(NF):
                    fc1(b, par, f, lo)
                    if f in NEXT_H and NEXT_H[f] in H_EARLY:
                        next_h(b, f)
                    fc2(*back(b, f, 2))
                    if f in NEXT_H and NEXT_H[f] not in H_EARLY:
                        next_h(b, f)

            def others(lo):
                body(1, 1, lo)
                with pe.Fori(1, BATCH // 2 - 1) as pair:
                    body(pair * 2, 0, lo)
                    body(pair * 2 + 1, 1, lo)
                body(BATCH - 2, 0, lo)
                body(LAST, 1, lo)
                fc2(LAST, NF - 2)
                fc2(LAST, NF - 1)

            start()
            body(0, 0, True)
            pe.wait_ge(lo_known, 1)
            used = pe.value_load(lo_used[0:1, 0:1], min_val=0, max_val=1)
            with pe.If(used != 0):
                others(True)
            with pe.Else():
                others(False)


def xattn_ffn(nc, x, ctxT, mask, wqT, b_q, wkT, b_k, wvT, b_v, woT, b_o, ident, gamma, beta, q1, s1, b1, q2, s2, b2,
              out):
    k_dram = nc.dram_tensor("k_kept_dram", (BATCH, P, 2, KT, KEYS), F32R, kind="Internal").ap()
    v_dram = nc.dram_tensor("v_kept_dram", (CTX, 2 * DM), F32R, kind="Internal").ap()
    x2_dram = nc.dram_tensor("x2_kept_dram", (BATCH, SEQ, DM), F32, kind="Internal").ap()
    with ExitStack() as ctx:
        w_q = ctx.enter_context(nc.sbuf_tensor("w_q", [P, 2, KT, DM], F32R))
        w_o = ctx.enter_context(nc.sbuf_tensor("w_o", [P, 2, KT, DM], F32R))
        k_diag = ctx.enter_context(nc.sbuf_tensor("k_diag", [P, 2, 2 * KT, GK], F32R))
        v_diag = ctx.enter_context(nc.sbuf_tensor("v_diag", [P, 2, 3, 2 * KT, P], F32R))
        head = attention_head(nc, ctx, x, ident, b_q, b_o)
        keys_and_values(nc, head, ctxT, (wkT, wvT, wqT, woT), b_k, b_v, k_dram, v_dram, w_q, w_o, k_diag, v_diag)
        attention(nc, head, x, mask, k_dram, v_dram, x2_dram, w_q, w_o, k_diag, v_diag)
    feed_forward(nc, x2_dram, out, ident, gamma, beta, q1, s1, b1, q2, s2, b2)


def kernel(x, ctx_1024, mask_Bx1xSxS2_ik0, L0_xattn_w_q, L0_xattn_b_q, L0_xattn_w_k, L0_xattn_b_k, L0_xattn_w_v,
           L0_xattn_b_v, L0_xattn_w_out, L0_xattn_b_out, L0_ffn_ln_gamma, L0_ffn_ln_beta, L0_ffn_fc1_q,
           L0_ffn_fc1_scales, L0_ffn_fc1_bias, L0_ffn_fc2_q, L0_ffn_fc2_scales, L0_ffn_fc2_bias):
    import numpy as np
    import concourse.bacc as bacc
    from concourse.bass_utils import run_bass_kernel_spmd

    def column(v):
        return np.asarray(v).reshape(-1, P).T

    arrays = {
        "x": x,
        "ctxT": np.asarray(ctx_1024).reshape(CTX, DM).T,
        "mask": np.asarray(mask_Bx1xSxS2_ik0).reshape(BATCH, SEQ, KEYS),
        "wqT": np.asarray(L0_xattn_w_q).T,
        "b_q": column(L0_xattn_b_q),
        "wkT": np.asarray(L0_xattn_w_k).T,
        "b_k": column(L0_xattn_b_k),
        "wvT": np.asarray(L0_xattn_w_v).T,
        "b_v": L0_xattn_b_v,
        "woT": np.asarray(L0_xattn_w_out).T,
        "b_o": L0_xattn_b_out,
        "identity": np.eye(P, dtype=np.float32),
        "gamma": column(L0_ffn_ln_gamma),
        "beta": column(L0_ffn_ln_beta),
        "fc1_q": L0_ffn_fc1_q,
        "fc1_scales": np.asarray(L0_ffn_fc1_scales).reshape(KT, NF, P).transpose(2, 0, 1),
        "fc1_bias": column(L0_ffn_fc1_bias),
        "fc2_q": L0_ffn_fc2_q,
        "fc2_scales": L0_ffn_fc2_scales,
        "fc2_bias": L0_ffn_fc2_bias,
    }
    nc = bacc.Bacc("TRN2", target_bir_lowering=False, num_devices=1)
    given, args = {}, []
    for name, a in arrays.items():
        a = np.ascontiguousarray(a)
        given[f"in_{name}"] = a
        args.append(nc.dram_tensor(f"in_{name}", a.shape, mybir.dt.from_np(a.dtype), kind="ExternalInput").ap())
    out = nc.dram_tensor("out_x", (BATCH, SEQ, DM), F32, kind="ExternalOutput").ap()
    xattn_ffn(nc, *args, out)
    return run_bass_kernel_spmd(nc, [given], core_ids=[0]).results[0]["out_x"]
```

```python
from contextlib import ExitStack

import concourse.bass as bass
from concourse import mybir

F32 = mybir.dt.float32
F32R = mybir.dt.float32r
I32 = mybir.dt.int32
ALU = mybir.AluOpType
ACT = mybir.ActivationFunctionType
AX = mybir.AxisListType
RMAX = bass.bass_isa.ReduceOp.max

P = 128
HI, LO = 0, 1
C_LO, C_HI, W2 = 0, 1, 2
PASSES = ((HI, HI), (HI, LO), (LO, HI))

BATCH, SEQ, DM = 16, 512, 512
KEYS = 77
HEADS, DK = 16, 32
FF = 2048
EPS = 1e-5
ZERO_POINT = 128.0
SCALE = float(DK) ** -0.5
MASKED = -1.0e30

TT = SEQ // P
KT = DM // P
HG = P // DK
GK = HG * KEYS
NF = FF // P
CUTS = (0, 103, 206, GK)
CTX = BATCH * KEYS
CHUNK_B = 4
CHUNK = CHUNK_B * KEYS
LAST = BATCH - 1


AHEAD = 2
UNDER = AHEAD
LOADS = 4


class AttentionHead:

    def __init__(self, buffers, semaphores, steps, under_stage_1):
        self.ident, self.bq, self.bo, self.x_sb = buffers
        self.const_in, self.bq_done, self.xn_done = semaphores
        self.load_x, self.token_stats, self.layernorm, self.finish_ln, self.make_xn = steps
        self.on_sync, self.on_vector, self.on_gpsimd, self.on_scalar = under_stage_1


def value_pieces():
    out = []
    for t in range(3):
        for j in range(HG):
            a, b = max(CUTS[t], j * KEYS), min(CUTS[t + 1], (j + 1) * KEYS)
            if a < b:
                out.append((t, a - CUTS[t], a - j * KEYS, b - a, j))
    return out


def wait(eng, sem, value):
    if isinstance(value, int) and value <= 0:
        return
    eng.wait_ge(sem, value)


def by_parity(b, par):
    return b - par if par else b


def one(ap, b):
    return ap[b:b + 1] if isinstance(b, int) else ap[bass.ds(b, 1)]


def attention_head(nc, outer, x_sb, x, ident_dram, b_q, b_o):
    def sb(name, shape, dt=F32):
        return outer.enter_context(nc.sbuf_tensor(name, shape, dt))

    def sem(name):
        return outer.enter_context(nc.semaphore(name))

    ident = sb("ident", [P, P])
    bq_in = sb("bq_in", [P, KT])
    bq = sb("bq_col", [P, KT])
    bo = sb("bo_row", [P, DM])
    stats = sb("stats", [P, TT, 6])
    mv = sb("mv", [P, TT, 2])
    var_eps = sb("var_eps", [P, TT])
    neg_mean = sb("neg_mean", [P, TT])
    rstd = sb("rstd", [P, TT])
    shift = sb("shift", [P, TT])
    minus_half = sb("minus_half", [P, TT])
    carrier = sb("carrier", [P, 2])
    const_in, bq_done = sem("const_in"), sem("bq_done")
    x_in = sem("x_in")
    half_set, ln_own, var_done, rstd_done, ln_done, xn_done = (
        sem(n) for n in ("half_set", "ln_own", "var_done", "rstd_done", "ln_done", "xn_done"))

    def exists(b):
        return not isinstance(b, int) or 0 <= b < BATCH

    def load_x(sp, b):
        sp.dma_start(x_sb[:, :, :], one(x, b).rearrange("o (t p) n -> (o p) t n", p=P)).then_inc(x_in, 16)

    def token_stats(dve, b, tiles):
        if exists(b):
            if tiles[0] == 0:
                dve.wait_ge(x_in, b * 16 + 16)
                wait(dve, ln_done, b)
            for t in tiles:
                nc.vector.bn_stats(stats[:, t, :], x_sb[:, t, :]).then_inc(ln_own, 1)

    def layernorm(dve, b):
        if exists(b):
            dve.wait_ge(ln_own, b * 8 + 4)
            nc.vector.tensor_copy(carrier[:, 1:2], carrier[:, 0:1])
            for t in range(TT):
                nc.vector.bn_aggr(mv[:, t, :], stats[:, t, :]).then_inc(ln_own, 1)
            dve.wait_ge(ln_own, b * 8 + 8)
            nc.vector.tensor_scalar(var_eps[:, :], mv[:, :, 1], EPS, None, ALU.add).then_inc(var_done, 1)
            nc.vector.tensor_scalar(neg_mean[:, :], mv[:, :, 0], -1.0, None, ALU.mult).then_inc(var_done, 1)

    def finish_ln(pool, b):
        if exists(b):
            pool.wait_ge(var_done, b * 2 + 2)
            wait(pool, xn_done, b * TT)
            nc.gpsimd.tensor_tensor(rstd[:, :], var_eps[:, :], minus_half[:, :], ALU.pow).then_inc(rstd_done, 1)
            pool.wait_ge(rstd_done, b + 1)
            nc.gpsimd.tensor_tensor(shift[:, :], neg_mean[:, :], rstd[:, :], ALU.mult).then_inc(ln_done, 1)

    def make_xn(act, b, tiles):
        if exists(b):
            act.wait_ge(ln_done, b + 1)
            for t in tiles:
                nc.scalar.activation(x_sb[:, t, :], x_sb[:, t, :], ACT.Identity,
                                     scale=rstd[:, t:t + 1], bias=shift[:, t:t + 1]).then_inc(xn_done, 1)

    def on_sync(sp):
        load_x(sp, 0)
        sp.dma_start(ident[:, :], ident_dram).then_inc(const_in, 16)
        sp.dma_start(bq_in[:, :], b_q).then_inc(const_in, 16)
        sp.dma_start(bo[:, :], b_o.partition_broadcast(P)).then_inc(const_in, 16)

    def on_vector(dve):
        nc.vector.memset(carrier[:, 0:1], 0.0)
        token_stats(dve, 0, range(TT))
        layernorm(dve, 0)
        dve.wait_ge(const_in, 48)
        nc.vector.tensor_scalar(bq[:, :], bq_in[:, :], SCALE, None, ALU.mult).then_inc(bq_done, 1)

    def on_gpsimd(pool):
        nc.gpsimd.memset(minus_half[:, :], -0.5).then_inc(half_set, 1)
        pool.wait_ge(half_set, 1)
        finish_ln(pool, 0)

    def on_scalar(act):
        make_xn(act, 0, range(TT))

    return AttentionHead((ident, bq, bo, x_sb), (const_in, bq_done, xn_done),
                         (load_x, token_stats, layernorm, finish_ln, make_xn),
                         (on_sync, on_vector, on_gpsimd, on_scalar))


def keys_and_values(nc, head, ctxT, wT, b_k, b_v, k_dram, v_dram, w_q, w_o, k_diag, v_diag):
    ROWS = [(r, min(P, CTX - r)) for r in range(0, CTX, P)]
    NR = len(ROWS)
    NC = BATCH // CHUNK_B
    NB = 8
    HALVES = (slice(0, KT // 2), slice(KT // 2, KT))
    NKO = 3
    NVO = 4
    with ExitStack() as ctx:
        def sb(name, shape, dt=F32):
            return ctx.enter_context(nc.sbuf_tensor(name, shape, dt))

        def sem(name):
            return ctx.enter_context(nc.semaphore(name))

        raw = [sb(f"w_raw{i}", [P, KT, DM]) for i in range(2)]
        ctx_raw = [sb(f"ctx_raw{i}", [P, KT, CHUNK]) for i in range(2)]
        w_k = sb("w_k", [P, 2, KT, DM], F32R)
        w_v = sb("w_v", [P, 2, KT, DM], F32R)
        ctx_s = sb("ctx_split", [P, 2, KT, CTX], F32R)
        bk = sb("bk_col", [P, KT])
        bv = sb("bv_row", [P, DM])
        k_out = [sb(f"k_out{i}", [P, 2, CHUNK], F32R) for i in range(NKO)]
        v32 = [raw[i][:, 0, :] for i in range(2)]
        v_out = [sb(f"v_out{i}", [P, 2, DM], F32R) for i in range(NVO)]
        bank = [ctx.enter_context(nc.psum_tensor(f"kv_bank{i}", [P, 512], F32)) for i in range(NB)]

        split_to = [w_k, w_v, w_q, w_o]
        factor = [1.0, 1.0, SCALE, 1.0]
        w_in = [[sem(f"w_in{i}{half}") for half in "ab"] for i in range(4)]
        c_in = [sem(f"ctx_in{i}") for i in range(NC)]
        bias_in = sem("kv_bias_in")
        w_hi, w_lo = sem("kv_w_hi"), sem("kv_w_lo")
        c_hi, c_lo = sem("ctx_hi"), sem("ctx_lo")
        full = sem("kv_full")
        k_hi, k_lo = sem("k_hi"), sem("k_lo")
        v_sum, v_hi, v_lo = sem("v_sum"), sem("v_hi"), sem("v_lo")
        k_kept = [sem(f"k_kept{i}") for i in range(NKO)]
        v_kept = [sem(f"v_kept{i}") for i in range(NVO)]
        block = ctx.enter_context(nc.Block())
        NK = NC * KT

        @block.sync
        def _(sp):
            def load_w(i):
                for half, ks in enumerate(HALVES):
                    sp.dma_start(raw[i % 2][:, ks, :], wT[i].rearrange("(k p) n -> p k n", p=P)[:, ks, :]
                                 ).then_inc(w_in[i][half], 16)

            def load_ctx(c):
                sp.dma_start(ctx_raw[c % 2][:, :, :],
                             ctxT.rearrange("(k p) n -> p k n", p=P)[:, :, c * CHUNK:(c + 1) * CHUNK]
                             ).then_inc(c_in[c], 16)

            load_ctx(0)
            load_w(0)
            sp.dma_start(bk[:, :], b_k).then_inc(bias_in, 16)
            sp.dma_start(bv[:, :], b_v.partition_broadcast(P)).then_inc(bias_in, 16)
            load_ctx(1)
            load_w(1)
            for c in range(2, NC):
                sp.wait_ge(c_lo, c - 1)
                load_ctx(c)
            for i in range(2, 4):
                sp.wait_ge(w_lo, 2 * (i - 1))
                load_w(i)
            head.on_sync(sp)
            for n in range(NK):
                c, g = n // KT, n % KT
                sp.wait_ge(k_lo, n + 1)
                for part in (HI, LO):
                    sp.dma_start(
                        k_dram[c * CHUNK_B:(c + 1) * CHUNK_B, :, part, g, :].rearrange("b p k -> p b k").bitcast(F32),
                        k_out[n % NKO][:, part, :].rearrange("p (b k) -> p b k", k=KEYS).bitcast(F32),
                    ).then_inc(k_kept[n % NKO], 16)
            for r, (row, rows) in enumerate(ROWS):
                sp.wait_ge(v_lo, r + 1)
                sp.dma_start(v_dram[row:row + rows, :].bitcast(F32),
                             v_out[r % NVO][0:rows, :, :].rearrange("p t n -> p (t n)").bitcast(F32)
                             ).then_inc(v_kept[r % NVO], 16)
            for i in range(NKO):
                sp.wait_ge(k_kept[i], 32 * len(range(i, NK, NKO)))
            for i in range(NVO):
                sp.wait_ge(v_kept[i], 16 * len(range(i, NR, NVO)))

        @block.gpsimd
        def _(pool):
            nc.gpsimd.memset(k_diag[:, :, :, :].bitcast(F32), 0.0)
            nc.gpsimd.memset(v_diag[:, :, :, :, :].bitcast(F32), 0.0)
            head.on_gpsimd(pool)

        @block.scalar
        def _(act):
            def hi_w(i):
                for half, ks in enumerate(HALVES):
                    act.wait_ge(w_in[i][half], 16)
                    nc.scalar.activation(split_to[i][:, HI, ks, :], raw[i % 2][:, ks, :], ACT.Copy,
                                         scale=factor[i]).then_inc(w_hi, 1)

            def hi_ctx(c):
                act.wait_ge(c_in[c], 16)
                nc.scalar.activation(ctx_s[:, HI, :, c * CHUNK:(c + 1) * CHUNK], ctx_raw[c % 2][:, :, :],
                                     ACT.Copy).then_inc(c_hi, 1)

            hi_ctx(0)
            hi_w(0)
            hi_ctx(1)
            hi_w(1)
            for c in range(2, NC):
                hi_ctx(c)
            act.wait_ge(bias_in, 32)
            for n in range(NK):
                c, g = n // KT, n % KT
                act.wait_ge(full, n + 1)
                if n >= NKO:
                    act.wait_ge(k_kept[n % NKO], 32 * (n // NKO))
                nc.scalar.activation(k_out[n % NKO][:, HI, :], bank[n % NB][:, 0:CHUNK], ACT.Identity,
                                     bias=bk[:, g:g + 1]).then_inc(k_hi, 1)
                if n in (4, 8):
                    hi_w(1 + n // 4)
            head.on_scalar(act)
            for r, (row, rows) in enumerate(ROWS):
                act.wait_ge(v_sum, r + 1)
                if r >= NVO:
                    act.wait_ge(v_kept[r % NVO], 16 * (r // NVO))
                nc.scalar.activation(v_out[r % NVO][0:rows, HI, :], v32[r % 2][0:rows, :], ACT.Copy).then_inc(v_hi, 1)

        @block.vector
        def _(dve):
            def lo_w(i):
                for half, ks in enumerate(HALVES):
                    dve.wait_ge(w_hi, 2 * i + half + 1)
                    nc.vector.scalar_tensor_tensor(
                        out=split_to[i][:, LO, ks, :], in0=raw[i % 2][:, ks, :], scalar=factor[i],
                        in1=split_to[i][:, HI, ks, :].bitcast(F32), op0=ALU.mult, op1=ALU.subtract
                    ).then_inc(w_lo, 1)

            def lo_ctx(c):
                dve.wait_ge(c_hi, c + 1)
                cols = slice(c * CHUNK, (c + 1) * CHUNK)
                nc.vector.tensor_tensor(ctx_s[:, LO, :, cols], ctx_raw[c % 2][:, :, :],
                                        ctx_s[:, HI, :, cols].bitcast(F32), ALU.subtract).then_inc(c_lo, 1)

            lo_ctx(0)
            lo_w(0)
            lo_ctx(1)
            lo_w(1)
            for c in range(2, NC):
                lo_ctx(c)
            for n in range(NK):
                g = n % KT
                dve.wait_ge(k_hi, n + 1)
                nc.vector.scalar_tensor_tensor(
                    out=k_out[n % NKO][:, LO, :], in0=bank[n % NB][:, 0:CHUNK], scalar=bk[:, g:g + 1],
                    in1=k_out[n % NKO][:, HI, :].bitcast(F32), op0=ALU.add, op1=ALU.subtract).then_inc(k_lo, 1)
                if n in (4, 8):
                    lo_w(1 + n // 4)
                if n == NK - 2:
                    head.on_vector(dve)

            def lo_v(r):
                rows = ROWS[r][1]
                dve.wait_ge(v_hi, r + 1)
                nc.vector.tensor_tensor(v_out[r % NVO][0:rows, LO, :], v32[r % 2][0:rows, :],
                                        v_out[r % NVO][0:rows, HI, :].bitcast(F32), ALU.subtract).then_inc(v_lo, 1)

            for r, (row, rows) in enumerate(ROWS):
                dve.wait_ge(full, NK + r + 1)
                wait(dve, v_lo, r - 1)
                nc.vector.tensor_tensor(v32[r % 2][0:rows, :], bank[(NK + r) % NB][0:rows, :], bv[0:rows, :],
                                        ALU.add).then_inc(v_sum, 1)
                if r:
                    lo_v(r - 1)
            lo_v(NR - 1)

        @block.tensor
        def _(pe):
            for n in range(NK):
                c, g = n // KT, n % KT
                if n == 0:
                    pe.wait_ge(w_lo, 2)
                if g == 0:
                    pe.wait_ge(c_lo, c + 1)
                if n >= NB:
                    pe.wait_ge(k_lo, n - NB + 1)
                for i, (s, m) in enumerate(PASSES):
                    for k in range(KT):
                        mm = nc.tensor.matmul(bank[n % NB][:, 0:CHUNK], w_k[:, s, k, g * P:(g + 1) * P],
                                              ctx_s[:, m, k, c * CHUNK:(c + 1) * CHUNK],
                                              start=(i == 0 and k == 0), stop=(i == 2 and k == KT - 1))
                mm.then_inc(full, 1)
            pe.wait_ge(w_lo, 4)
            for r, (row, rows) in enumerate(ROWS):
                if r < NB:
                    pe.wait_ge(k_lo, NK - NB + 1 + r)
                else:
                    pe.wait_ge(v_sum, r - NB + 1)
                for i, (s, m) in enumerate(PASSES):
                    for k in range(KT):
                        mm = nc.tensor.matmul(bank[(NK + r) % NB][0:rows, :], ctx_s[:, s, k, row:row + rows],
                                              w_v[:, m, k, :],
                                              start=(i == 0 and k == 0), stop=(i == 2 and k == KT - 1))
                mm.then_inc(full, 1)


def attention_order():
    work = [(f"Q{g}", 0) for g in range(KT)]
    tile = [(f"A{k}", b) for b in range(2) for k in range(KT)]
    for b in range(BATCH):
        work += [("Q0", b + 1), ("O3", b - 2), ("V3", b - 1)]
        for g in range(1, KT):
            work += [(f"Q{g}", b + 1), (f"O{g - 1}", b - 1), (f"V{g - 1}", b)]
        tile += [(f"T{g}{t}", b) for g in range(KT) for t in range(3)] + [(f"A{k}", b + 2) for k in range(KT)]
    work += [("O3", LAST - 1), ("V3", LAST)] + [(f"O{t}", LAST) for t in range(TT)]
    orders = {}
    for ring in (work, tile):
        orders.update({x: n for n, x in enumerate(x for x in ring if 0 <= x[1] < BATCH)})
    return orders


ORDER = attention_order()
PER_SEQ = {"Q": 12, "V": 12, "O": 12, "A": 16, "T": 16}


def ordinal(what, b):
    if isinstance(b, int):
        return ORDER[(what, b)]
    middle = BATCH // 2
    return b * PER_SEQ[what[0]] + (ORDER[(what, middle)] - PER_SEQ[what[0]] * middle)


def bank_of(what, b):
    return ORDER[(what, b if isinstance(b, int) else BATCH // 2)] % 2


def attention(nc, head, ff_head, x, mask, k_dram, v_dram, x2_dram, w_q, w_o, k_diag, v_diag):
    with ExitStack() as ctx:
        def sb(name, shape, dt=F32):
            return ctx.enter_context(nc.sbuf_tensor(name, shape, dt))

        def sem(name):
            return ctx.enter_context(nc.semaphore(name))

        ident, bq, bo, x_sb = head.ident, head.bq, head.bo, head.x_sb
        bq_done, xn_done = head.bq_done, head.xn_done
        xT = sb("xT", [P, 2, KT, SEQ], F32R)
        qT = sb("qT", [P, 2, 2, SEQ], F32R)
        prob = sb("prob", [P, KT, TT, GK])
        neg_peak = sb("neg_peak", [P, KT, TT * HG])
        total = sb("total", [P, KT, TT * HG])
        inv = sb("inv", [P, KT, TT * HG])
        pT = sb("pT", [P, 2, 2, 3, SEQ], F32R)
        aT = sb("aT", [P, 2, 2, KT, SEQ], F32R)
        res = sb("res", [P, TT, DM])
        mask_sb = sb("mask_sb", [P, 2, TT, KEYS], I32)
        bias = sb("bias", [P, 2, TT, KEYS])
        score = ctx.enter_context(nc.psum_tensor("score", [P, TT, 512], F32))
        work = [ctx.enter_context(nc.psum_tensor(f"work{i}", [P, 512], F32)) for i in range(2)]
        tbank = [ctx.enter_context(nc.psum_tensor(f"tbank{i}", [P, 512], F32)) for i in range(2)]

        mask_in, k_in, v_in = ([sem(f"{n}{i}") for i in range(2)] for n in ("mask_in", "k_in", "v_in"))
        res_in = [sem(f"res_in{t}") for t in range(TT)]
        x2_out = [sem(f"x2_out{t}") for t in range(TT)]
        bias_done, res_ready = sem("bias_done"), sem("res_ready")
        work_full, work_free = sem("work_full"), sem("work_free")
        t_full, t_hi, t_lo = sem("t_full"), sem("t_hi"), sem("t_lo")
        x_hi, q_hi, a_hi = sem("x_hi"), sem("q_hi"), sem("a_hi")
        score_full, masked, peaked = (sem(n) for n in ("score_full", "masked", "peaked"))
        exp_done, totalled, inverted, normed = (sem(n) for n in ("exp_done", "totalled", "inverted", "normed"))
        block = ctx.enter_context(nc.Block())

        def run(eng, start, body, end):
            start()
            body(0, 0)
            body(1, 1)
            with eng.Fori(1, BATCH // 2 - 1) as pair:
                body(pair * 2, 0)
                body(pair * 2 + 1, 1)
            body(BATCH - 2, 0)
            body(LAST, 1)
            end()

        def exists(b):
            return not isinstance(b, int) or 0 <= b < BATCH

        @block.sync
        def _(sp):
            def load_x(b):
                if exists(b):
                    sp.wait_ge(t_full, ordinal("A3", b - 1) + 1)
                    head.load_x(sp, b)

            def load_mask(b, par):
                if exists(b):
                    wait(sp, bias_done, b - 1)
                    sp.dma_start(mask_sb[:, par, :, :],
                                 one(mask, b).rearrange("o (t p) k -> (o p) t k", p=P)).then_inc(mask_in[par], 16)

            def load_k(b, par):
                if exists(b):
                    wait(sp, score_full, b * KT - KT)
                    for j in range(HG):
                        rows = slice(j * DK, (j + 1) * DK)
                        sp.dma_start(
                            k_diag[rows, par, :, j * KEYS:(j + 1) * KEYS].bitcast(F32),
                            one(k_dram, b)[:, rows, :, :, :].rearrange("o p t g k -> (o p) (t g) k").bitcast(F32),
                        ).then_inc(k_in[par], 16)

            def load_v(b, par):
                if exists(b):
                    if not (isinstance(b, int) and b < 2):
                        sp.wait_ge(work_full, ordinal("V3", b - 2) + 1)
                    seqs = v_dram.rearrange("(b k) (m d) -> b k m d", k=KEYS, d=P)
                    for t, row, key, n, j in value_pieces():
                        sp.dma_start(
                            v_diag[row:row + n, par, t, :, j * DK:(j + 1) * DK].bitcast(F32),
                            one(seqs, b)[:, key:key + n, :, j * DK:(j + 1) * DK]
                            .rearrange("o k m d -> (o k) m d").bitcast(F32),
                        ).then_inc(v_in[par], 16)

            def load_res(b, t):
                if exists(b):
                    wait(sp, x2_out[t], b * 16)
                    sp.dma_start(res[:, t, :], one(x, b)[:, t * P:(t + 1) * P, :].rearrange("o p n -> (o p) n")
                                 ).then_inc(res_in[t], 16)

            def store_x2(b, t):
                if exists(b):
                    sp.wait_ge(work_free, ordinal(f"O{t}", b) + 1)
                    sp.dma_start(one(x2_dram, b)[:, t * P:(t + 1) * P, :].rearrange("o p n -> (o p) n"),
                                 res[:, t, :]).then_inc(x2_out[t], 16)

            def start():
                load_k(0, 0)
                load_mask(0, 0)
                load_x(1)
                load_k(1, 1)
                load_mask(1, 1)
                load_v(0, 0)

            def body(b, par):
                load_res(b - 1, 0)
                load_x(b + 2)
                load_res(b - 1, 1)
                load_res(b - 1, 2)
                load_k(b + 2, par)
                store_x2(b - 2, 3)
                load_v(b + 1, 1 - par)
                load_res(b - 1, 3)
                load_mask(b + 2, par)
                if isinstance(b, int) and b == LAST:
                    sp.wait_ge(score_full, BATCH * KT)
                    ff_head.on_sync(sp)
                for t in range(3):
                    store_x2(b - 1, t)

            def end():
                store_x2(LAST - 1, 3)
                for t in range(TT):
                    load_res(LAST, t)
                for t in range(TT):
                    store_x2(LAST, t)
                for t in range(TT):
                    sp.wait_ge(x2_out[t], 16 * BATCH)

            run(sp, start, body, end)

        @block.gpsimd
        def _(pool):
            def add_bo(b, t):
                if exists(b):
                    pool.wait_ge(res_in[t], b * 16 + 16)
                    nc.gpsimd.tensor_tensor(res[:, t, :], res[:, t, :], bo[:, :], ALU.add).then_inc(res_ready, 1)

            def norm(b, g):
                if exists(b):
                    pool.wait_ge(inverted, b * KT + (g + 1))
                    p = prob[:, g, :, :].rearrange("p t (h k) -> p (t h) k", k=KEYS)
                    nc.gpsimd.tensor_tensor(p, p, inv[:, g, :].unsqueeze(2).to_broadcast([P, TT * HG, KEYS]),
                                            ALU.mult).then_inc(normed, 1)

            def start():
                head.finish_ln(pool, 1)
                norm(0, 0)

            def body(b, par):
                norm(b, 1)
                add_bo(b - 1, 0)
                norm(b, 2)
                add_bo(b - 1, 1)
                norm(b, 3)
                head.finish_ln(pool, b + 2)
                add_bo(b - 1, 2)
                norm(b + 1, 0)
                add_bo(b - 1, 3)

            def end():
                ff_head.on_gpsimd(pool)
                for t in range(TT):
                    add_bo(LAST, t)
                for f in range(UNDER):
                    ff_head.code_lo(pool, f)

            run(pool, start, body, end)

        @block.scalar
        def _(act):
            def x_his(b, k):
                if exists(b):
                    act.wait_ge(t_full, ordinal(f"A{k}", b) + 1)
                    if k == 0 and exists(b - 1):
                        act.wait_ge(work_full, ordinal("Q3", b - 1) + 1)
                    nc.scalar.activation(xT[:, HI, k, :], tbank[bank_of(f"A{k}", b)][:, :],
                                         ACT.Copy).then_inc(x_hi, 1)

            def q_his(b, g):
                if exists(b):
                    act.wait_ge(work_full, ordinal(f"Q{g}", b) + 1)
                    wait(act, score_full, b * KT + (g - 1))
                    nc.scalar.activation(qT[:, g % 2, HI, :], work[bank_of(f"Q{g}", b)][:, :], ACT.Identity,
                                         bias=bq[:, g:g + 1]).then_inc(q_hi, 1)

            def t_his(b, g, t):
                n = CUTS[t + 1] - CUTS[t]
                act.wait_ge(t_full, ordinal(f"T{g}{t}", b) + 1)
                if t == 0:
                    if g >= 2:
                        act.wait_ge(work_full, ordinal(f"V{g - 2}", b) + 1)
                    elif exists(b - 1):
                        act.wait_ge(work_full, ordinal(f"V{g + 2}", b - 1) + 1)
                nc.scalar.activation(pT[0:n, g % 2, HI, t, :], tbank[bank_of(f"T{g}{t}", b)][0:n, :],
                                     ACT.Copy).then_inc(t_hi, 1)

            def exps(b, g, t):
                if exists(b):
                    if t == 0:
                        act.wait_ge(peaked, b * KT + (g + 1))
                    for j in range(HG):
                        tile = prob[:, g, t, j * KEYS:(j + 1) * KEYS]
                        ins = nc.scalar.activation(tile, tile, ACT.Exp, scale=1.0,
                                                   bias=neg_peak[:, g, t * HG + j:t * HG + j + 1])
                    if t == TT - 1:
                        ins.then_inc(exp_done, 1)

            def a_his(b, par, g):
                if exists(b):
                    act.wait_ge(work_full, ordinal(f"V{g}", b) + 1)
                    if g == 0 and exists(b - 2):
                        act.wait_ge(work_full, ordinal("O3", b - 2) + 1)
                    nc.scalar.activation(aT[:, par, HI, g, :], work[bank_of(f"V{g}", b)][:, :],
                                         ACT.Copy).then_inc(a_hi, 1)

            def start():
                for k in range(KT):
                    x_his(0, k)
                act.wait_ge(bq_done, 1)
                for g in range(3):
                    q_his(0, g)
                for t in range(TT):
                    exps(0, 0, t)
                q_his(0, 3)
                head.make_xn(act, 1, range(TT))
                for k in range(KT):
                    x_his(1, k)
                for t in range(TT):
                    exps(0, 1, t)

            def body(b, par):
                for g in range(KT):
                    eb, eg = (b, g + 2) if g < 2 else (b + 1, g - 2)
                    t_his(b, g, 0)
                    t_his(b, g, 1)
                    exps(eb, eg, 0)
                    exps(eb, eg, 1)
                    t_his(b, g, 2)
                    exps(eb, eg, 2)
                    q_his(b + 1, g)
                    if g == 2:
                        head.make_xn(act, b + 2, (0, 1))
                    exps(eb, eg, 3)
                    if g == 2:
                        head.make_xn(act, b + 2, (2, 3))
                    if g == 3:
                        for k in range(KT):
                            x_his(b + 2, k)
                    if g == 0:
                        a_his(b - 1, 1 - par, 3)
                    else:
                        a_his(b, par, g - 1)

            def end():
                a_his(LAST, 1, 3)
                ff_head.on_scalar(act)

            run(act, start, body, end)

        @block.vector
        def _(dve):
            def make_bias(b, par):
                if exists(b):
                    dve.wait_ge(mask_in[par], by_parity(b, par) * 8 + 16)
                    nc.vector.tensor_scalar(bias[:, par, :, :], mask_sb[:, par, :, :], 0.0, MASKED,
                                            ALU.is_equal, ALU.mult).then_inc(bias_done, 1)

            def x_los(b, k):
                if exists(b):
                    dve.wait_ge(x_hi, b * KT + (k + 1))
                    nc.vector.tensor_tensor(xT[:, LO, k, :], tbank[bank_of(f"A{k}", b)][:, :],
                                            xT[:, HI, k, :].bitcast(F32), ALU.subtract).then_inc(t_lo, 1)

            def q_los(b, g):
                if exists(b):
                    dve.wait_ge(q_hi, b * KT + (g + 1))
                    nc.vector.scalar_tensor_tensor(
                        out=qT[:, g % 2, LO, :], in0=work[bank_of(f"Q{g}", b)][:, :], scalar=bq[:, g:g + 1],
                        in1=qT[:, g % 2, HI, :].bitcast(F32), op0=ALU.add, op1=ALU.subtract).then_inc(work_free, 1)

            def t_los(b, g, t):
                n = CUTS[t + 1] - CUTS[t]
                dve.wait_ge(t_hi, (b * KT + g) * 3 + (t + 1))
                nc.vector.tensor_tensor(pT[0:n, g % 2, LO, t, :], tbank[bank_of(f"T{g}{t}", b)][0:n, :],
                                        pT[0:n, g % 2, HI, t, :].bitcast(F32), ALU.subtract).then_inc(t_lo, 1)

            def a_los(b, par, g):
                if exists(b):
                    dve.wait_ge(a_hi, b * KT + (g + 1))
                    nc.vector.tensor_tensor(aT[:, par, LO, g, :], work[bank_of(f"V{g}", b)][:, :],
                                            aT[:, par, HI, g, :].bitcast(F32), ALU.subtract).then_inc(work_free, 1)

            def mask_scores(b, par, g):
                if exists(b):
                    dve.wait_ge(score_full, b * KT + (g + 1))
                    if g == 0:
                        dve.wait_ge(bias_done, b + 1)
                    if exists(b - 1):
                        dve.wait_ge(t_full, ordinal(f"T{g}2", b - 1) + 1)
                    nc.vector.tensor_tensor(
                        prob[:, g, :, :].rearrange("p t (h k) -> p t h k", k=KEYS),
                        score[:, :, 0:GK].rearrange("p t (h k) -> p t h k", k=KEYS),
                        bias[:, par, :, :].unsqueeze(2).to_broadcast([P, TT, HG, KEYS]),
                        ALU.add).then_inc(masked, 1)

            def by_head(g):
                return prob[:, g, :, :].rearrange("p t (h k) -> p (t h) k", k=KEYS)

            def peaks(b, g):
                if exists(b):
                    dve.wait_ge(masked, b * KT + (g + 1))
                    nc.vector.tensor_reduce(neg_peak[:, g, :], by_head(g), AX.X, ALU.max,
                                            negate=True).then_inc(peaked, 1)

            def totals(b, g):
                if exists(b):
                    dve.wait_ge(exp_done, b * KT + (g + 1))
                    nc.vector.tensor_reduce(total[:, g, :], by_head(g), AX.X, ALU.add).then_inc(totalled, 1)
                    dve.wait_ge(totalled, b * KT + (g + 1))
                    nc.vector.reciprocal(inv[:, g, :], total[:, g, :]).then_inc(inverted, 1)

            def project(b, t):
                if exists(b):
                    dve.wait_ge(work_full, ordinal(f"O{t}", b) + 1)
                    dve.wait_ge(res_ready, b * TT + (t + 1))
                    nc.vector.tensor_tensor(res[:, t, :], work[bank_of(f"O{t}", b)][:, :], res[:, t, :],
                                            ALU.add).then_inc(work_free, 1)

            def start():
                for k in range(KT):
                    x_los(0, k)
                dve.wait_ge(bq_done, 1)
                q_los(0, 0)
                q_los(0, 1)
                make_bias(0, 0)
                mask_scores(0, 0, 0)
                q_los(0, 2)
                peaks(0, 0)
                head.token_stats(dve, 1, range(TT))
                head.layernorm(dve, 1)
                mask_scores(0, 0, 1)
                q_los(0, 3)
                totals(0, 0)
                peaks(0, 1)
                mask_scores(0, 0, 2)
                peaks(0, 2)
                for k in range(KT):
                    x_los(1, k)
                totals(0, 1)

            def body(b, par):
                for g in range(KT):
                    t_los(b, g, 0)
                    t_los(b, g, 1)
                    if g == 0:
                        mask_scores(b, par, 3)
                    else:
                        mask_scores(b + 1, 1 - par, g - 1)
                    t_los(b, g, 2)
                    if g == 0:
                        peaks(b, 3)
                    else:
                        peaks(b + 1, g - 1)
                    q_los(b + 1, g)
                    if g < 2:
                        totals(b, g + 2)
                    else:
                        totals(b + 1, g - 2)
                    if g == 3:
                        x_los(b + 2, 0)
                        x_los(b + 2, 1)
                    if g == 0:
                        project(b - 2, 3)
                        make_bias(b + 1, 1 - par)
                        head.token_stats(dve, b + 2, (0, 1))
                        a_los(b - 1, 1 - par, 3)
                    else:
                        project(b - 1, g - 1)
                        if g == 1:
                            head.token_stats(dve, b + 2, (2, 3))
                        if g == 3:
                            x_los(b + 2, 2)
                            x_los(b + 2, 3)
                        a_los(b, par, g - 1)
                        if g == 1:
                            head.layernorm(dve, b + 2)
                        if g == 3 and isinstance(b, int) and b == LAST:
                            ff_head.on_vector(dve)

            def end():
                project(LAST - 1, 3)
                a_los(LAST, 1, 3)
                for t in range(TT):
                    if t < UNDER:
                        ff_head.dequantise(dve, t)
                    project(LAST, t)
                    if t < UNDER:
                        ff_head.split_lo(dve, t)
                        ff_head.peak_of_lo(dve, t)

            run(dve, start, body, end)

        @block.tensor
        def _(pe):
            def free_bank(what, b):
                wait(pe, work_free, ordinal(what, b) - 1)
                return work[bank_of(what, b)]

            def free_tile_bank(what, b):
                wait(pe, t_lo, ordinal(what, b) - 1)
                return tbank[bank_of(what, b)]

            def transpose_x(b, k):
                if exists(b):
                    if k == 0:
                        pe.wait_ge(xn_done, b * TT + TT)
                    to = free_tile_bank(f"A{k}", b)
                    for t in range(TT):
                        mm = nc.tensor.transpose(to[:, t * P:(t + 1) * P], x_sb[:, t, k * P:(k + 1) * P],
                                                 ident[:, :])
                    mm.then_inc(t_full, 1)

            def queries(b, g):
                if exists(b):
                    to = free_bank(f"Q{g}", b)
                    if g == 0:
                        pe.wait_ge(t_lo, ordinal("A3", b) + 1)
                    for i, (s, m) in enumerate(PASSES):
                        for k in range(KT):
                            mm = nc.tensor.matmul(to[:, :], w_q[:, s, k, g * P:(g + 1) * P], xT[:, m, k, :],
                                                  start=(i == 0 and k == 0), stop=(i == 2 and k == KT - 1))
                    mm.then_inc(work_full, 1)

            def scores(b, par, g):
                if exists(b):
                    pe.wait_ge(work_free, ordinal(f"Q{g}", b) + 1)
                    if g == 0:
                        pe.wait_ge(k_in[par], by_parity(b, par) * (8 * HG) + 16 * HG)
                    wait(pe, masked, b * KT + g)
                    for t in range(TT):
                        for i, (s, m) in enumerate(PASSES):
                            mm = nc.tensor.matmul(score[:, t, 0:GK], qT[:, g % 2, s, t * P:(t + 1) * P],
                                                  k_diag[:, par, m * KT + g, :], start=(i == 0), stop=(i == 2))
                    mm.then_inc(score_full, 1)

            def transpose_p(b, g, t):
                if t == 0:
                    pe.wait_ge(normed, b * KT + (g + 1))
                to = free_tile_bank(f"T{g}{t}", b)
                for tt in range(TT):
                    mm = nc.tensor.transpose(to[0:CUTS[t + 1] - CUTS[t], tt * P:(tt + 1) * P],
                                             prob[:, g, tt, CUTS[t]:CUTS[t + 1]], ident[:, :])
                mm.then_inc(t_full, 1)

            def weigh_values(b, par, g):
                if exists(b):
                    to = free_bank(f"V{g}", b)
                    pe.wait_ge(t_lo, ordinal(f"T{g}2", b) + 1)
                    if g == 0:
                        pe.wait_ge(v_in[par], (by_parity(b, par) + 2) * (8 * len(value_pieces())))
                    for t in range(3):
                        n = CUTS[t + 1] - CUTS[t]
                        for i, (s, m) in enumerate(PASSES):
                            mm = nc.tensor.matmul(to[:, :], v_diag[0:n, par, t, s * KT + g, :],
                                                  pT[0:n, g % 2, m, t, :],
                                                  start=(t == 0 and i == 0), stop=(t == 2 and i == 2))
                    mm.then_inc(work_full, 1)

            def project(b, par, t):
                if exists(b):
                    to = free_bank(f"O{t}", b)
                    if t == 0:
                        pe.wait_ge(work_free, ordinal("V3", b) + 1)
                    for i, (s, m) in enumerate(PASSES):
                        for g in range(KT):
                            mm = nc.tensor.matmul(to[:, :], aT[:, par, s, g, t * P:(t + 1) * P], w_o[:, m, g, :],
                                                  start=(i == 0 and g == 0), stop=(i == 2 and g == KT - 1))
                    mm.then_inc(work_full, 1)

            def start():
                pe.wait_ge(head.const_in, 48)
                for k in range(KT):
                    transpose_x(0, k)
                queries(0, 0)
                queries(0, 1)
                scores(0, 0, 0)
                queries(0, 2)
                scores(0, 0, 1)
                queries(0, 3)
                scores(0, 0, 2)
                for k in range(KT):
                    transpose_x(1, k)

            def body(b, par):
                for g in range(KT):
                    transpose_p(b, g, 0)
                    transpose_p(b, g, 1)
                    if g == 0:
                        scores(b, par, 3)
                    else:
                        scores(b + 1, 1 - par, g - 1)
                    transpose_p(b, g, 2)
                    queries(b + 1, g)
                    if g == 0:
                        project(b - 2, par, 3)
                        weigh_values(b - 1, 1 - par, 3)
                    else:
                        if g == 3:
                            transpose_x(b + 2, 0)
                            transpose_x(b + 2, 1)
                        project(b - 1, 1 - par, g - 1)
                        if g == 3:
                            transpose_x(b + 2, 2)
                            transpose_x(b + 2, 3)
                        weigh_values(b, par, g - 1)

            def end():
                project(LAST - 1, 0, 3)
                weigh_values(LAST, 1, 3)
                for t in range(TT):
                    project(LAST, 1, t)

            run(pe, start, body, end)


class FeedForwardHead:

    def __init__(self, size, constants, x2_0, buffers, of_loads, of_weights, of_rows, steps, under_stage_2):
        self.size, self.constants, self.x2_0, self.buffers = size, constants, x2_0, buffers
        self.of_loads, self.of_weights, self.of_rows = of_loads, of_weights, of_rows
        (self.load_x2, self.load_w, self.finish_ln, self.code_lo, self.make_h, self.split_hi, self.token_stats,
         self.layernorms, self.dequantise, self.split_lo, self.peak_of_lo) = steps
        self.on_sync, self.on_vector, self.on_gpsimd, self.on_scalar = under_stage_2


def feed_forward_head(nc, outer, free, x2_dram, ident_dram, gamma, beta, q1, s1, b1, q2, s2, b2):
    base = (nc.sbuf_base + 31) // 32 * 32
    at = [base]

    def place(name, shape, dt=F32, over=None):
        size = 4
        for n in shape[1:]:
            size *= n
        t = nc.alloc_sbuf_tensor_at(name, shape, dt, offset=at[0] if over is None else over)
        if over is None:
            at[0] += (size + 31) // 32 * 32
        return t

    def sem(name):
        return outer.enter_context(nc.semaphore(name))

    ident = place("ident3", [P, P])
    gam, bet = place("gamma_col", [P, KT]), place("beta_col", [P, KT])
    s1_col, b1_col = place("s1_col", [P, KT, NF]), place("b1_col", [P, NF])
    b2_half = place("b2_half", [P, DM])
    stats, mv = place("stats3", [P, TT, 6]), place("mv3", [P, TT, 2])
    var_eps, rstds = place("var_eps3", [P, 2, TT]), place("rstds", [P, 2, TT])
    neg_mean, minus_half = place("neg_mean3", [P, TT]), place("minus_half3", [P, 2, TT])
    carrier = place("carrier3", [P, 2])
    h_scale, h_shift = rstds[:, 1, :], place("h_shift", [P, TT])
    u_scale, u_shift = place("u_scale", [P, TT]), place("u_shift", [P, TT])
    lo_peak = place("lo_peak", [P, NF * KT])
    x2_0 = place("x2_0", [P, TT, DM])
    h = place("h", [P, TT, DM])
    w, w_f32, w_codes = [], [], []
    for f in range(NF):
        w_at = at[0]
        w.append(place(f"w{f}", [P, 4, DM], F32R))
        w_f32.append(place(f"w_f32_{f}", [P, 4, DM], F32, over=w_at))
        w_codes.append(place(f"w_codes{f}", [P, 4, DM], I32, over=w_at))
        assert f >= UNDER or at[0] <= base + free

    const_in, b2_done = sem("const_in3"), sem("b2_done")
    w_in = [sem(f"w_in3_{i}") for i in range(LOADS)]
    c_f, w_f, w2_hi, w2_lo = (sem(n) for n in ("c_f", "w_f", "w2_hi", "w2_lo"))
    c_hi, c_lo, peaked = sem("c_hi"), sem("c_lo"), sem("lo_peaked")
    x2_in = [sem(f"x2_in{i}") for i in range(2)]
    out_kept = [sem(f"out_kept{i}") for i in range(2)]
    half_set, own, var_done, rstd_done, ln_done = (
        sem(n) for n in ("half_set3", "ln_own3", "var_done3", "rstd_done3", "ln_done3"))
    h_done, h_full, r_done = sem("h_done"), sem("h_full"), sem("r_done")

    def exists(b):
        return not isinstance(b, int) or 0 <= b < BATCH

    def load_x2(sp, b, par, x2):
        if exists(b):
            if exists(b - 2):
                sp.wait_ge(out_kept[par], by_parity(b, par) * (8 * TT))
            sp.dma_start(x2[:, :, :], one(x2_dram, b).rearrange("o (t p) n -> (o p) t n", p=P)
                         ).then_inc(x2_in[par], 16)

    def load_w(sp, f):
        if f >= LOADS:
            sp.wait_ge(w2_lo, f - LOADS + 1)
        cols = slice(f * P, (f + 1) * P)
        sp.dma_start(w_codes[f][:, C_LO, :].rearrange("p (k n) -> p k n", n=P), q1.rearrange("(k p) n -> p k n", p=P)[:, :, cols]
                     ).then_inc(w_in[f % LOADS], 16)
        sp.dma_start(w_codes[f][:, W2 + LO, :], q2[cols, :]).then_inc(w_in[f % LOADS], 16)
        sp.dma_start(w_f32[f][:, W2 + HI, :], s2[f, :].partition_broadcast(P)).then_inc(w_in[f % LOADS], 16)

    def token_stats(dve, b, par, tiles, x2):
        if exists(b):
            if tiles[0] == 0:
                dve.wait_ge(x2_in[par], by_parity(b, par) * 8 + 16)
                wait(dve, ln_done, b * 3)
            for t in tiles:
                nc.vector.bn_stats(stats[:, t, :], x2[:, t, :]).then_inc(own, 1)

    def layernorms(dve, b):
        if exists(b):
            dve.wait_ge(own, b * 8 + 4)
            nc.vector.tensor_copy(carrier[:, 1:2], carrier[:, 0:1])
            for t in range(TT):
                nc.vector.bn_aggr(mv[:, t, :], stats[:, t, :]).then_inc(own, 1)
            mean, var = mv[:, :, 0], mv[:, :, 1]
            dve.wait_ge(own, b * 8 + 8)
            nc.vector.tensor_scalar(var_eps[:, 0, :], var, EPS, None, ALU.add).then_inc(var_done, 1)
            nc.vector.tensor_scalar(var_eps[:, 1, :], var, 1.0 + EPS, EPS * EPS,
                                    ALU.mult, ALU.add).then_inc(var_done, 1)
            nc.vector.tensor_scalar(neg_mean[:, :], mean, -1.0, None, ALU.mult).then_inc(var_done, 1)

    def dequantise(dve, f):
        dve.wait_ge(w_in[f % LOADS], 48 * (f // LOADS + 1))
        nc.vector.tensor_scalar(w_f32[f][:, C_LO, :], w_codes[f][:, C_LO, :], -ZERO_POINT, None,
                                ALU.add).then_inc(c_f, 1)
        nc.vector.scalar_tensor_tensor(out=w_f32[f][:, W2 + LO, :], in0=w_codes[f][:, W2 + LO, :], scalar=-ZERO_POINT,
                                       in1=w_f32[f][:, W2 + HI, :], op0=ALU.add, op1=ALU.mult).then_inc(w_f, 1)

    def split_lo(dve, f):
        dve.wait_ge(w2_hi, f + 1)
        nc.vector.scalar_tensor_tensor(out=w[f][:, W2 + LO, :], in0=w_f32[f][:, W2 + LO, :], scalar=0.25,
                                       in1=w[f][:, W2 + HI, :].bitcast(F32),
                                       op0=ALU.mult, op1=ALU.subtract).then_inc(w2_lo, 1)

    def peak_of_lo(dve, f):
        dve.wait_ge(c_lo, f + 1)
        nc.vector.tensor_reduce(lo_peak[:, f * KT:(f + 1) * KT],
                                w[f][:, C_LO, :].rearrange("p (k n) -> p k n", n=P).bitcast(F32), AX.X, ALU.max,
                                apply_absolute_value=True).then_inc(peaked, 1)

    def finish_ln(pool, b):
        if exists(b):
            pool.wait_ge(var_done, b * 3 + 3)
            wait(pool, r_done, b * TT)
            nc.gpsimd.tensor_tensor(rstds[:, :, :], var_eps[:, :, :], minus_half[:, :, :],
                                    ALU.pow).then_inc(rstd_done, 1)
            pool.wait_ge(rstd_done, b + 1)
            nc.gpsimd.tensor_tensor(h_shift[:, :], neg_mean[:, :], h_scale, ALU.mult).then_inc(ln_done, 1)
            nc.gpsimd.tensor_tensor(u_shift[:, :], neg_mean[:, :], rstds[:, 0, :], ALU.mult).then_inc(ln_done, 1)
            nc.gpsimd.tensor_scalar(u_scale[:, :], rstds[:, 0, :], 1.0, None, ALU.add).then_inc(ln_done, 1)

    def code_lo(pool, f):
        pool.wait_ge(c_hi, f + 1)
        nc.gpsimd.tensor_tensor(w[f][:, C_LO, :], w_f32[f][:, C_LO, :], w[f][:, C_HI, :].bitcast(F32),
                                ALU.subtract).then_inc(c_lo, 1)

    def make_h(act, b, par, tiles, x2):
        if exists(b):
            if tiles[0] == 0:
                act.wait_ge(ln_done, b * 3 + 3)
                if exists(b - 1):
                    act.wait_ge(h_full, b * KT)
            for t in tiles:
                nc.scalar.activation(h[:, t, :], x2[:, t, :], ACT.Identity,
                                     scale=rstds[:, 1, t:t + 1], bias=h_shift[:, t:t + 1]).then_inc(h_done, 1)

    def split_hi(act, f):
        act.wait_ge(c_f, f + 1)
        nc.scalar.activation(w[f][:, C_HI, :], w_f32[f][:, C_LO, :], ACT.Copy).then_inc(c_hi, 1)
        act.wait_ge(w_f, f + 1)
        nc.scalar.activation(w[f][:, W2 + HI, :], w_f32[f][:, W2 + LO, :], ACT.Copy,
                             scale=0.25).then_inc(w2_hi, 1)

    def on_sync(sp):
        load_x2(sp, 0, 0, x2_0)
        for to, of in ((ident, ident_dram), (gam, gamma), (bet, beta), (b1_col, b1)):
            sp.dma_start(to[:, :], of).then_inc(const_in, 16)
        sp.dma_start(s1_col[:, :, :], s1).then_inc(const_in, 16)
        sp.dma_start(b2_half[:, :], b2.partition_broadcast(P)).then_inc(const_in, 16)
        for f in range(UNDER):
            load_w(sp, f)

    def on_vector(dve):
        dve.wait_ge(const_in, 96)
        nc.vector.memset(carrier[:, 0:1], 0.0)
        token_stats(dve, 0, 0, range(TT), x2_0)
        layernorms(dve, 0)
        nc.vector.tensor_scalar(b2_half[:, :], b2_half[:, :], 0.5, None, ALU.mult).then_inc(b2_done, 1)

    def on_gpsimd(pool):
        pool.wait_ge(x2_in[0], 16)
        nc.gpsimd.memset(minus_half[:, :, :], -0.5).then_inc(half_set, 1)
        pool.wait_ge(half_set, 1)
        finish_ln(pool, 0)

    def on_scalar(act):
        make_h(act, 0, 0, range(TT), x2_0)
        for f in range(UNDER):
            split_hi(act, f)

    return FeedForwardHead(
        at[0] - nc.sbuf_base, (ident, gam, bet, s1_col, b1_col, b2_half), x2_0,
        (w, w_f32, w_codes, lo_peak, h, h_shift, rstds, u_scale, u_shift),
        (const_in, b2_done, w_in, x2_in, out_kept), (c_f, w_f, w2_hi, w2_lo, c_hi, c_lo, peaked),
        (ln_done, h_done, h_full, r_done),
        (load_x2, load_w, finish_ln, code_lo, make_h, split_hi, token_stats, layernorms, dequantise, split_lo,
         peak_of_lo), (on_sync, on_vector, on_gpsimd, on_scalar))


def feed_forward(nc, head, out):
    with ExitStack() as ctx:
        def sb(name, shape, dt=F32):
            return ctx.enter_context(nc.sbuf_tensor(name, shape, dt))

        def sem(name):
            return ctx.enter_context(nc.semaphore(name))

        ctx.enter_context(nc.sbuf_tensor("placed", [P, head.size // 4], F32))
        ident, gam, bet, s1_col, b1_col, b2_half = head.constants
        w, w_f32, w_codes, lo_peak, h, h_shift, rstds, u_scale, u_shift = head.buffers
        x2 = [head.x2_0, sb("x2_1", [P, TT, DM])]
        const_in, b2_done, w_in, x2_in, out_kept = head.of_loads
        c_f, w_f, w2_hi, w2_lo, c_hi, c_lo, peaked = head.of_weights
        ln_done, h_done, h_full, r_done = head.of_rows
        row_peak, any_peak = sb("row_peak", [P, 1]), sb("any_peak", [P, 1])
        lo_used = sb("lo_used", [P, 1], I32)
        hT = [sb(f"hT{i}", [P, 2, KT, SEQ], F32R) for i in range(2)]
        h_f = sb("h_f", [P, 2, SEQ])
        y = sb("y", [P, 2, SEQ])
        th = sb("th", [P, 2, SEQ])
        a = sb("a", [P, 2, 2, SEQ], F32R)
        acc = ctx.enter_context(nc.psum_tensor("acc", [P, TT, 512], F32))
        g_bank = [ctx.enter_context(nc.psum_tensor(f"g_bank{k}", [P, 512], F32)) for k in range(KT)]

        all_peaked, any_peaked, lo_known = sem("lo_all_peaked"), sem("lo_any_peaked"), sem("lo_known")
        res_done = sem("res_done")
        h_scaled, h_hi, h_lo = sem("h_scaled"), sem("h_hi"), sem("h_lo")
        g_full, y_begun, added, th_done, a_done, a_hi, a_lo = (
            sem(n) for n in ("g_full", "y_begun", "added", "th_done", "a_done", "a_hi3", "a_lo3"))
        f2_done, acc_full, out_ready = sem("f2_done"), sem("acc_full"), sem("out_ready")
        block = ctx.enter_context(nc.Block())

        ADDS = KT - 1
        NEXT_STATS = {4: 0, 5: 1, 6: 2, 7: 3}
        NEXT_ROWS = {8: (0, 1), 9: (2, 3)}
        NEXT_H = {10: 0, 11: 1, 12: 2, 13: 3}
        NEXT_RES = {12: (0, 1), 13: (2, 3)}
        H_EARLY = (0, 1)

        def run(eng, start, body, end):
            start()
            body(0, 0)
            body(1, 1)
            with eng.Fori(1, BATCH // 2 - 1) as pair:
                body(pair * 2, 0)
                body(pair * 2 + 1, 1)
            body(BATCH - 2, 0)
            body(LAST, 1)
            end()

        def exists(b):
            return not isinstance(b, int) or 0 <= b < BATCH

        def first(b):
            return isinstance(b, int) and b == 0

        def back(b, f, steps):
            return (b, f - steps) if f >= steps else (b - 1, f - steps + NF)

        @block.sync
        def _(sp):
            def store(b, par):
                if exists(b):
                    for t in range(TT):
                        sp.wait_ge(out_ready, b * TT + (t + 1))
                        sp.dma_start(one(out, b)[:, t * P:(t + 1) * P, :].rearrange("o p n -> (o p) n"),
                                     x2[par][:, t, :]).then_inc(out_kept[par], 16)

            def start():
                for f in range(UNDER, LOADS):
                    head.load_w(sp, f)
                head.load_x2(sp, 1, 1, x2[1])
                for f in range(LOADS, NF):
                    head.load_w(sp, f)

            def body(b, par):
                if not first(b):
                    store(b - 1, 1 - par)
                    head.load_x2(sp, b + 1, 1 - par, x2[1 - par])

            def end():
                store(LAST, 1)
                for i in range(2):
                    sp.wait_ge(out_kept[i], 8 * TT * BATCH)

            run(sp, start, body, end)

        @block.gpsimd
        def _(pool):
            def residual(b, par, tiles):
                if exists(b):
                    for t in tiles:
                        pool.wait_ge(r_done, b * TT + (t + 1))
                        nc.gpsimd.tensor_tensor(x2[par][:, t, :], x2[par][:, t, :], b2_half[:, :],
                                                ALU.add).then_inc(res_done, 1)

            def h_los(b, par, k):
                if exists(b):
                    pool.wait_ge(h_hi, b * KT + (k + 1))
                    nc.gpsimd.tensor_tensor(hT[par][:, LO, k, :], h_f[:, k % 2, :],
                                            hT[par][:, HI, k, :].bitcast(F32), ALU.subtract).then_inc(h_lo, 1)

            def a_los(b, f):
                if exists(b):
                    pool.wait_ge(a_hi, b * NF + (f + 1))
                    nc.gpsimd.tensor_tensor(a[:, f % 2, LO, :], y[:, f % 2, :], a[:, f % 2, HI, :].bitcast(F32),
                                            ALU.subtract).then_inc(a_lo, 1)

            def start():
                for k in range(KT):
                    h_los(0, 0, k)
                pool.wait_ge(b2_done, 1)

            def body(b, par):
                for f in range(NF):
                    if f - 1 in NEXT_H and NEXT_H[f - 1] not in H_EARLY:
                        h_los(b + 1, 1 - par, NEXT_H[f - 1])
                    if f == min(NEXT_ROWS):
                        head.finish_ln(pool, b + 1)
                    a_los(*back(b, f, 1))
                    if first(b) and f + AHEAD < NF:
                        head.code_lo(pool, f + AHEAD)
                    if first(b) and f == NF - 1:
                        pool.wait_ge(all_peaked, 1)
                        nc.gpsimd.partition_all_reduce(any_peak[:, :], row_peak[:, :], P, RMAX).then_inc(any_peaked, 1)
                    if first(b) and f in (4, 5):
                        residual(0, 0, (2 * (f - 4), 2 * (f - 4) + 1))
                    if f in NEXT_H and NEXT_H[f] in H_EARLY:
                        h_los(b + 1, 1 - par, NEXT_H[f])
                    if f - 2 in NEXT_RES:
                        residual(b + 1, 1 - par, NEXT_RES[f - 2])

            def end():
                a_los(LAST, NF - 1)

            run(pool, start, body, end)

        @block.scalar
        def _(act):
            def make_r(b, par, tiles):
                if exists(b):
                    for t in tiles:
                        act.wait_ge(h_done, b * TT + (t + 1))
                        nc.scalar.activation(x2[par][:, t, :], x2[par][:, t, :], ACT.Identity,
                                             scale=u_scale[:, t:t + 1], bias=u_shift[:, t:t + 1]).then_inc(r_done, 1)

            def scale_h(b, k):
                if exists(b):
                    act.wait_ge(h_full, b * KT + (k + 1))
                    wait(act, h_lo, b * KT + (k - 1))
                    nc.scalar.activation(h_f[:, k % 2, :], g_bank[k][:, :], ACT.Identity,
                                         scale=gam[:, k:k + 1], bias=bet[:, k:k + 1]).then_inc(h_scaled, 1)

            def h_his(b, par, k):
                if exists(b):
                    act.wait_ge(h_scaled, b * KT + (k + 1))
                    if k == 0 and exists(b - 2):
                        act.wait_ge(g_full, (b - 1) * (NF * KT))
                    nc.scalar.activation(hT[par][:, HI, k, :], h_f[:, k % 2, :], ACT.Copy).then_inc(h_hi, 1)

            def begin(b, f):
                n = b * NF + f
                act.wait_ge(g_full, n * KT + 1)
                wait(act, a_lo, n - 1)
                nc.scalar.activation(y[:, f % 2, :], g_bank[0][:, :], ACT.Identity, scale=s1_col[:, 0, f:f + 1],
                                     bias=b1_col[:, f:f + 1]).then_inc(y_begun, 1)

            def tanh(b, f):
                if exists(b):
                    act.wait_ge(added, (b * NF + (f + 1)) * ADDS)
                    nc.scalar.activation(th[:, f % 2, :], y[:, f % 2, :], ACT.Tanh, scale=0.5).then_inc(th_done, 1)

            def a_his(b, f):
                if exists(b):
                    n = b * NF + f
                    act.wait_ge(a_done, n + 1)
                    wait(act, f2_done, n - 1)
                    nc.scalar.activation(a[:, f % 2, HI, :], y[:, f % 2, :], ACT.Copy).then_inc(a_hi, 1)

            def start():
                for k in range(KT):
                    scale_h(0, k)
                    h_his(0, 0, k)
                make_r(0, 0, range(TT))

            def body(b, par):
                for f in range(NF):
                    late = f - 1 in NEXT_H and NEXT_H[f - 1] not in H_EARLY
                    if late:
                        scale_h(b + 1, NEXT_H[f - 1])
                    begin(b, f)
                    tanh(*back(b, f, 1))
                    if late:
                        h_his(b + 1, 1 - par, NEXT_H[f - 1])
                    a_his(*back(b, f, 1))
                    if f in NEXT_H and NEXT_H[f] in H_EARLY:
                        scale_h(b + 1, NEXT_H[f])
                        h_his(b + 1, 1 - par, NEXT_H[f])
                    if first(b) and f + AHEAD < NF:
                        head.split_hi(act, f + AHEAD)
                    if f in NEXT_ROWS:
                        head.make_h(act, b + 1, 1 - par, NEXT_ROWS[f], x2[1 - par])
                    if f in NEXT_RES:
                        make_r(b + 1, 1 - par, NEXT_RES[f])

            def end():
                tanh(LAST, NF - 1)
                a_his(LAST, NF - 1)

            run(act, start, body, end)

        @block.vector
        def _(dve):
            def gather_peaks():
                dve.wait_ge(peaked, NF)
                nc.vector.tensor_reduce(row_peak[:, :], lo_peak[:, :], AX.X, ALU.max).then_inc(all_peaked, 1)

            def know_lo():
                dve.wait_ge(any_peaked, 1)
                nc.vector.tensor_scalar(lo_used[:, :], any_peak[:, :], 0.0, None, ALU.not_equal).then_inc(lo_known, 1)

            def add_group(b, f, k):
                n = b * NF + f
                dve.wait_ge(g_full, n * KT + (k + 1))
                if k == 1:
                    dve.wait_ge(y_begun, n + 1)
                else:
                    dve.wait_ge(added, n * ADDS + (k - 1))
                nc.vector.scalar_tensor_tensor(out=y[:, f % 2, :], in0=g_bank[k][:, :], scalar=s1_col[:, k, f:f + 1],
                                               in1=y[:, f % 2, :], op0=ALU.mult, op1=ALU.add).then_inc(added, 1)

            def activate(b, f):
                if exists(b):
                    dve.wait_ge(th_done, b * NF + (f + 1))
                    nc.vector.scalar_tensor_tensor(out=y[:, f % 2, :], in0=th[:, f % 2, :], scalar=1.0,
                                                   in1=y[:, f % 2, :], op0=ALU.add, op1=ALU.mult).then_inc(a_done, 1)

            def outputs(b, par, tiles):
                if exists(b):
                    for t in tiles:
                        if t < TT - 1:
                            dve.wait_ge(acc_full, b * (TT - 1) + (t + 1))
                        else:
                            dve.wait_ge(f2_done, b * NF + NF)
                        dve.wait_ge(res_done, b * TT + (t + 1))
                        nc.vector.tensor_tensor(x2[par][:, t, :], acc[:, t, :], x2[par][:, t, :],
                                                ALU.add).then_inc(out_ready, 1)

            def start():
                head.dequantise(dve, UNDER)

            def body(b, par):
                for f in range(NF):
                    if f == 2:
                        outputs(b - 1, 1 - par, (2,))
                    add_group(b, f, 1)
                    if f == 2:
                        outputs(b - 1, 1 - par, (3,))
                    activate(*back(b, f, 1))
                    if first(b) and AHEAD <= f + 1 < NF:
                        head.peak_of_lo(dve, f + 1)
                    add_group(b, f, 2)
                    if first(b) and f + AHEAD + 1 < NF:
                        head.dequantise(dve, f + AHEAD + 1)
                    if f == 1:
                        outputs(b - 1, 1 - par, (0, 1))
                    add_group(b, f, 3)
                    if first(b) and f + AHEAD < NF:
                        head.split_lo(dve, f + AHEAD)
                    if first(b) and f == NF - AHEAD:
                        gather_peaks()
                    if first(b) and f == NF - 1:
                        know_lo()
                    if f in NEXT_STATS:
                        head.token_stats(dve, b + 1, 1 - par, (NEXT_STATS[f],), x2[1 - par])
                    if f == max(NEXT_STATS):
                        head.layernorms(dve, b + 1)

            def end():
                activate(LAST, NF - 1)
                outputs(LAST, 1, range(TT))

            run(dve, start, body, end)

        @block.tensor
        def _(pe):
            def transpose_h(b, k):
                if exists(b):
                    if k == 0:
                        pe.wait_ge(h_done, b * TT + TT)
                    for t in range(TT):
                        mm = nc.tensor.transpose(g_bank[k][:, t * P:(t + 1) * P], h[:, t, k * P:(k + 1) * P],
                                                 ident[:, :])
                    mm.then_inc(h_full, 1)

            def group_used(b, f, k):
                if k == 0:
                    wait(pe, y_begun, b * NF + (f + 1))
                else:
                    wait(pe, added, (b * NF + f) * ADDS + k)

            def fc1(b, par, f, lo):
                if f == 0:
                    pe.wait_ge(h_lo, b * KT + KT)
                if first(b):
                    pe.wait_ge(c_lo, f + 1)
                for k in range(KT):
                    cols = slice(k * P, (k + 1) * P)
                    group_used(*back(b, f, 1), k)
                    if f and NEXT_H.get(f - 1) == k and exists(b + 1):
                        pe.wait_ge(h_scaled, (b + 1) * KT + (k + 1))
                    nc.tensor.matmul(g_bank[k][:, :], w[f][:, C_HI, cols], hT[par][:, HI, k, :], start=True, stop=False)
                    if lo:
                        nc.tensor.matmul(g_bank[k][:, :], w[f][:, C_LO, cols], hT[par][:, HI, k, :],
                                         start=False, stop=False)
                    nc.tensor.matmul(g_bank[k][:, :], w[f][:, C_HI, cols], hT[par][:, LO, k, :],
                                     start=False, stop=True).then_inc(g_full, 1)

            def fc2(b, f):
                if not exists(b):
                    return
                n = b * NF + f
                pe.wait_ge(a_lo, n + 1)
                if first(b):
                    pe.wait_ge(w2_lo, f + 1)
                for t in range(TT):
                    if f == 0 and exists(b - 1):
                        pe.wait_ge(out_ready, b * TT + (t - 3))
                    for i, (s, m) in enumerate(PASSES):
                        mm = nc.tensor.matmul(acc[:, t, :], a[:, f % 2, s, t * P:(t + 1) * P], w[f][:, W2 + m, :],
                                              start=(f == 0 and i == 0), stop=(f == NF - 1 and i == 2))
                    if f == NF - 1 and t < TT - 1:
                        mm.then_inc(acc_full, 1)
                mm.then_inc(f2_done, 1)

            def next_h(b, f):
                if exists(b + 1):
                    group_used(b, f, NEXT_H[f])
                    transpose_h(b + 1, NEXT_H[f])

            def start():
                pe.wait_ge(const_in, 96)
                for k in range(KT):
                    transpose_h(0, k)

            def body(b, par, lo):
                for f in range(NF):
                    fc1(b, par, f, lo)
                    if f in NEXT_H and NEXT_H[f] in H_EARLY:
                        next_h(b, f)
                    fc2(*back(b, f, 2))
                    if f in NEXT_H and NEXT_H[f] not in H_EARLY:
                        next_h(b, f)

            def others(lo):
                body(1, 1, lo)
                with pe.Fori(1, BATCH // 2 - 1) as pair:
                    body(pair * 2, 0, lo)
                    body(pair * 2 + 1, 1, lo)
                body(BATCH - 2, 0, lo)
                body(LAST, 1, lo)
                fc2(LAST, NF - 2)
                fc2(LAST, NF - 1)

            start()
            body(0, 0, True)
            pe.wait_ge(lo_known, 1)
            used = pe.value_load(lo_used[0:1, 0:1], min_val=0, max_val=1)
            with pe.If(used != 0):
                others(True)
            with pe.Else():
                others(False)


def xattn_ffn(nc, x, ctxT, mask, wqT, b_q, wkT, b_k, wvT, b_v, woT, b_o, ident, gamma, beta, q1, s1, b1, q2, s2, b2,
              out):
    k_dram = nc.dram_tensor("k_kept_dram", (BATCH, P, 2, KT, KEYS), F32R, kind="Internal").ap()
    v_dram = nc.dram_tensor("v_kept_dram", (CTX, 2 * DM), F32R, kind="Internal").ap()
    x2_dram = nc.dram_tensor("x2_kept_dram", (BATCH, SEQ, DM), F32, kind="Internal").ap()
    with ExitStack() as whole:
        free = 4 * (2 * KT * DM + 2 * 2 * KT * GK + TT * DM)
        ff_head = feed_forward_head(nc, whole, free, x2_dram, ident, gamma, beta, q1, s1, b1, q2, s2, b2)
        with ExitStack() as ctx:
            w_q = ctx.enter_context(nc.sbuf_tensor("w_q", [P, 2, KT, DM], F32R))
            k_diag = ctx.enter_context(nc.sbuf_tensor("k_diag", [P, 2, 2 * KT, GK], F32R))
            x_sb = ctx.enter_context(nc.sbuf_tensor("x_sb", [P, TT, DM], F32))
            w_o = ctx.enter_context(nc.sbuf_tensor("w_o", [P, 2, KT, DM], F32R))
            v_diag = ctx.enter_context(nc.sbuf_tensor("v_diag", [P, 2, 3, 2 * KT, P], F32R))
            head = attention_head(nc, ctx, x_sb, x, ident, b_q, b_o)
            keys_and_values(nc, head, ctxT, (wkT, wvT, wqT, woT), b_k, b_v, k_dram, v_dram, w_q, w_o, k_diag, v_diag)
            attention(nc, head, ff_head, x, mask, k_dram, v_dram, x2_dram, w_q, w_o, k_diag, v_diag)
        feed_forward(nc, ff_head, out)


def kernel(x, ctx_1024, mask_Bx1xSxS2_ik0, L0_xattn_w_q, L0_xattn_b_q, L0_xattn_w_k, L0_xattn_b_k, L0_xattn_w_v,
           L0_xattn_b_v, L0_xattn_w_out, L0_xattn_b_out, L0_ffn_ln_gamma, L0_ffn_ln_beta, L0_ffn_fc1_q,
           L0_ffn_fc1_scales, L0_ffn_fc1_bias, L0_ffn_fc2_q, L0_ffn_fc2_scales, L0_ffn_fc2_bias):
    import numpy as np
    import concourse.bacc as bacc
    from concourse.bass_utils import run_bass_kernel_spmd

    def column(v):
        return np.asarray(v).reshape(-1, P).T

    arrays = {
        "x": x,
        "ctxT": np.asarray(ctx_1024).reshape(CTX, DM).T,
        "mask": np.asarray(mask_Bx1xSxS2_ik0).reshape(BATCH, SEQ, KEYS),
        "wqT": np.asarray(L0_xattn_w_q).T,
        "b_q": column(L0_xattn_b_q),
        "wkT": np.asarray(L0_xattn_w_k).T,
        "b_k": column(L0_xattn_b_k),
        "wvT": np.asarray(L0_xattn_w_v).T,
        "b_v": L0_xattn_b_v,
        "woT": np.asarray(L0_xattn_w_out).T,
        "b_o": L0_xattn_b_out,
        "identity": np.eye(P, dtype=np.float32),
        "gamma": column(L0_ffn_ln_gamma),
        "beta": column(L0_ffn_ln_beta),
        "fc1_q": L0_ffn_fc1_q,
        "fc1_scales": np.asarray(L0_ffn_fc1_scales).reshape(KT, NF, P).transpose(2, 0, 1),
        "fc1_bias": column(L0_ffn_fc1_bias),
        "fc2_q": L0_ffn_fc2_q,
        "fc2_scales": L0_ffn_fc2_scales,
        "fc2_bias": L0_ffn_fc2_bias,
    }
    nc = bacc.Bacc("TRN2", target_bir_lowering=False, num_devices=1)
    given, args = {}, []
    for name, a in arrays.items():
        a = np.ascontiguousarray(a)
        given[f"in_{name}"] = a
        args.append(nc.dram_tensor(f"in_{name}", a.shape, mybir.dt.from_np(a.dtype), kind="ExternalInput").ap())
    out = nc.dram_tensor("out_x", (BATCH, SEQ, DM), F32, kind="ExternalOutput").ap()
    xattn_ffn(nc, *args, out)
    return run_bass_kernel_spmd(nc, [given], core_ids=[0]).results[0]["out_x"]
```
